# Optimizing a Trainium2 kernel written in Bass

```python
import numpy as np
import jax
import jax.numpy as jnp

def _softmax(x, axis=-1):
    return jax.nn.softmax(x, axis=axis)

def _gelu(x):
    return jax.nn.gelu(x, approximate=True)

def _silu(x):
    return jax.nn.silu(x)

def _sigmoid(x):
    return jax.nn.sigmoid(x)

def _layernorm(x, axis=-1, eps=1e-05):
    m = jnp.mean(x, axis=axis, keepdims=True)
    v = jnp.var(x, axis=axis, keepdims=True)
    return (x - m) / jnp.sqrt(v + eps)

def _scatter_add(tgt, idx, src, axis=0):
    return tgt.at[idx].add(src)

def _segment_sum(src, seg, n):
    return jax.ops.segment_sum(src, seg, n)
kernel_name = 'mk_cond_resid_d4_seqx_r4_0da226'

def setup_inputs(seed: int=0):
    np.random.seed(seed)
    _w = jnp.asarray

    def _rec_inputs():
        import jax
        import jax.numpy as jnp
        _rk = jax.random.key(seed)
        x = -0.0002928 + 1 * jax.random.normal(jax.random.fold_in(_rk, 1), (2, 1024, 256), jnp.float32)
        _lenS = 1024 - jax.random.randint(jax.random.fold_in(_rk, 7), (2,), 0, max(1, 1024 // 4) + 1, jnp.int32)
        _lenS2 = 1024 - jax.random.randint(jax.random.fold_in(_rk, 8), (2,), 0, max(1, 1024 // 4) + 1, jnp.int32)
        cond_64 = -0.0184271 + 1.00439 * jax.random.normal(jax.random.fold_in(_rk, 12), (2, 64), jnp.float32)
        fside_16xSxS_0 = -5.72187e-05 + 0.999849 * jax.random.normal(jax.random.fold_in(_rk, 13), (16, 1024, 1024), jnp.float32)
        _validS = jnp.arange(1024)[None, :] < _lenS[:, None]
        _validS2 = jnp.arange(1024)[None, :] < _lenS2[:, None]
        _causal = jnp.tril(jnp.ones((1024, 1024), dtype=bool))
        mask_BxS_bf1 = jnp.ones((2, 1024), dtype=bool)
        mask_BxS_bk0 = jnp.logical_not(jnp.broadcast_to(_validS[:, :], (2, 1024)))
        return (x, cond_64, fside_16xSxS_0, mask_BxS_bf1, mask_BxS_bk0)
    x, cond_64, fside_16xSxS_0, mask_BxS_bf1, mask_BxS_bk0 = _rec_inputs()

    def _L0_cond_setup():
        import jax, jax.numpy as jnp
        import numpy as np
        DIM = 256
        HEADS = 16
        DIM_HEAD = 64
        SCALE = 8.0

        def ln(x, g, eps=1e-05):
            mean = x.mean(axis=-1, keepdims=True)
            var = ((x - mean) ** 2).mean(axis=-1, keepdims=True)
            return (x - mean) * jax.lax.rsqrt(var + eps) * g

        def l2norm(t):
            n = jnp.maximum(jnp.linalg.norm(t, axis=-1, keepdims=True), 1e-12)
            return t / n

        def rel_pos_bias(n, w0, b0, g0, w1, b1, g1, w2, b2, dtype):
            pos = jnp.arange(-n + 1, n, dtype=dtype)[:, None]
            h = jax.nn.silu(ln(pos @ w0 + b0, g0))
            h = jax.nn.silu(ln(h @ w1 + b1, g1))
            h = h @ w2 + b2
            i = jnp.arange(n)
            idx = i[:, None] - i[None, :] + n - 1
            bias = h[idx]
            return jnp.transpose(bias, (2, 0, 1))
        key = jax.random.key(seed)
        ks = jax.random.split(key, 16)
        b, n = (2, 512)
        inner = HEADS * DIM_HEAD
        s = 0.02
        return {'x': jax.random.normal(ks[0], (b, n, DIM), jnp.float32), 'mask': jnp.ones((b, n), dtype=bool), 'g_norm': jnp.ones((DIM,), jnp.float32), 'Wq': jax.random.normal(ks[1], (DIM, inner), jnp.float32) * s, 'Wkv': jax.random.normal(ks[2], (DIM, 2 * DIM_HEAD), jnp.float32) * s, 'q_scale': jnp.ones((DIM_HEAD,), jnp.float32), 'k_scale': jnp.ones((DIM_HEAD,), jnp.float32), 'null_kv': jax.random.normal(ks[3], (2, DIM_HEAD), jnp.float32), 'null_attn_bias': jax.random.normal(ks[4], (HEADS,), jnp.float32), 'w0': jax.random.normal(ks[5], (1, DIM), jnp.float32) * s, 'b0': jnp.zeros((DIM,), jnp.float32), 'g0': jnp.ones((DIM,), jnp.float32), 'w1': jax.random.normal(ks[6], (DIM, DIM), jnp.float32) * s, 'b1': jnp.zeros((DIM,), jnp.float32), 'g1': jnp.ones((DIM,), jnp.float32), 'w2': jax.random.normal(ks[7], (DIM, HEADS), jnp.float32) * s, 'b2': jnp.zeros((HEADS,), jnp.float32), 'Wout': jax.random.normal(ks[8], (inner, DIM), jnp.float32) * s, 'g_out': jnp.ones((DIM,), jnp.float32)}
    _L0_cond_all = _L0_cond_setup()
    _L0_cond_in = {k: v for k, v in _L0_cond_all.items() if k in ('g_norm', 'Wq', 'Wkv', 'q_scale', 'k_scale', 'null_attn_bias', 'w0', 'b0', 'g0', 'w1', 'b1', 'g1', 'w2', 'b2', 'Wout', 'g_out')}
    del _L0_cond_all

    def _L1_cond_setup():
        import jax, jax.numpy as jnp
        import numpy as np
        B, N, DIM, H, DH = (2, 512, 256, 16, 64)
        INNER = H * DH
        EPS = 1e-05

        def layernorm(x, g):
            mean = jnp.mean(x, axis=-1, keepdims=True)
            var = jnp.var(x, axis=-1, keepdims=True)
            return (x - mean) * jax.lax.rsqrt(var + EPS) * g
        key = jax.random.key(seed)
        ks = jax.random.split(key, 10)
        x = jax.random.normal(ks[0], (B, N, DIM), dtype=jnp.float32)
        attn_bias = jax.random.normal(ks[1], (H, N, N), dtype=jnp.float32)
        mask = jax.random.randint(ks[2], (B, N), 0, 2).astype(bool)
        g_in = jnp.ones((DIM,), dtype=jnp.float32)
        null_attn_bias = jax.random.normal(ks[3], (H,), dtype=jnp.float32)
        null_kv = jax.random.normal(ks[4], (2, DH), dtype=jnp.float32)
        Wq = jax.random.normal(ks[5], (DIM, INNER), dtype=jnp.float32) * 0.02
        Wkv = jax.random.normal(ks[6], (DIM, 2 * DH), dtype=jnp.float32) * 0.02
        Wo = jax.random.normal(ks[7], (INNER, DIM), dtype=jnp.float32) * 0.02
        g_out = jnp.ones((DIM,), dtype=jnp.float32)
        return {'x': x, 'attn_bias': attn_bias, 'mask': mask, 'g_in': g_in, 'null_attn_bias': null_attn_bias, 'null_kv': null_kv, 'Wq': Wq, 'Wkv': Wkv, 'Wo': Wo, 'g_out': g_out}
    _L1_cond_all = _L1_cond_setup()
    _L1_cond_in = {k: v for k, v in _L1_cond_all.items() if k in ('g_in', 'null_attn_bias', 'Wq', 'Wkv', 'Wo', 'g_out')}
    del _L1_cond_all

    def _L2_cond_setup():
        import jax, jax.numpy as jnp
        import numpy as np
        B, S, H = (4, 512, 256)
        E = 8
        M = 128
        K = 2
        N_SHARED = 2
        SM = M * N_SHARED
        G = 64
        GE_TEMP = 1.0
        ALPHA = 0.001
        SEQ_AUX = True
        NORM_TOPK = True
        COS_TEMP = 0.78
        CONS_ALPHA = 0.01
        LEAKY_SLOPE = 0.01
        EPS_COS = 1e-08

        def _leaky(x):
            return jnp.where(x >= 0, x, LEAKY_SLOPE * x)

        def _moe_forward(hidden_states, g, wt, wg, w_gate, w_up, w_down, sw_gate, sw_up, sw_down):
            b, s, h = hidden_states.shape
            x = hidden_states.reshape(-1, h)
            T = x.shape[0]
            logits_h = x @ wt.T
            logits_g = g @ wg.T
            logits_g = jnp.repeat(logits_g, s, axis=0)
            logits = (logits_h + logits_g / GE_TEMP) / (1.0 + 1.0 / GE_TEMP)
            scores = jax.nn.softmax(logits, axis=-1)
            topk_w, topk_idx = jax.lax.top_k(scores, K)
            if K > 1 and NORM_TOPK:
                topk_w = topk_w / (topk_w.sum(-1, keepdims=True) + 1e-20)
            onehot = jax.nn.one_hot(topk_idx.reshape(b, s * K), E, dtype=jnp.float32)
            ce = onehot.sum(1) / (s * K / E)
            aux_loss = (ce * scores.reshape(b, s, E).mean(1)).sum(1).mean() * ALPHA
            gp = _leaky(jnp.einsum('th,ehm->etm', x, w_gate))
            up = jnp.einsum('th,ehm->etm', x, w_up)
            y_all = jnp.einsum('etm,emh->eth', gp * up, w_down)
            y_sel = y_all[topk_idx, jnp.arange(T)[:, None], :]
            y = (y_sel * topk_w[..., None]).sum(1).reshape(b, s, h)
            p = _leaky(hidden_states @ sw_gate) * (hidden_states @ sw_up) @ sw_down
            y = y + p
            num = jnp.sum(y * p, -1)
            den = jnp.maximum(jnp.linalg.norm(y, axis=-1), EPS_COS) * jnp.maximum(jnp.linalg.norm(p, axis=-1), EPS_COS)
            closs = CONS_ALPHA * jnp.mean(num / den / (1.0 + COS_TEMP))
            return (y, aux_loss + closs)
        key = jax.random.key(seed)
        ks = jax.random.split(key, 12)
        sh = 1.0 / np.sqrt(H)
        sm = 1.0 / np.sqrt(M)
        ssm = 1.0 / np.sqrt(SM)
        sg = 1.0 / np.sqrt(G)
        return {'hidden_states': jax.random.normal(ks[0], (B, S, H), jnp.float32), 'g': jax.random.normal(ks[1], (B, G), jnp.float32), 'wt': jax.random.uniform(ks[2], (E, H), jnp.float32, -sh, sh), 'wg': jax.random.uniform(ks[3], (E, G), jnp.float32, -sg, sg), 'w_gate': jax.random.uniform(ks[4], (E, H, M), jnp.float32, -sh, sh), 'w_up': jax.random.uniform(ks[5], (E, H, M), jnp.float32, -sh, sh), 'w_down': jax.random.uniform(ks[6], (E, M, H), jnp.float32, -sm, sm), 'sw_gate': jax.random.uniform(ks[7], (H, SM), jnp.float32, -sh, sh), 'sw_up': jax.random.uniform(ks[8], (H, SM), jnp.float32, -sh, sh), 'sw_down': jax.random.uniform(ks[9], (SM, H), jnp.float32, -ssm, ssm)}
    _L2_cond_all = _L2_cond_setup()
    _L2_cond_in = {k: v for k, v in _L2_cond_all.items() if k in ('wt', 'wg', 'w_gate', 'w_up', 'w_down', 'sw_gate', 'sw_up', 'sw_down')}
    del _L2_cond_all

    def _L3_cond_setup():
        import jax, jax.numpy as jnp
        import numpy as np
        B, S, H = (4, 512, 256)
        E = 8
        M = 128
        K = 2
        N_SHARED = 2
        SM = M * N_SHARED
        G = 64
        GE_TEMP = 1.0
        ALPHA = 0.001
        SEQ_AUX = True
        NORM_TOPK = True
        COS_TEMP = 0.78
        CONS_ALPHA = 0.01
        LEAKY_SLOPE = 0.01
        EPS_COS = 1e-08

        def _leaky(x):
            return jnp.where(x >= 0, x, LEAKY_SLOPE * x)

        def _moe_forward(hidden_states, g, wt, wg, w_gate, w_up, w_down, sw_gate, sw_up, sw_down):
            b, s, h = hidden_states.shape
            x = hidden_states.reshape(-1, h)
            T = x.shape[0]
            logits_h = x @ wt.T
            logits_g = g @ wg.T
            logits_g = jnp.repeat(logits_g, s, axis=0)
            logits = (logits_h + logits_g / GE_TEMP) / (1.0 + 1.0 / GE_TEMP)
            scores = jax.nn.softmax(logits, axis=-1)
            topk_w, topk_idx = jax.lax.top_k(scores, K)
            if K > 1 and NORM_TOPK:
                topk_w = topk_w / (topk_w.sum(-1, keepdims=True) + 1e-20)
            onehot = jax.nn.one_hot(topk_idx.reshape(b, s * K), E, dtype=jnp.float32)
            ce = onehot.sum(1) / (s * K / E)
            aux_loss = (ce * scores.reshape(b, s, E).mean(1)).sum(1).mean() * ALPHA
            gp = _leaky(jnp.einsum('th,ehm->etm', x, w_gate))
            up = jnp.einsum('th,ehm->etm', x, w_up)
            y_all = jnp.einsum('etm,emh->eth', gp * up, w_down)
            y_sel = y_all[topk_idx, jnp.arange(T)[:, None], :]
            y = (y_sel * topk_w[..., None]).sum(1).reshape(b, s, h)
            p = _leaky(hidden_states @ sw_gate) * (hidden_states @ sw_up) @ sw_down
            y = y + p
            num = jnp.sum(y * p, -1)
            den = jnp.maximum(jnp.linalg.norm(y, axis=-1), EPS_COS) * jnp.maximum(jnp.linalg.norm(p, axis=-1), EPS_COS)
            closs = CONS_ALPHA * jnp.mean(num / den / (1.0 + COS_TEMP))
            return (y, aux_loss + closs)
        key = jax.random.key(seed)
        ks = jax.random.split(key, 12)
        sh = 1.0 / np.sqrt(H)
        sm = 1.0 / np.sqrt(M)
        ssm = 1.0 / np.sqrt(SM)
        sg = 1.0 / np.sqrt(G)
        return {'hidden_states': jax.random.normal(ks[0], (B, S, H), jnp.float32), 'g': jax.random.normal(ks[1], (B, G), jnp.float32), 'wt': jax.random.uniform(ks[2], (E, H), jnp.float32, -sh, sh), 'wg': jax.random.uniform(ks[3], (E, G), jnp.float32, -sg, sg), 'w_gate': jax.random.uniform(ks[4], (E, H, M), jnp.float32, -sh, sh), 'w_up': jax.random.uniform(ks[5], (E, H, M), jnp.float32, -sh, sh), 'w_down': jax.random.uniform(ks[6], (E, M, H), jnp.float32, -sm, sm), 'sw_gate': jax.random.uniform(ks[7], (H, SM), jnp.float32, -sh, sh), 'sw_up': jax.random.uniform(ks[8], (H, SM), jnp.float32, -sh, sh), 'sw_down': jax.random.uniform(ks[9], (SM, H), jnp.float32, -ssm, ssm)}
    _L3_cond_all = _L3_cond_setup()
    _L3_cond_in = {k: v for k, v in _L3_cond_all.items() if k in ('wt', 'wg', 'w_gate', 'w_up', 'w_down', 'sw_gate', 'sw_up', 'sw_down')}
    del _L3_cond_all
    return {'x': x, 'cond_64': cond_64, 'fside_16xSxS_0': fside_16xSxS_0, 'mask_BxS_bf1': mask_BxS_bf1, 'mask_BxS_bk0': mask_BxS_bk0, 'L0_cond_g_norm': _L0_cond_in['g_norm'], 'L0_cond_Wq': _L0_cond_in['Wq'], 'L0_cond_Wkv': _L0_cond_in['Wkv'], 'L0_cond_q_scale': _L0_cond_in['q_scale'], 'L0_cond_k_scale': _L0_cond_in['k_scale'], 'L0_cond_null_attn_bias': _L0_cond_in['null_attn_bias'], 'L0_cond_w0': _L0_cond_in['w0'], 'L0_cond_b0': _L0_cond_in['b0'], 'L0_cond_g0': _L0_cond_in['g0'], 'L0_cond_w1': _L0_cond_in['w1'], 'L0_cond_b1': _L0_cond_in['b1'], 'L0_cond_g1': _L0_cond_in['g1'], 'L0_cond_w2': _L0_cond_in['w2'], 'L0_cond_b2': _L0_cond_in['b2'], 'L0_cond_Wout': _L0_cond_in['Wout'], 'L0_cond_g_out': _L0_cond_in['g_out'], 'L1_cond_g_in': _L1_cond_in['g_in'], 'L1_cond_null_attn_bias': _L1_cond_in['null_attn_bias'], 'L1_cond_Wq': _L1_cond_in['Wq'], 'L1_cond_Wkv': _L1_cond_in['Wkv'], 'L1_cond_Wo': _L1_cond_in['Wo'], 'L1_cond_g_out': _L1_cond_in['g_out'], 'L2_cond_wt': _L2_cond_in['wt'], 'L2_cond_wg': _L2_cond_in['wg'], 'L2_cond_w_gate': _L2_cond_in['w_gate'], 'L2_cond_w_up': _L2_cond_in['w_up'], 'L2_cond_w_down': _L2_cond_in['w_down'], 'L2_cond_sw_gate': _L2_cond_in['sw_gate'], 'L2_cond_sw_up': _L2_cond_in['sw_up'], 'L2_cond_sw_down': _L2_cond_in['sw_down'], 'L3_cond_wt': _L3_cond_in['wt'], 'L3_cond_wg': _L3_cond_in['wg'], 'L3_cond_w_gate': _L3_cond_in['w_gate'], 'L3_cond_w_up': _L3_cond_in['w_up'], 'L3_cond_w_down': _L3_cond_in['w_down'], 'L3_cond_sw_gate': _L3_cond_in['sw_gate'], 'L3_cond_sw_up': _L3_cond_in['sw_up'], 'L3_cond_sw_down': _L3_cond_in['sw_down']}

def reference(x, cond_64, fside_16xSxS_0, mask_BxS_bf1, mask_BxS_bk0, L0_cond_g_norm, L0_cond_Wq, L0_cond_Wkv, L0_cond_q_scale, L0_cond_k_scale, L0_cond_null_attn_bias, L0_cond_w0, L0_cond_b0, L0_cond_g0, L0_cond_w1, L0_cond_b1, L0_cond_g1, L0_cond_w2, L0_cond_b2, L0_cond_Wout, L0_cond_g_out, L1_cond_g_in, L1_cond_null_attn_bias, L1_cond_Wq, L1_cond_Wkv, L1_cond_Wo, L1_cond_g_out, L2_cond_wt, L2_cond_wg, L2_cond_w_gate, L2_cond_w_up, L2_cond_w_down, L2_cond_sw_gate, L2_cond_sw_up, L2_cond_sw_down, L3_cond_wt, L3_cond_wg, L3_cond_w_gate, L3_cond_w_up, L3_cond_w_down, L3_cond_sw_gate, L3_cond_sw_up, L3_cond_sw_down):
    import jax
    import jax.numpy as jnp

    def _L0_cond_ref(x, mask, g_norm, Wq, Wkv, q_scale, k_scale, null_kv, null_attn_bias, w0, b0, g0, w1, b1, g1, w2, b2, Wout, g_out):
        import jax, jax.numpy as jnp
        import numpy as np
        DIM = 256
        HEADS = 16
        DIM_HEAD = 64
        SCALE = 8.0

        def ln(x, g, eps=1e-05):
            mean = x.mean(axis=-1, keepdims=True)
            var = ((x - mean) ** 2).mean(axis=-1, keepdims=True)
            return (x - mean) * jax.lax.rsqrt(var + eps) * g

        def l2norm(t):
            n = jnp.maximum(jnp.linalg.norm(t, axis=-1, keepdims=True), 1e-12)
            return t / n

        def rel_pos_bias(n, w0, b0, g0, w1, b1, g1, w2, b2, dtype):
            pos = jnp.arange(-n + 1, n, dtype=dtype)[:, None]
            h = jax.nn.silu(ln(pos @ w0 + b0, g0))
            h = jax.nn.silu(ln(h @ w1 + b1, g1))
            h = h @ w2 + b2
            i = jnp.arange(n)
            idx = i[:, None] - i[None, :] + n - 1
            bias = h[idx]
            return jnp.transpose(bias, (2, 0, 1))
        b, n, _ = x.shape
        xn = ln(x, g_norm)
        q = (xn @ Wq).reshape(b, n, HEADS, DIM_HEAD).transpose(0, 2, 1, 3)
        kv = xn @ Wkv
        k, v = (kv[..., :DIM_HEAD], kv[..., DIM_HEAD:])
        nk = jnp.broadcast_to(null_kv[0], (b, 1, DIM_HEAD))
        nv = jnp.broadcast_to(null_kv[1], (b, 1, DIM_HEAD))
        k = jnp.concatenate([nk, k], axis=1)
        v = jnp.concatenate([nv, v], axis=1)
        q = l2norm(q) * q_scale
        k = l2norm(k) * k_scale
        sim = jnp.einsum('bhid,bjd->bhij', q, k) * SCALE
        bias = rel_pos_bias(n, w0, b0, g0, w1, b1, g1, w2, b2, q.dtype)
        null_bias = jnp.broadcast_to(null_attn_bias[:, None, None], (HEADS, n, 1))
        attn_bias = jnp.concatenate([null_bias, bias], axis=-1)
        sim = sim + attn_bias
        neg = -jnp.finfo(sim.dtype).max
        causal = jnp.triu(jnp.ones((n, n + 1), dtype=bool), k=2)
        sim = jnp.where(causal, neg, sim)
        m = jnp.pad(mask, ((0, 0), (1, 0)), constant_values=True)[:, None, None, :]
        sim = jnp.where(m, sim, neg)
        attn = jax.nn.softmax(sim, axis=-1)
        out = jnp.einsum('bhij,bjd->bhid', attn, v)
        out = out.transpose(0, 2, 1, 3).reshape(b, n, HEADS * DIM_HEAD)
        return ln(out @ Wout, g_out)

    def _L1_cond_ref(x, attn_bias, mask, g_in, null_attn_bias, null_kv, Wq, Wkv, Wo, g_out):
        import jax, jax.numpy as jnp
        import numpy as np
        B, N, DIM, H, DH = (2, 512, 256, 16, 64)
        INNER = H * DH
        EPS = 1e-05

        def layernorm(x, g):
            mean = jnp.mean(x, axis=-1, keepdims=True)
            var = jnp.var(x, axis=-1, keepdims=True)
            return (x - mean) * jax.lax.rsqrt(var + EPS) * g
        b, n, _ = x.shape
        scale = DH ** (-0.5)
        xn = layernorm(x, g_in)
        q = (xn @ Wq).reshape(b, n, H, DH).transpose(0, 2, 1, 3) * scale
        kv = xn @ Wkv
        k, v = (kv[..., :DH], kv[..., DH:])
        nk = jnp.broadcast_to(null_kv[0], (b, 1, DH))
        nv = jnp.broadcast_to(null_kv[1], (b, 1, DH))
        k = jnp.concatenate([nk, k], axis=1)
        v = jnp.concatenate([nv, v], axis=1)
        sim = jnp.einsum('bhid,bjd->bhij', q, k)
        null_col = jnp.broadcast_to(null_attn_bias[:, None, None], (H, n, 1))
        bias = jnp.concatenate([null_col, attn_bias], axis=-1)
        sim = sim + bias
        neg = -jnp.finfo(sim.dtype).max
        j = n + 1
        causal_mask = jnp.triu(jnp.ones((n, j), dtype=bool), k=j - n + 1)
        sim = jnp.where(causal_mask, neg, sim)
        mask_p = jnp.pad(mask, ((0, 0), (1, 0)), constant_values=True)
        sim = jnp.where(mask_p[:, None, None, :], sim, neg)
        attn = jax.nn.softmax(sim, axis=-1)
        out = jnp.einsum('bhij,bjd->bhid', attn, v)
        out = out.transpose(0, 2, 1, 3).reshape(b, n, INNER)
        out = out @ Wo
        return layernorm(out, g_out)

    def _L2_cond_ref(hidden_states, g, wt, wg, w_gate, w_up, w_down, sw_gate, sw_up, sw_down):
        import jax, jax.numpy as jnp
        import numpy as np
        B, S, H = (4, 512, 256)
        E = 8
        M = 128
        K = 2
        N_SHARED = 2
        SM = M * N_SHARED
        G = 64
        GE_TEMP = 1.0
        ALPHA = 0.001
        SEQ_AUX = True
        NORM_TOPK = True
        COS_TEMP = 0.78
        CONS_ALPHA = 0.01
        LEAKY_SLOPE = 0.01
        EPS_COS = 1e-08

        def _leaky(x):
            return jnp.where(x >= 0, x, LEAKY_SLOPE * x)

        def _moe_forward(hidden_states, g, wt, wg, w_gate, w_up, w_down, sw_gate, sw_up, sw_down):
            b, s, h = hidden_states.shape
            x = hidden_states.reshape(-1, h)
            T = x.shape[0]
            logits_h = x @ wt.T
            logits_g = g @ wg.T
            logits_g = jnp.repeat(logits_g, s, axis=0)
            logits = (logits_h + logits_g / GE_TEMP) / (1.0 + 1.0 / GE_TEMP)
            scores = jax.nn.softmax(logits, axis=-1)
            topk_w, topk_idx = jax.lax.top_k(scores, K)
            if K > 1 and NORM_TOPK:
                topk_w = topk_w / (topk_w.sum(-1, keepdims=True) + 1e-20)
            onehot = jax.nn.one_hot(topk_idx.reshape(b, s * K), E, dtype=jnp.float32)
            ce = onehot.sum(1) / (s * K / E)
            aux_loss = (ce * scores.reshape(b, s, E).mean(1)).sum(1).mean() * ALPHA
            gp = _leaky(jnp.einsum('th,ehm->etm', x, w_gate))
            up = jnp.einsum('th,ehm->etm', x, w_up)
            y_all = jnp.einsum('etm,emh->eth', gp * up, w_down)
            y_sel = y_all[topk_idx, jnp.arange(T)[:, None], :]
            y = (y_sel * topk_w[..., None]).sum(1).reshape(b, s, h)
            p = _leaky(hidden_states @ sw_gate) * (hidden_states @ sw_up) @ sw_down
            y = y + p
            num = jnp.sum(y * p, -1)
            den = jnp.maximum(jnp.linalg.norm(y, axis=-1), EPS_COS) * jnp.maximum(jnp.linalg.norm(p, axis=-1), EPS_COS)
            closs = CONS_ALPHA * jnp.mean(num / den / (1.0 + COS_TEMP))
            return (y, aux_loss + closs)
        y, _ = _moe_forward(hidden_states, g, wt, wg, w_gate, w_up, w_down, sw_gate, sw_up, sw_down)
        return y

    def _L3_cond_ref(hidden_states, g, wt, wg, w_gate, w_up, w_down, sw_gate, sw_up, sw_down):
        import jax, jax.numpy as jnp
        import numpy as np
        B, S, H = (4, 512, 256)
        E = 8
        M = 128
        K = 2
        N_SHARED = 2
        SM = M * N_SHARED
        G = 64
        GE_TEMP = 1.0
        ALPHA = 0.001
        SEQ_AUX = True
        NORM_TOPK = True
        COS_TEMP = 0.78
        CONS_ALPHA = 0.01
        LEAKY_SLOPE = 0.01
        EPS_COS = 1e-08

        def _leaky(x):
            return jnp.where(x >= 0, x, LEAKY_SLOPE * x)

        def _moe_forward(hidden_states, g, wt, wg, w_gate, w_up, w_down, sw_gate, sw_up, sw_down):
            b, s, h = hidden_states.shape
            x = hidden_states.reshape(-1, h)
            T = x.shape[0]
            logits_h = x @ wt.T
            logits_g = g @ wg.T
            logits_g = jnp.repeat(logits_g, s, axis=0)
            logits = (logits_h + logits_g / GE_TEMP) / (1.0 + 1.0 / GE_TEMP)
            scores = jax.nn.softmax(logits, axis=-1)
            topk_w, topk_idx = jax.lax.top_k(scores, K)
            if K > 1 and NORM_TOPK:
                topk_w = topk_w / (topk_w.sum(-1, keepdims=True) + 1e-20)
            onehot = jax.nn.one_hot(topk_idx.reshape(b, s * K), E, dtype=jnp.float32)
            ce = onehot.sum(1) / (s * K / E)
            aux_loss = (ce * scores.reshape(b, s, E).mean(1)).sum(1).mean() * ALPHA
            gp = _leaky(jnp.einsum('th,ehm->etm', x, w_gate))
            up = jnp.einsum('th,ehm->etm', x, w_up)
            y_all = jnp.einsum('etm,emh->eth', gp * up, w_down)
            y_sel = y_all[topk_idx, jnp.arange(T)[:, None], :]
            y = (y_sel * topk_w[..., None]).sum(1).reshape(b, s, h)
            p = _leaky(hidden_states @ sw_gate) * (hidden_states @ sw_up) @ sw_down
            y = y + p
            num = jnp.sum(y * p, -1)
            den = jnp.maximum(jnp.linalg.norm(y, axis=-1), EPS_COS) * jnp.maximum(jnp.linalg.norm(p, axis=-1), EPS_COS)
            closs = CONS_ALPHA * jnp.mean(num / den / (1.0 + COS_TEMP))
            return (y, aux_loss + closs)
        y, _ = _moe_forward(hidden_states, g, wt, wg, w_gate, w_up, w_down, sw_gate, sw_up, sw_down)
        return y
    x = x + _L0_cond_ref(x, mask_BxS_bf1, L0_cond_g_norm, L0_cond_Wq, L0_cond_Wkv, L0_cond_q_scale, L0_cond_k_scale, cond_64, L0_cond_null_attn_bias, L0_cond_w0, L0_cond_b0, L0_cond_g0, L0_cond_w1, L0_cond_b1, L0_cond_g1, L0_cond_w2, L0_cond_b2, L0_cond_Wout, L0_cond_g_out)
    x = x + _L1_cond_ref(x, fside_16xSxS_0, mask_BxS_bk0, L1_cond_g_in, L1_cond_null_attn_bias, cond_64, L1_cond_Wq, L1_cond_Wkv, L1_cond_Wo, L1_cond_g_out)
    x = x + _L2_cond_ref(x, cond_64, L2_cond_wt, L2_cond_wg, L2_cond_w_gate, L2_cond_w_up, L2_cond_w_down, L2_cond_sw_gate, L2_cond_sw_up, L2_cond_sw_down)
    x = x + _L3_cond_ref(x, cond_64, L3_cond_wt, L3_cond_wg, L3_cond_w_gate, L3_cond_w_up, L3_cond_w_down, L3_cond_sw_gate, L3_cond_sw_up, L3_cond_sw_down)
    return x

_drawn_inputs = setup_inputs


def setup_inputs(seed=0):
    import zlib

    import numpy as np

    out = dict(_drawn_inputs(seed))
    spreads = {'L0_cond_g_norm': (1.0, 0.2),
     'L0_cond_q_scale': (1.0, 0.2),
     'L0_cond_k_scale': (1.0, 0.2),
     'L0_cond_b0': (0.0, 0.343),
     'L0_cond_g0': (1.0, 0.6),
     'L0_cond_b1': (0.0, 0.341),
     'L0_cond_g1': (1.0, 0.6),
     'L0_cond_b2': (0.0, 0.425),
     'L0_cond_g_out': (1.0, 0.2),
     'L1_cond_g_in': (1.0, 0.2),
     'L1_cond_g_out': (1.0, 0.2)}
    factors = {}
    for name, (base, spread) in spreads.items():
        noise = np.random.default_rng([zlib.crc32(name.encode()), seed]).standard_normal(out[name].shape)
        drawn = base * np.exp(spread * noise) if base else spread * noise
        out[name] = jnp.asarray(drawn.astype(out[name].dtype))
    for name, factor in factors.items():
        out[name] = (out[name] * factor).astype(out[name].dtype)
    return out
```

```python
import concourse.bass as bass
from concourse import mybir
from contextlib import ExitStack

F32 = mybir.dt.float32
F16 = mybir.dt.float16
I32 = mybir.dt.int32
U8 = mybir.dt.uint8
ALU = mybir.AluOpType
ACT = mybir.ActivationFunctionType
AX = mybir.AxisListType.X

P = 128
B, S, D = 2, 1024, 256
H, DH = 16, 64
INNER = H * DH
TILES = S // P
KC = D // P
HU = 4
HG = H // HU
UNITS = HG * B
STEPS = 2 * TILES
UW = HU * DH
E, M = 8, 128
SM = 256
G = 64
CHUNK = 4
CHUNKS = B * TILES // CHUNK
EB = E + SM // M

WS = 256.0
BIG = 60000.0
NEG = -1.0e30
EPS = 1e-5
TAB = S + P


class Plan:

    def __init__(self):
        self.steps = STEPS * UNITS * HU
        self.groups = []
        self.first_group = []
        for n in range(self.steps):
            self.first_group.append(len(self.groups))
            nk = self.tile(n) + 1
            for j in range(0, nk, 4):
                self.groups.append((n, j, min(4, nk - j)))
        self.first_group.append(len(self.groups))

    def tile(self, n):
        return (n // (UNITS * HU)) % TILES

    def layer(self, n):
        return n // (UNITS * HU * TILES)

    def unit(self, n):
        return n // HU

    def of(self, n):
        return range(self.first_group[n], self.first_group[n + 1])

    def groups_done(self, n):
        return self.first_group[n + 1]


def model(nc, a, out):
    plan = Plan()
    N = plan.steps
    ctx = ExitStack()
    with ctx:
        def sb(name, shape, dt=F32):
            return ctx.enter_context(nc.sbuf_tensor(name, shape, dt))

        def pb(name, shape):
            return ctx.enter_context(nc.psum_tensor(name, shape, F32))

        def sem(name):
            return ctx.enter_context(nc.semaphore(name))

        table = nc.dram_tensor("rel_table", (H, P, TAB + P), F32).ap()

        x = sb("x", [P, B * TILES, D])
        bias = sb("bias", [P, 2, HU, S])
        moe_w = sb("moe_w", [P, 7680])
        wq = [sb(f"wq{i}", [P, 2, KC, INNER], F16) for i in range(2)]
        wkv = [sb(f"wkv{i}", [P, 2, KC, 2 * DH], F16) for i in range(2)]
        wo = [sb(f"wo{i}", [P, 2, INNER // P, D], F16) for i in range(2)]
        stage = sb("stage", [P, 2, 2048])
        k_a = [sb(f"k_a{i}", [P, B, S], F16) for i in range(2)]
        k_b = [sb(f"k_b{i}", [P, B, S], F16) for i in range(2)]
        v_s = [sb(f"v_s{i}", [P, B * TILES, 2, DH], F16) for i in range(2)]
        q_a = sb("q_a", [P, 2, HU * P], F16)
        q_b = sb("q_b", [P, 2, HU * P], F16)
        q_n = sb("q_n", [P, UW])
        q_sq = sb("q_sq", [P, UW])
        q_ss = sb("q_ss", [P, HU])
        q_r = sb("q_r", [P, HU])
        xt = sb("xt", [P, 2, 2, B, KC, P], F16)
        xn = sb("xn", [P, B, D])
        st6 = sb("st6", [P, B, 6])
        mv = sb("mv", [P, B, 2])
        rstd = sb("rstd", [P, B])
        k_d = sb("k_d", [P, B, 2 * DH])
        k_sq = sb("k_sq", [P, B, DH])
        k_ss = sb("k_ss", [P, B])
        k_r = sb("k_r", [P, B])
        biased = sb("biased", [P, 2, S])
        probs = sb("probs", [P, 2, S])
        p_hi = sb("p_hi", [P, 3, 4 * P], F16)
        p_lo = sb("p_lo", [P, 3, 4 * P], F16)
        neg_null = sb("neg_null", [P, 2, HU])
        neg_max = sb("neg_max", [P, 2, HU])
        rows = sb("rows", [P, 2, HU])
        d_null = sb("d_null", [P, HU])
        p_null = sb("p_null", [P, HU])
        denom = sb("denom", [P, HU])
        r_den = sb("r_den", [P, HU])
        o_null = sb("o_null", [P, HU, DH])
        o_raw = sb("o_raw", [P, HU, DH])
        o_n = sb("o_n", [P, HU, DH])
        ot_hi = sb("ot_hi", [P, UW], F16)
        ot_lo = sb("ot_lo", [P, UW], F16)
        y_acc = sb("y_acc", [P, B, D])
        y_st = sb("y_st", [P, 6])
        y_mv = sb("y_mv", [P, 2])
        y_rs = sb("y_rs", [P, 1])
        y_n = sb("y_n", [P, D])
        y_g = sb("y_g", [P, D])
        ident = sb("ident", [P, P])
        mhalf = sb("mhalf", [P, 16])
        k_scale = sb("k_scale", [P, DH])
        q_scale = sb("q_scale", [P, DH])
        null_b = [sb(f"null_b{i}", [P, H]) for i in range(2)]
        null_k = sb("null_k", [P, DH])
        null_kd = sb("null_kd", [P, 2, 2 * DH])
        null_v = sb("null_v", [P, DH])
        null_sq = sb("null_sq", [P, DH])
        null_r = sb("null_r", [P, 1])
        kn_a = sb("kn_a", [P, 2], F16)
        kn_b = sb("kn_b", [P, 2], F16)
        g_in = [sb(f"g_in{i}", [P, KC]) for i in range(2)]
        g_out = [sb(f"g_out{i}", [P, D]) for i in range(2)]
        mask_words = probs[:, 0, :].bitcast(I32).rearrange("p (l n) -> p l n", l=2)
        mask8 = probs[:, 0, :].bitcast(U8).rearrange("p (l n) -> p l n", l=2)
        ones64 = sb("ones64", [G, P])
        w1_sb = bias[:, 1, 0, 0:KC * D].rearrange("p (k n) -> p k n", k=KC)
        w2_sb = bias[:, 1, 1, 0:KC * H].rearrange("p (k n) -> p k n", k=KC)
        b2_sb = sb("b2_sb", [H, 1])
        rel_i = sb("rel_i", [P, TILES], I32)
        rel_f = sb("rel_f", [P, TILES])
        r_st = sb("r_st", [P, TILES, 6])
        r_mv = sb("r_mv", [P, TILES, 2])
        r_rs = sb("r_rs", [P, TILES])
        rh = moe_w[:, 0:2048].rearrange("p (k n) -> p k n", k=TILES)
        re = moe_w[:, 2048:4096].rearrange("p (k n) -> p k n", k=TILES)
        rht = moe_w[:, 4096:6144].rearrange("p (c k n) -> p c k n", c=KC, k=TILES)
        rvec = moe_w[:, 6144:7424].rearrange("p (v n) -> p v n", v=5)
        tab = biased[0:H, :, :].rearrange("p a n -> p (a n)")[:, 0:TAB]
        wt_n = sb("wt_n", [E, 2, D])
        wg_n = sb("wg_n", [E, 2, G])
        cond_n = sb("cond_n", [B, G])
        wt_s = sb("wt_s", [P, 2, 2, KC, E], F16)
        wt_f = sb("wt_f", [P, 2, KC, E])
        wg_t = sb("wg_t", [G, 2, E])
        cond_t = sb("cond_t", [G, B])
        cond_b = sb("cond_b", [G, B, P])
        lg_half = sb("lg_half", [P, 2, B, E])
        place = sb("place", [P, E])
        mx_hi, mx_lo = (t_[:, :, :].rearrange("p a (k n) -> p a k n", k=KC) for t_ in (k_a[0], k_b[0]))
        gl = [sb(f"gl{i}", [P, CHUNK, E]) for i in range(6)]
        gm = [sb(f"gm{i}", [P, CHUNK]) for i in range(6)]
        comb = sb("comb", [P, 2, CHUNK, E])
        g_t = biased[:, 0, 0:512]
        g_l = biased[:, 1, 0:512]
        h_f = probs[:, :, 0:512]
        h_hi = p_hi[:, 0:2, :]
        h_lo = p_lo[:, 0:2, :]
        moe_h = [moe_w[:, :].bitcast(F16),
                 bias[:, :, :, :].rearrange("p a h n -> p (a h n)")[:, 0:7680].bitcast(F16)]

        def moe_view(layer, hl, off, n):
            base = 2 * off_base[off]
            size = off_size[off]
            return moe_h[layer][:, base + hl * size: base + hl * size + n]

        sizes = {"gate": 2048, "up": 2048, "down": 2048, "sgate": 512, "sup": 512, "sdown": 512}
        off_base, off_size, at = {}, {}, 0
        for name, size in sizes.items():
            off_base[name], off_size[name] = at, size
            at += size

        sc = [pb(f"sc{i}", [P, S]) for i in range(2)]
        tp = [pb(f"tp{i}", [P, 512]) for i in range(2)]
        op = pb("op", [P, 512])
        aux = pb("aux", [P, 512])

        def sems(part, names):
            return {name: sem(part + "_" + name) for name in names.split()}

        setup = sems("setup", """mhalf ident rel kn0 place ones penalty big pad nss nrinv nkd nt nka nkb
                    mt mtd cb lg lgh stats rstd z exp h pt t mm tab""")
        s = sems("attn", """scores bias biased probs
                    pt p_hi p_lo pv
                    q_proj q_sq q_ss q_r q_nd q_na q_t q_hi q_lo q_dup q_null null
                    x_st x_rs xn xt xt_hi xt_lo kv kv_act kv_r kv_d kv_v k_dup kt k_hi k_lo
                    d_null p_null denom r_den o_null o_raw o_n ot ot_hi ot_lo y y_acc
                    y_st y_rs y_n x_new""")
        f = sems("moe", """xt xt_hi xt_lo logit shifted exp comb gu tenth leaky h h_hi h_lo down y out""")
        job_done = sem("job_done")
        dve_chain = sem("dve_chain")
        pool_chain = sem("pool_chain")
        table_in = [sem(f"table_in{i}") for i in range(HG)]
        s_bias = [sem(f"bias_in{i}") for i in range(2)]
        s_stage = [sem(f"stage_in{i}") for i in range(2)]
        s_in = {name: sem("in_" + name) for name in ("x", "rel", "w1", "w2", "head", "mask", "moe")}

        def bcast(ap, n):
            return bass.AP(ap.tensor, ap.offset, [[0, P], [1, n]])

        def flat(t):
            names_ = {3: "p a b -> p (a b)", 4: "p a b c -> p (a b c)"}
            return t.rearrange(names_[len(t.shape)]) if len(t.shape) > 2 else t

        jobs = []
        for i, pre in ((0, "L0_cond_"), (1, "L1_cond_")):
            w_o = a[pre + ("Wout" if i == 0 else "Wo")]
            jobs.append(([(a[pre + "Wq"].rearrange("(k p) n -> p k n", p=P), 0, (KC, INNER))],
                         [(flat(wq[i][:, 0]), flat(wq[i][:, 1]), 0, 2048)], i, INNER))
            jobs.append(([(a[pre + "Wkv"].rearrange("(k p) n -> p k n", p=P), 0, (KC, 2 * DH))],
                         [(flat(wkv[i][:, 0]), flat(wkv[i][:, 1]), 0, 256)], i, 2 * DH))
            jobs.append(([(w_o.rearrange("(c p) n -> p c n", p=P), 0, (INNER // P, D))],
                         [(flat(wo[i][:, 0]), flat(wo[i][:, 1]), 0, 2048)], None, 0))
        for i, pre in ((0, "L2_cond_"), (1, "L3_cond_")):
            def ends(name):
                return moe_view(i, 0, name, sizes[name]), moe_view(i, 1, name, sizes[name])
            jobs.append(([(a[pre + "w_gate"].rearrange("e (k p) m -> p (e k) m", p=P), 0, (E * KC, M))],
                         [(*ends("gate"), 0, 2048)], None, 0))
            jobs.append(([(a[pre + "w_up"].rearrange("e (k p) m -> p (e k) m", p=P), 0, (E * KC, M))],
                         [(*ends("up"), 0, 2048)], None, 0))
            jobs.append(([(a[pre + "w_down"].rearrange("e m n -> m e n"), 0, (E, D))],
                         [(*ends("down"), 0, 2048)], None, 0))
            jobs.append(([(a[pre + "sw_gate"].rearrange("(k p) m -> p k m", p=P), 0, (KC, SM)),
                          (a[pre + "sw_up"].rearrange("(k p) m -> p k m", p=P), 512, (KC, SM)),
                          (a[pre + "sw_down"].rearrange("(k p) m -> p k m", p=P), 1024, (SM // P, D))],
                         [(*ends("sgate"), 0, 512), (*ends("sup"), 512, 512),
                          (*ends("sdown"), 1024, 512)], None, 0))
        PIECE = 512
        pieces = []
        job_end = []
        for jn, (_, ends_, gain, per) in enumerate(jobs):
            for hi, lo, at, size in ends_:
                step = min(PIECE, per) if gain is not None else PIECE
                for c in range(0, size, step):
                    w = min(step, size - c)
                    pieces.append((jn, hi[:, c:c + w], lo[:, c:c + w], at + c, w, gain,
                                   (at + c) // per if gain is not None else 0))
            job_end.append(len(pieces))
        stage_value = []
        so_far = [0, 0]
        for jn, (loads, *_rest) in enumerate(jobs):
            so_far[jn % 2] += 16 * len(loads)
            stage_value.append(so_far[jn % 2])

        def load_job(eng, jn):
            if jn >= 2:
                eng.wait_ge(job_done, job_end[jn - 2])
            for src, at_, (c, n_) in jobs[jn][0]:
                eng.dma_start(stage[:, jn % 2, at_:at_ + c * n_].rearrange("p (c n) -> p c n", c=c),
                              src).then_inc(s_stage[jn % 2], 16)

        def load_bias(eng, g):
            step, hg = g // HG, g % HG
            layer, t = step // TILES, step % TILES
            w = P * (t + 1)
            if g >= 2:
                eng.wait_ge(s["biased"], UNITS // HG * HU * (g - 1))
            if layer == 0:
                if step == 0:
                    eng.wait_ge(table_in[hg], 16)
                src = table[hg * HU:(hg + 1) * HU, :, (TILES - 1 - t) * P + P - 1:TILES * P + P - 1]\
                    .rearrange("h p j -> p h j")
            else:
                src = a["fside_16xSxS_0"][hg * HU:(hg + 1) * HU, t * P:(t + 1) * P, 0:w]\
                    .rearrange("h p j -> p h j")
            eng.dma_start(bias[:, g % 2, :, 0:w], src).then_inc(s_bias[g % 2], 16)

        HEAD_LOADS = 13
        NU = N // HU
        U0 = NU // 2
        STEP_N = UNITS * HU
        FIRST, LAST = -16, N + 8

        block = ctx.enter_context(nc.Block())

        @block.sync
        def _(sp):
            load_job(sp, 0)
            load_job(sp, 1)
            sp.dma_start(w1_sb[:, :, :], a["L0_cond_w1"].rearrange("(k p) n -> p k n", p=P)).then_inc(s_in["w1"], 16)
            sp.dma_start(w2_sb[:, :, :], a["L0_cond_w2"].rearrange("(k p) n -> p k n", p=P)).then_inc(s_in["w2"], 16)
            sp.dma_start(b2_sb[:, :], a["L0_cond_b2"].rearrange("(h a) -> h a", a=1)).then_inc(s_in["w2"], 16)
            load_job(sp, 2)
            sp.wait_ge(setup["tab"], 2)
            sp.wait_ge(setup["pad"], 1)
            for hg in range(HG):
                dst = bass.AP(table.tensor, hg * HU * P * (TAB + P), [[P * (TAB + P), HU], [TAB + P + 1, P], [1, TAB]])
                sp.dma_start(dst, tab[hg * HU:(hg + 1) * HU, :].unsqueeze(1).to_broadcast([HU, P, TAB]))\
                    .then_inc(table_in[hg], 16)
            n_jobs = 3
            for g in range(STEPS * HG):
                load_bias(sp, g)
                if n_jobs < 10 and g % 2 == 1:
                    load_job(sp, n_jobs)
                    n_jobs += 1
            for jn in range(n_jobs, len(jobs)):
                load_job(sp, jn)
            for ch in range(CHUNKS):
                sp.wait_ge(f["y"], CHUNK * EB * (CHUNKS + ch + 1))
                bt, t0 = divmod(ch * CHUNK, TILES)
                sp.dma_start(out[bt, t0 * P:(t0 + CHUNK) * P, :].rearrange("(t p) n -> p t n", p=P),
                             x[:, ch * CHUNK:(ch + 1) * CHUNK, :]).then_inc(f["out"], 16)
            sp.wait_ge(f["out"], 16 * CHUNKS)

        @block.gpsimd
        def _(pool):
            gp = nc.gpsimd
            chain = [0]

            def link(ins):
                chain[0] += 1
                ins.then_inc(pool_chain, 1)
                pool.wait_ge(pool_chain, chain[0])

            gp.memset(mhalf[:, :], -0.5).then_inc(setup["mhalf"], 1)
            link(gp.memset(ident[:, :], 0.0))
            gp.affine_select(out=ident[:, :], in_=ident[:, :], compare_op=ALU.not_equal, fill=1.0, base=0,
                             pattern=[[-1, P]], channel_multiplier=1).then_inc(setup["ident"], 1)
            link(gp.iota(rel_i[:, :], [[-P, TILES]], base=S - 1, channel_multiplier=-1))
            gp.tensor_copy(rel_f[:, :], rel_i[:, :]).then_inc(setup["rel"], 1)
            gp.memset(tab[:, S:TAB], NEG).then_inc(setup["pad"], 1)
            gp.memset(kn_b[:, :], 0.0).then_inc(setup["kn0"], 1)
            gp.memset(ones64[:, :], 1.0).then_inc(setup["ones"], 1)
            for e in range(E):
                gp.memset(place[:, e:e + 1], float(E - e)).then_inc(setup["place"], 1)
            pool.wait_ge(setup["place"], E)
            gp.memset(q_b[DH:P, :, :], BIG).then_inc(setup["big"], 1)
            pool.wait_ge(s_in["mask"], 2 * 16)
            for i in range(2):
                gp.tensor_scalar(k_b[i][DH:P, :, :].rearrange("p b n -> p (b n)"), mask8[DH:P, i, :],
                                 -1.0, BIG, ALU.add, ALU.mult).then_inc(setup["penalty"], 1)
            pool.wait_ge(setup["big"], 1)
            pool.wait_ge(setup["penalty"], 2)

            def piece(n):
                jn, hi, lo, at_, w, gain, gc = pieces[n]
                pool.wait_ge(s_stage[jn % 2], stage_value[jn])
                src = stage[:, jn % 2, at_:at_ + w]
                if gain is None:
                    link(gp.tensor_scalar(src, src, WS, 1.0, ALU.mult, ALU.mult))
                else:
                    link(gp.tensor_scalar(src, src, g_in[gain][:, gc:gc + 1], WS, ALU.mult, ALU.mult))
                link(gp.tensor_copy(hi, src))
                gp.tensor_tensor(lo, src, hi, ALU.subtract).then_inc(job_done, 1)

            split = [0]

            def split_to(n):
                while split[0] < n:
                    piece(split[0])
                    split[0] += 1

            def rel_rstd(r):
                pool.wait_ge(setup["stats"], r + 1)
                link(gp.tensor_scalar(r_rs[:, :], r_mv[:, :, 1], EPS, 0.0, ALU.add, ALU.add))
                gp.tensor_tensor(r_rs[:, :], r_rs[:, :], mhalf[:, 0:TILES], ALU.pow).then_inc(setup["rstd"], 1)

            pool.wait_ge(s_in["head"], 16 * HEAD_LOADS)
            pool.wait_ge(setup["nss"], 1)
            link(gp.tensor_tensor(null_r[:, :], null_r[:, :], mhalf[:, 0:1], ALU.pow))
            gp.tensor_scalar(null_r[:, :], null_r[:, :], 1e12, 1.0, ALU.min, ALU.mult).then_inc(setup["nrinv"], 1)
            rel_rstd(0)
            split_to(job_end[1])
            rel_rstd(1)
            split_to(job_end[2])
            for n in range(FIRST, LAST):
                m, k = divmod(n, HU)
                for T in range(STEPS):
                    n0 = T * STEP_N
                    if n == n0 - 15:
                        pool.wait_ge(s["x_st"], T + 1)
                        link(gp.tensor_scalar(rstd[:, :], mv[:, :, 1], EPS, 0.0, ALU.add, ALU.add))
                        gp.tensor_tensor(rstd[:, :], rstd[:, :], mhalf[:, 0:B], ALU.pow).then_inc(s["x_rs"], 1)
                    if n == n0 - 9 and T < TILES:
                        pool.wait_ge(s["kv_act"], 3 * (T + 1))
                        link(gp.tensor_tensor(k_r[:, :], k_ss[:, :], mhalf[:, 0:B], ALU.pow))
                        gp.tensor_scalar(k_r[:, :], k_r[:, :], 1e12 / WS, 1.0, ALU.min, ALU.mult)\
                            .then_inc(s["kv_r"], 1)
                    if n == n0 - 7 and T < TILES:
                        pool.wait_ge(s["kv_d"], T + 1)
                        gp.tensor_copy(k_d[:, :, DH:2 * DH], k_d[:, :, 0:DH]).then_inc(s["k_dup"], 1)
                if k == 0 and 1 <= m <= NU:
                    u = m - 1
                    pool.wait_ge(s["o_raw"], u + 1)
                    pool.wait_ge(s["r_den"], u + 1)
                    if u >= 1:
                        pool.wait_ge(s["ot"], u)
                    gp.tensor_tensor(o_n[:, :, :], o_raw[:, :, :],
                                     r_den[:, :].unsqueeze(2).to_broadcast([P, HU, DH]), ALU.mult)\
                        .then_inc(s["o_n"], 1)
                if k == 0 and 0 <= m + 1 < NU:
                    u = m + 1
                    pool.wait_ge(s["q_hi"], u + 1)
                    gp.tensor_copy(q_a[0:DH, u % 2, :], q_b[0:DH, u % 2, :]).then_inc(s["q_dup"], 1)
                if k == 2 and 0 <= m + 2 < U0:
                    u = m + 2
                    pool.wait_ge(s["q_ss"], u + 1)
                    link(gp.tensor_tensor(q_r[:, :], q_ss[:, :], mhalf[:, 0:HU], ALU.pow))
                    gp.tensor_scalar(q_r[:, :], q_r[:, :], 1e12 / WS, 1.0, ALU.min, ALU.mult).then_inc(s["q_r"], 1)
                g, at_g = divmod(n + 8, 2 * HU)
                if at_g == 0 and TILES * HG <= g < STEPS * HG:
                    t = (g // HG) % TILES
                    pool.wait_ge(s_bias[g % 2], 16 * (g // 2 + 1))
                    blk = bias[:, g % 2, :, t * P:(t + 1) * P]
                    gp.affine_select(out=blk, in_=blk, compare_op=ALU.is_ge, fill=NEG, base=0,
                                     pattern=[[0, HU], [-1, P]], channel_multiplier=1).then_inc(s["bias"], 1)
                if k == 3 and 0 <= m < NU:
                    u = m
                    pool.wait_ge(s["probs"], HU * (u + 1))
                    gp.tensor_tensor(d_null[:, :], neg_max[:, u % 2, :], neg_null[:, u % 2, :], ALU.subtract)\
                        .then_inc(s["d_null"], 1)
                    pool.wait_ge(s["p_null"], u + 1)
                    if u >= 1:
                        pool.wait_ge(s["r_den"], u)
                    gp.tensor_tensor(denom[:, :], rows[:, u % 2, :], p_null[:, :], ALU.add).then_inc(s["denom"], 1)
                    if u >= 1:
                        pool.wait_ge(s["o_raw"], u)
                    gp.tensor_tensor(o_null[:, :, :], null_v[:, :].unsqueeze(1).to_broadcast([P, HU, DH]),
                                     p_null[:, :].unsqueeze(2).to_broadcast([P, HU, DH]), ALU.mult)\
                        .then_inc(s["o_null"], 1)
                for p_ in range(STEPS * B):
                    T, bt = divmod(p_, B)
                    mu = T * UNITS + (HG - 1) * B + bt
                    if n == HU * (mu + 1) + 3:
                        pool.wait_ge(s["y_st"], p_ + 1)
                        link(gp.tensor_scalar(y_rs[:, :], y_mv[:, 1:2], EPS, 0.0, ALU.add, ALU.add))
                        gp.tensor_tensor(y_rs[:, :], y_rs[:, :], mhalf[:, 0:1], ALU.pow).then_inc(s["y_rs"], 1)
                    if n == HU * (mu + 2) + 1:
                        pool.wait_ge(s["y_n"], p_ + 1)
                        link(gp.tensor_tensor(y_g[:, :], y_n[:, :], g_out[T // TILES][:, :], ALU.mult))
                        x_t = x[:, bt * TILES + T % TILES, :]
                        gp.tensor_tensor(x_t, x_t, y_g[:, :], ALU.add).then_inc(s["x_new"], 1)
                if k == 1 and split[0] < job_end[9] and n >= 2 * HU * (2 * (pieces[split[0]][0] - 3) + 1):
                    split_to(split[0] + 1)
            split_to(job_end[9])
            pool.wait_ge(s["biased"], N)
            for en in range(2 * CHUNKS * EB):
                if split[0] < len(pieces):
                    split_to(split[0] + 1)
                pool.wait_ge(f["h_hi"], en + 1)
                gp.tensor_tensor(h_lo[:, en % 2, :], h_f[:, en % 2, :], h_hi[:, en % 2, :], ALU.subtract)\
                    .then_inc(f["h_lo"], 1)

        @block.scalar
        def _(act):
            ac = nc.scalar
            for i, v in enumerate(("w0", "b0", "g0", "b1", "g1")):
                act.dma_start(rvec[:, i, :], bcast(a["L0_cond_" + v], D)).then_inc(s_in["rel"], 16)
            act.dma_start(k_scale[:, :], bcast(a["L0_cond_k_scale"], DH)).then_inc(s_in["head"], 16)
            act.dma_start(q_scale[:, :], bcast(a["L0_cond_q_scale"], DH)).then_inc(s_in["head"], 16)
            for i, pre in ((0, "L0_cond_"), (1, "L1_cond_")):
                act.dma_start(g_in[i][:, :], a[pre + ("g_norm" if i == 0 else "g_in")].rearrange("(k p) -> p k", p=P),
                              allow_slow_non_contiguous=True).then_inc(s_in["head"], 16)
                act.dma_start(g_out[i][:, :], bcast(a[pre + "g_out"], D)).then_inc(s_in["head"], 16)
                act.dma_start(null_b[i][:, :], bcast(a[pre + "null_attn_bias"], H)).then_inc(s_in["head"], 16)
            act.dma_start(null_k[:, :], bcast(a["cond_64"][0, :], DH)).then_inc(s_in["head"], 16)
            act.dma_start(null_v[:, :], bcast(a["cond_64"][1, :], DH)).then_inc(s_in["head"], 16)
            act.dma_start(cond_n[:, :], a["cond_64"]).then_inc(s_in["head"], 16)
            for i, pre in ((0, "L2_cond_"), (1, "L3_cond_")):
                act.dma_start(wt_n[:, i, :], a[pre + "wt"]).then_inc(s_in["head"], 16)
                act.dma_start(wg_n[:, i, :], a[pre + "wg"]).then_inc(s_in["moe"], 16)
            for i, v in enumerate(("mask_BxS_bf1", "mask_BxS_bk0")):
                mk = a[v]
                act.dma_start(mask_words[DH:P, i, :], bass.AP(mk.tensor, mk.offset, [[0, DH], [1, B * S // 4]]))\
                    .then_inc(s_in["mask"], 16)
            act.dma_start(x[:, :, :], a["x"].rearrange("b (t p) n -> p (b t) n", p=P)).then_inc(s_in["x"], 16)

            act.wait_ge(setup["nt"], 1)
            ac.activation(kn_a[:, :], aux[:, 0:2 * P].rearrange("p (l n) -> p l n", l=2)[:, :, 0], ACT.Copy)\
                .then_inc(setup["nka"], 1)
            for r in range(2):
                act.wait_ge(setup["z"], r + 1)
                ac.activation(re, rh, ACT.Exp, scale=-1.0).then_inc(setup["exp"], 1)
                for kc in range(KC):
                    act.wait_ge(setup["pt"], KC * r + kc + 1)
                    ac.activation(rht[:, kc, :, :].rearrange("p k n -> p (k n)"), sc[kc][:, :], ACT.Copy)\
                        .then_inc(setup["t"], 1)

            for n in range(FIRST, LAST):
                m, k = divmod(n, HU)
                i = n + 1
                if 0 <= i < N:
                    w = P * (plan.tile(i) + 1)
                    u = plan.unit(i)
                    act.wait_ge(s["biased"], i + 1)
                    if i >= 2:
                        act.wait_ge(s["pt"], plan.groups_done(i - 2))
                    if i % HU == 0 and u >= 2:
                        act.wait_ge(s["denom"], u - 1)
                    ac.activation(probs[:, i % 2, 0:w], biased[:, i % 2, 0:w], ACT.Exp,
                                  bias=neg_max[:, u % 2, i % HU:i % HU + 1], scale=-1.0,
                                  accum_out=rows[:, u % 2, i % HU:i % HU + 1]).then_inc(s["probs"], 1)
                for T in range(STEPS):
                    n0 = T * STEP_N
                    layer, t = divmod(T, TILES)
                    if n == n0 - 13:
                        act.wait_ge(s["xt"], T + 1)
                        if T >= 2:
                            act.wait_ge(s["q_proj"], UNITS * (T - 1))
                        ac.activation(xt[:, T % 2, 0, :, :, :].rearrange("p b c n -> p (b c n)"), aux[:, :], ACT.Copy)\
                            .then_inc(s["xt_hi"], 1)
                    if n == n0 - 9:
                        act.wait_ge(s["kv"], T + 1)
                        kv_ps = aux[:, 0:B * 2 * DH].rearrange("p (b n) -> p b n", b=B)
                        if layer == 0:
                            for bt in range(B):
                                ac.activation(k_sq[:, bt, :], kv_ps[:, bt, 0:DH], ACT.Square,
                                              accum_out=k_ss[:, bt:bt + 1]).then_inc(s["kv_act"], 1)
                        else:
                            for i_ in range(2):
                                ac.activation(k_d[:, :, i_ * DH:(i_ + 1) * DH], kv_ps[:, :, 0:DH], ACT.Copy,
                                              scale=1.0 / WS).then_inc(s["kv_act"], 1)
                        ac.activation(v_s[layer][:, t::TILES, 0, :], kv_ps[:, :, DH:2 * DH], ACT.Copy, scale=1.0 / WS)\
                            .then_inc(s["kv_act"], 1)
                    if n == n0 - 5:
                        act.wait_ge(s["kt"], T + 1)
                        ac.activation(k_a[layer][:, :, t * P:(t + 1) * P],
                                      aux[:, 0:B * P].rearrange("p (b n) -> p b n", b=B), ACT.Copy)\
                            .then_inc(s["k_hi"], 1)
                if k == 0 and 0 <= m + 1 < NU:
                    u = m + 1
                    act.wait_ge(s["q_t"], u + 1)
                    if u >= 2:
                        act.wait_ge(s["scores"], HU * (u - 1))
                    ac.activation(q_b[0:DH, u % 2, :], aux[0:DH, :], ACT.Copy).then_inc(s["q_hi"], 1)
                if k == 3 and 0 <= m < NU:
                    u = m
                    act.wait_ge(s["d_null"], u + 1)
                    if u >= 1:
                        act.wait_ge(s["o_null"], u)
                    ac.activation(p_null[:, :], d_null[:, :], ACT.Exp).then_inc(s["p_null"], 1)
                if 0 <= n < N:
                    for gi in plan.of(n):
                        nb = plan.groups[gi][2]
                        act.wait_ge(s["pt"], gi + 1)
                        if gi >= 3:
                            act.wait_ge(s["pv"], gi - 2)
                        ac.activation(p_hi[:, gi % 3, 0:nb * P], tp[gi % 2][:, 0:nb * P], ACT.Copy)\
                            .then_inc(s["p_hi"], 1)
                if k == 1 and 0 <= m - 1 < NU:
                    u = m - 1
                    act.wait_ge(s["ot"], u + 1)
                    ac.activation(ot_hi[:, :], aux[:, 0:UW], ACT.Copy).then_inc(s["ot_hi"], 1)
                if k == 2 and 0 <= m + 2 < NU:
                    u = m + 2
                    act.wait_ge(s["q_proj"], u + 1)
                    if u < U0:
                        ac.activation(q_sq[:, :], aux[:, 0:UW], ACT.Square).then_inc(s["q_sq"], 1)
                    else:
                        ac.activation(q_n[:, :], aux[:, 0:UW], ACT.Copy, scale=DH ** -0.5 / WS).then_inc(s["q_na"], 1)

            def x_hi(cn):
                for kc, bank in enumerate((op, aux)):
                    act.wait_ge(f["xt"], KC * cn + kc + 1)
                    if cn >= 2 and kc == 0:
                        act.wait_ge(f["gu"], EB * (cn - 1))
                    ac.activation(mx_hi[:, cn % 2, kc, :], bank[:, :], ACT.Copy).then_inc(f["xt_hi"], 1)

            def gate_exp(cn):
                act.wait_ge(f["shifted"], cn + 1)
                ac.activation(gl[1][:, :, :], gl[0][:, :, :], ACT.Exp).then_inc(f["exp"], 1)

            x_hi(0)
            gate_exp(0)
            for en in range(2 * CHUNKS * EB):
                cn, e = divmod(en, EB)
                act.wait_ge(f["gu"], en + 1)
                if en >= 1:
                    act.wait_ge(f["leaky"], en)
                ac.activation(g_t, sc[en % 2][:, 0:512], ACT.Copy, scale=0.01 / WS).then_inc(f["tenth"], 1)
                act.wait_ge(f["h"], en + 1)
                if en >= 2:
                    act.wait_ge(f["down"], 2 * (en - 1))
                ac.activation(h_hi[:, en % 2, :], h_f[:, en % 2, :], ACT.Copy).then_inc(f["h_hi"], 1)
                if cn + 1 < 2 * CHUNKS and e == 4:
                    x_hi(cn + 1)
                if cn + 1 < 2 * CHUNKS and e == 6:
                    gate_exp(cn + 1)

        @block.vector
        def _(dve):
            ve = nc.vector
            chain = [0]

            def link(ins):
                chain[0] += 1
                ins.then_inc(dve_chain, 1)
                dve.wait_ge(dve_chain, chain[0])

            dve.wait_ge(s_in["head"], 16 * HEAD_LOADS)
            ve.tensor_tensor_reduce(out=null_sq[:, :], in0=null_k[:, :], in1=null_k[:, :], scale=1.0, scalar=0.0,
                                    op0=ALU.mult, op1=ALU.add, accum_out=null_r[:, :]).then_inc(setup["nss"], 1)
            link(ve.scalar_tensor_tensor(k_scale[:, :], k_scale[:, :], 8.0, q_scale[:, :], ALU.mult, ALU.mult))
            dve.wait_ge(setup["nrinv"], 1)
            for i in range(2):
                half = slice(i * DH, (i + 1) * DH)
                ve.scalar_tensor_tensor(null_kd[:, 0, half], null_k[:, :], null_r[:, 0:1], k_scale[:, :],
                                        ALU.mult, ALU.mult)
                last = ve.tensor_copy(null_kd[:, 1, half], null_k[:, :])
            last.then_inc(setup["nkd"], 1)
            dve.wait_ge(setup["nka"], 1)
            dve.wait_ge(setup["kn0"], 1)
            ve.tensor_tensor(kn_b[0:DH, :], aux[0:DH, 0:2 * P].rearrange("p (l n) -> p l n", l=2)[:, :, 0],
                             kn_a[0:DH, :], ALU.subtract).then_inc(setup["nkb"], 1)
            dve.wait_ge(setup["mt"], 1)
            link(ve.tensor_scalar(wt_f[:, :, :, :].rearrange("p l k e -> p (l k e)"), op[:, 0:32], WS, None, ALU.mult))
            for l in range(2):
                link(ve.tensor_copy(wt_s[:, l, 0, :, :], wt_f[:, l, :, :]))
                ve.tensor_tensor(wt_s[:, l, 1, :, :], wt_f[:, l, :, :], wt_s[:, l, 0, :, :], ALU.subtract)
            ve.tensor_copy(wg_t[:, :, :].rearrange("p l e -> p (l e)"), op[0:G, 32:48])
            link(ve.tensor_copy(cond_t[:, :], op[0:G, 48:50]))
            dve.wait_ge(setup["ones"], 1)
            for b in range(B):
                last = ve.tensor_scalar(cond_b[:, b, :], ones64[:, :], cond_t[:, b:b + 1], None, ALU.mult)
            last.then_inc(setup["cb"], 1)
            dve.wait_ge(setup["lg"], 1)
            ve.tensor_scalar(lg_half[:, :, :, :].rearrange("p l b e -> p (l b e)"), op[:, 64:96], 0.5, None, ALU.mult)\
                .then_inc(setup["lgh"], 1)

            dve.wait_ge(s_in["rel"], 5 * 16)
            dve.wait_ge(setup["rel"], 1)
            for k in range(TILES):
                last = ve.scalar_tensor_tensor(rh[:, k, :], rvec[:, 0, :], rel_f[:, k:k + 1], rvec[:, 1, :],
                                               ALU.mult, ALU.add)
            link(last)
            for r in range(2):
                if r == 1:
                    dve.wait_ge(setup["mm"], 1)
                    for i in range(2):
                        last = ve.tensor_tensor(rh[:, 4 * i:4 * i + 4, :],
                                                sc[i][:, :].rearrange("p (k n) -> p k n", k=4),
                                                rvec[:, 3, :].unsqueeze(1).to_broadcast([P, 4, D]), ALU.add)
                    link(last)
                for k in range(TILES):
                    last = ve.bn_stats(r_st[:, k, :], rh[:, k, :])
                link(last)
                for k in range(TILES):
                    last = ve.bn_aggr(r_mv[:, k, :], r_st[:, k, :])
                last.then_inc(setup["stats"], 1)
                dve.wait_ge(setup["rstd"], r + 1)
                for k in range(TILES):
                    last = ve.tensor_scalar(rh[:, k, :], rh[:, k, :], r_mv[:, k, 0:1], r_rs[:, k:k + 1],
                                            ALU.subtract, ALU.mult)
                link(last)
                ve.tensor_tensor(rh, rh, rvec[:, 2 + 2 * r, :].unsqueeze(1).to_broadcast([P, TILES, D]), ALU.mult)\
                    .then_inc(setup["z"], 1)
                dve.wait_ge(setup["exp"], r + 1)
                link(ve.tensor_scalar(re, re, 1.0, None, ALU.add))
                link(ve.reciprocal(re, re))
                ve.tensor_tensor(rh, rh, re, ALU.mult).then_inc(setup["h"], 1)
            for i in range(2):
                dve.wait_ge(setup["mm"], 2 + i)
                ve.tensor_scalar(tab[:, i * 512:(i + 1) * 512], tp[i][0:H, :], b2_sb[:, 0:1], None, ALU.add)\
                    .then_inc(setup["tab"], 1)

            dve.wait_ge(s_in["x"], 16)
            for n in range(FIRST, LAST):
                m, k = divmod(n, HU)
                i = n + 2
                if 0 <= i < N:
                    w = P * (plan.tile(i) + 1)
                    u = plan.unit(i)
                    g = i // (2 * HU)
                    dve.wait_ge(s["scores"], i + 1)
                    if i >= 2:
                        dve.wait_ge(s["probs"], i - 1)
                    if i % HU == 0:
                        dve.wait_ge(s["null"], u + 1)
                        if u >= 2:
                            dve.wait_ge(s["d_null"], u - 1)
                    if g < TILES * HG:
                        dve.wait_ge(s_bias[g % 2], 16 * (g // 2 + 1))
                    else:
                        dve.wait_ge(s["bias"], g - TILES * HG + 1)
                    ve.tensor_tensor_reduce(out=biased[:, i % 2, 0:w], in0=sc[i % 2][:, 0:w],
                                            in1=bias[:, g % 2, i % HU, 0:w], scale=-1.0,
                                            scalar=neg_null[:, u % 2, i % HU:i % HU + 1],
                                            op0=ALU.add, op1=ALU.min,
                                            accum_out=neg_max[:, u % 2, i % HU:i % HU + 1]).then_inc(s["biased"], 1)
                if k == 3 and 0 <= m + 2 < U0:
                    u = m + 2
                    dve.wait_ge(s["q_r"], u + 1)
                    ve.tensor_tensor(q_n[:, :].rearrange("p (h d) -> p h d", h=HU),
                                     aux[:, 0:UW].rearrange("p (h d) -> p h d", h=HU),
                                     q_r[:, :].unsqueeze(2).to_broadcast([P, HU, DH]), ALU.mult).then_inc(s["q_nd"], 1)
                for T in range(STEPS):
                    n0 = T * STEP_N
                    layer, t = divmod(T, TILES)
                    tiles = [bt * TILES + t for bt in range(B)]
                    if n == n0 - 15:
                        if layer == 1:
                            dve.wait_ge(s["x_new"], B * (T - TILES + 1))
                        for bt in range(B):
                            last = ve.bn_stats(st6[:, bt, :], x[:, tiles[bt], :])
                        link(last)
                        for bt in range(B):
                            last = ve.bn_aggr(mv[:, bt, :], st6[:, bt, :])
                        last.then_inc(s["x_st"], 1)
                    if n == n0 - 14:
                        dve.wait_ge(s["x_rs"], T + 1)
                        for bt in range(B):
                            last = ve.tensor_scalar(xn[:, bt, :], x[:, tiles[bt], :], mv[:, bt, 0:1],
                                                    rstd[:, bt:bt + 1], ALU.subtract, ALU.mult)
                        last.then_inc(s["xn"], 1)
                    if n == n0 - 13:
                        dve.wait_ge(s["xt_hi"], T + 1)
                        ve.tensor_tensor(xt[:, T % 2, 1, :, :, :].rearrange("p b c n -> p (b c n)"), aux[:, :],
                                         xt[:, T % 2, 0, :, :, :].rearrange("p b c n -> p (b c n)"), ALU.subtract)\
                            .then_inc(s["xt_lo"], 1)
                    if n == n0 - 8:
                        kv_ps = aux[:, 0:B * 2 * DH].rearrange("p (b n) -> p b n", b=B)
                        dve.wait_ge(s["kv_act"], 3 * (T + 1))
                        if layer == 0:
                            dve.wait_ge(s["kv_r"], T + 1)
                            for bt in range(B):
                                last = ve.scalar_tensor_tensor(k_d[:, bt, 0:DH], kv_ps[:, bt, 0:DH],
                                                               k_r[:, bt:bt + 1], k_scale[:, :], ALU.mult, ALU.mult)
                            last.then_inc(s["kv_d"], 1)
                        ve.scalar_tensor_tensor(v_s[layer][:, t::TILES, 1, :], kv_ps[:, :, DH:2 * DH], 1.0 / WS,
                                                v_s[layer][:, t::TILES, 0, :], ALU.mult, ALU.subtract)\
                            .then_inc(s["kv_v"], 1)
                    if n == n0 - 5:
                        dve.wait_ge(s["k_hi"], T + 1)
                        cols = slice(t * P, (t + 1) * P)
                        ve.tensor_tensor(k_b[layer][0:DH, :, cols],
                                         aux[0:DH, 0:B * P].rearrange("p (b n) -> p b n", b=B),
                                         k_a[layer][0:DH, :, cols], ALU.subtract).then_inc(s["k_lo"], 1)
                if k == 0 and 0 <= m + 1 < NU:
                    u = m + 1
                    dve.wait_ge(s["q_hi"], u + 1)
                    ve.tensor_tensor(q_a[DH:P, u % 2, :], aux[0:DH, :], q_b[0:DH, u % 2, :], ALU.subtract)\
                        .then_inc(s["q_lo"], 1)
                if k == 1 and 0 <= m + 1 < NU:
                    u = m + 1
                    hg = (u % UNITS) // B
                    dve.wait_ge(s["q_null"], u + 1)
                    if u >= 2:
                        dve.wait_ge(s["d_null"], u - 1)
                    ve.scalar_tensor_tensor(neg_null[:, u % 2, :], aux[:, 0:HU], -1.0,
                                            null_b[u // U0][:, hg * HU:(hg + 1) * HU], ALU.mult, ALU.subtract)\
                        .then_inc(s["null"], 1)
                if k == 2 and 0 <= m - 1 < NU:
                    u = m - 1
                    bt = u % B
                    dve.wait_ge(s["y"], u + 1)
                    if (u % UNITS) // B == 0:
                        T = u // UNITS
                        if T >= 1:
                            dve.wait_ge(s["y_n"], B * (T - 1) + bt + 1)
                        ve.tensor_scalar(y_acc[:, bt, :], aux[:, 0:D], 1.0 / WS, None, ALU.mult).then_inc(s["y_acc"], 1)
                    else:
                        dve.wait_ge(s["y_acc"], u - 1)
                        ve.scalar_tensor_tensor(y_acc[:, bt, :], aux[:, 0:D], 1.0 / WS, y_acc[:, bt, :],
                                                ALU.mult, ALU.add).then_inc(s["y_acc"], 1)
                def o_evict():
                    u = m - 1
                    dve.wait_ge(s["denom"], u + 1)
                    ve.reciprocal(r_den[:, :], denom[:, :]).then_inc(s["r_den"], 1)
                    dve.wait_ge(s["o_null"], u + 1)
                    dve.wait_ge(s["pv"], plan.groups_done(n - 1))
                    ve.tensor_tensor(o_raw[:, :, :], op[:, 0:UW].rearrange("p (h d) -> p h d", h=HU),
                                     o_null[:, :, :], ALU.add).then_inc(s["o_raw"], 1)

                if 0 <= n < N:
                    for gi in plan.of(n):
                        nb = plan.groups[gi][2]
                        dve.wait_ge(s["p_hi"], gi + 1)
                        ve.tensor_tensor(p_lo[:, gi % 3, 0:nb * P], tp[gi % 2][:, 0:nb * P],
                                         p_hi[:, gi % 3, 0:nb * P], ALU.subtract).then_inc(s["p_lo"], 1)
                        if k == 0 and m >= 1 and gi == plan.first_group[n]:
                            o_evict()
                elif n == N:
                    o_evict()
                if k == 1 and 0 <= m - 1 < NU:
                    u = m - 1
                    dve.wait_ge(s["ot_hi"], u + 1)
                    ve.tensor_tensor(ot_lo[:, :], aux[:, 0:UW], ot_hi[:, :], ALU.subtract).then_inc(s["ot_lo"], 1)
                if k == 2 and 0 <= m + 2 < U0:
                    u = m + 2
                    dve.wait_ge(s["q_sq"], u + 1)
                    ve.reduce_sum(q_ss[:, :], q_sq[:, :].rearrange("p (h d) -> p h d", h=HU), AX)\
                        .then_inc(s["q_ss"], 1)
                for p_ in range(STEPS * B):
                    T, bt = divmod(p_, B)
                    mu = T * UNITS + (HG - 1) * B + bt
                    if n == HU * (mu + 1) + 3:
                        dve.wait_ge(s["y_acc"], mu + 1)
                        link(ve.bn_stats(y_st[:, :], y_acc[:, bt, :]))
                        ve.bn_aggr(y_mv[:, :], y_st[:, :]).then_inc(s["y_st"], 1)
                    if n == HU * (mu + 2):
                        dve.wait_ge(s["y_rs"], p_ + 1)
                        ve.tensor_scalar(y_n[:, :], y_acc[:, bt, :], y_mv[:, 0:1], y_rs[:, 0:1],
                                         ALU.subtract, ALU.mult).then_inc(s["y_n"], 1)

            def x_lo(cn):
                for kc, bank in enumerate((op, aux)):
                    dve.wait_ge(f["xt_hi"], KC * cn + kc + 1)
                    ve.tensor_tensor(mx_lo[:, cn % 2, kc, :], bank[:, :], mx_hi[:, cn % 2, kc, :], ALU.subtract)\
                        .then_inc(f["xt_lo"], 1)

            def over_e(t_):
                return t_[:, :].unsqueeze(2).to_broadcast([P, CHUNK, E])

            def gate_shift(cn):
                layer, ch = divmod(cn, CHUNKS)
                bt = ch * CHUNK // TILES
                dve.wait_ge(f["logit"], cn + 1)
                link(ve.scalar_tensor_tensor(gl[2][:, :, :], aux[:, 0:CHUNK * E].rearrange("p (t e) -> p t e", t=CHUNK),
                                             0.5 / WS, lg_half[:, layer, bt, :].unsqueeze(1).to_broadcast([P, CHUNK, E]),
                                             ALU.mult, ALU.add))
                link(ve.reduce_max(gm[0][:, :], gl[2][:, :, :], AX))
                ve.tensor_tensor(gl[0][:, :, :], gl[2][:, :, :], over_e(gm[0]), ALU.subtract).then_inc(f["shifted"], 1)

            def gate_pick(cn):
                dve.wait_ge(f["exp"], cn + 1)
                sc_ = gl[2]
                link(ve.reduce_sum(gm[0][:, :], gl[1][:, :, :], AX))
                link(ve.reciprocal(gm[1][:, :], gm[0][:, :]))
                link(ve.tensor_tensor(sc_[:, :, :], gl[1][:, :, :], over_e(gm[1]), ALU.mult))
                left = sc_
                order = place[:, :].unsqueeze(1).to_broadcast([P, CHUNK, E])
                for r in range(2):
                    link(ve.reduce_max(gm[2 + r][:, :], left[:, :, :], AX))
                    link(ve.tensor_tensor(gl[3][:, :, :], left[:, :, :], over_e(gm[2 + r]), ALU.is_equal))
                    link(ve.tensor_tensor(gl[3][:, :, :], gl[3][:, :, :], order, ALU.mult))
                    link(ve.reduce_max(gm[4][:, :], gl[3][:, :, :], AX))
                    link(ve.tensor_tensor(gl[3][:, :, :], gl[3][:, :, :], over_e(gm[4]), ALU.is_equal))
                    link(ve.scalar_tensor_tensor(gl[4 + r][:, :, :], gl[3][:, :, :], -4.0, left[:, :, :],
                                                 ALU.mult, ALU.add))
                    left = gl[4 + r]
                link(ve.scalar_tensor_tensor(gm[4][:, :], gm[2][:, :], 1e-20, gm[3][:, :], ALU.add, ALU.add))
                link(ve.reciprocal(gm[5][:, :], gm[4][:, :]))
                link(ve.tensor_scalar(gl[3][:, :, :], left[:, :, :], 0.0, 1.0 / WS, ALU.is_lt, ALU.mult))
                link(ve.tensor_tensor(gl[3][:, :, :], gl[3][:, :, :], sc_[:, :, :], ALU.mult))
                ve.tensor_tensor(comb[:, cn % 2, :, :], gl[3][:, :, :], over_e(gm[5]), ALU.mult).then_inc(f["comb"], 1)

            def y_evict(en):
                cn, e = divmod(en, EB)
                ch = cn % CHUNKS
                for i in range(CHUNK):
                    if i % 2 == 0:
                        dve.wait_ge(f["down"], 2 * en + i // 2 + 1)
                    if e == 0 and i == 0:
                        dve.wait_ge(f["comb"], cn + 1)
                    if e > 0:
                        dve.wait_ge(f["y"], CHUNK * (en - 1) + i + 1)
                    x_t = x[:, ch * CHUNK + i, :]
                    weight = comb[:, cn % 2, i, e:e + 1] if e < E else 1.0 / WS
                    ve.scalar_tensor_tensor(x_t, tp[i // 2][:, (i % 2) * D:(i % 2 + 1) * D], weight, x_t,
                                            ALU.mult, ALU.add).then_inc(f["y"], 1)

            dve.wait_ge(setup["place"], E)
            x_lo(0)
            gate_shift(0)
            gate_pick(0)
            for en in range(2 * CHUNKS * EB + 1):
                cn, e = divmod(en, EB)
                if en < 2 * CHUNKS * EB:
                    dve.wait_ge(f["tenth"], en + 1)
                    ve.scalar_tensor_tensor(g_l, sc[en % 2][:, 0:512], 1.0 / WS, g_t, ALU.mult, ALU.max)\
                        .then_inc(f["leaky"], 1)
                    dve.wait_ge(f["leaky"], en + 1)
                    if en >= 2:
                        dve.wait_ge(f["h_lo"], en - 1)
                    ve.scalar_tensor_tensor(h_f[:, en % 2, :], sc[en % 2][:, 512:1024], 1.0 / WS, g_l,
                                            ALU.mult, ALU.mult).then_inc(f["h"], 1)
                if en >= 1:
                    y_evict(en - 1)
                if cn + 1 < 2 * CHUNKS:
                    if e == 4:
                        x_lo(cn + 1)
                    if e == 6:
                        gate_shift(cn + 1)
                    if e == 7:
                        gate_pick(cn + 1)

        @block.tensor
        def _(pe):
            te = nc.tensor

            def three(out_, l_hi, l_lo, r_hi, r_lo, first, last):
                te.matmul(out_, l_hi, r_hi, start=first, stop=False)
                te.matmul(out_, l_hi, r_lo, start=False, stop=False)
                return te.matmul(out_, l_lo, r_hi, start=False, stop=last)

            pe.wait_ge(setup["ident"], 1)
            pe.wait_ge(setup["nkd"], 1)
            for i in range(2):
                last = te.transpose(aux[:, i * P:(i + 1) * P], null_kd[:, i, :], ident[:, :])
            last.then_inc(setup["nt"], 1)
            pe.wait_ge(s_in["head"], 16 * HEAD_LOADS)
            pe.wait_ge(s_in["moe"], 2 * 16)
            for l in range(2):
                for kc in range(KC):
                    at_ = (l * KC + kc) * E
                    te.transpose(op[:, at_:at_ + E], wt_n[:, l, kc * P:(kc + 1) * P], ident[0:E, 0:E])
                te.transpose(op[0:G, 32 + l * E:32 + (l + 1) * E], wg_n[:, l, :], ident[0:E, 0:E])
            te.transpose(op[0:G, 48:50], cond_n[:, :], ident[0:B, 0:B]).then_inc(setup["mt"], 1)
            pe.wait_ge(setup["cb"], 1)
            for l in range(2):
                for b in range(B):
                    at_ = 64 + (l * B + b) * E
                    last = te.matmul(op[:, at_:at_ + E], cond_b[:, b, :], wg_t[:, l, :], start=True, stop=True)
            last.then_inc(setup["lg"], 1)
            for r in range(2):
                pe.wait_ge(setup["h"], r + 1)
                for kc in range(KC):
                    for k in range(TILES):
                        last = te.transpose(sc[kc][:, k * P:(k + 1) * P], rh[:, k, kc * P:(kc + 1) * P], ident[:, :])
                    last.then_inc(setup["pt"], 1)
                pe.wait_ge(setup["t"], KC * (r + 1))
                if r == 0:
                    pe.wait_ge(s_in["w1"], 16)
                    for k in range(TILES):
                        for kc in range(KC):
                            last = te.matmul(sc[k // 4][:, (k % 4) * D:(k % 4 + 1) * D], rht[:, kc, k, :],
                                             w1_sb[:, kc, :], start=(kc == 0), stop=(kc == KC - 1))
                    last.then_inc(setup["mm"], 1)
                else:
                    pe.wait_ge(s_in["w2"], 2 * 16)
                    for i in range(2):
                        for kc in range(KC):
                            last = te.matmul(tp[i][0:H, :], w2_sb[:, kc, :],
                                             rht[:, kc, 4 * i:4 * i + 4, :].rearrange("p k n -> p (k n)"),
                                             start=(kc == 0), stop=(kc == KC - 1))
                        last.then_inc(setup["mm"], 1)

            free = [(setup["nkb"], 1)]

            def take_aux(*after):
                for sem_, value in free:
                    pe.wait_ge(sem_, value)
                free[:] = after

            def pv(gi):
                n, j0, nb = plan.groups[gi]
                layer, h = plan.layer(n), n % HU
                bt = plan.unit(n) % B
                nk = plan.tile(n) + 1
                if gi == plan.first_group[n] and h == 0 and n > 0:
                    pe.wait_ge(s["o_raw"], plan.unit(n))
                if gi == plan.first_group[n] and plan.unit(n) % UNITS == 0 and h == 0:
                    pe.wait_ge(s["kv_v"], plan.unit(n) // UNITS + 1)
                pe.wait_ge(s["p_lo"], gi + 1)
                o_h = op[:, h * DH:(h + 1) * DH]
                for jj in range(nb):
                    j = j0 + jj
                    v_hi = v_s[layer][:, bt * TILES + j, 0, :]
                    v_lo = v_s[layer][:, bt * TILES + j, 1, :]
                    cols = slice(jj * P, (jj + 1) * P)
                    last = three(o_h, p_hi[:, gi % 3, cols], p_lo[:, gi % 3, cols], v_hi, v_lo,
                                 j == 0, j == nk - 1)
                last.then_inc(s["pv"], 1)

            for n in range(FIRST, LAST):
                m, k = divmod(n, HU)
                i = n + 2
                if 0 <= i < N:
                    layer, t, u = plan.layer(i), plan.tile(i), plan.unit(i)
                    bt, h = u % B, i % HU
                    if i == 0:
                        pe.wait_ge(setup["penalty"], 2)
                        pe.wait_ge(setup["mm"], 3)
                    if h == 0:
                        pe.wait_ge(s["q_dup"], u + 1)
                        pe.wait_ge(s["q_lo"], u + 1)
                        if u % UNITS == 0:
                            pe.wait_ge(s["k_lo"], u // UNITS + 1)
                    if i >= 2:
                        pe.wait_ge(s["biased"], i - 1)
                    cols = slice(h * P, (h + 1) * P)
                    w = P * (t + 1)
                    for c0 in range(0, w, 512):
                        cw = min(512, w - c0)
                        o_ = sc[i % 2][:, c0:c0 + cw]
                        te.matmul(o_, q_a[:, u % 2, cols], k_a[layer][:, bt, c0:c0 + cw], start=True, stop=False)
                        last = te.matmul(o_, q_b[:, u % 2, cols], k_b[layer][:, bt, c0:c0 + cw],
                                         start=False, stop=True)
                    last.then_inc(s["scores"], 1)
                for T in range(STEPS):
                    n0 = T * STEP_N
                    layer, t = divmod(T, TILES)
                    if n == n0 - 13:
                        take_aux((s["xt_lo"], T + 1))
                        pe.wait_ge(s["xn"], T + 1)
                        for bt in range(B):
                            for kc in range(KC):
                                at_ = (bt * KC + kc) * P
                                last = te.transpose(aux[:, at_:at_ + P], xn[:, bt, kc * P:(kc + 1) * P], ident[:, :])
                        last.then_inc(s["xt"], 1)
                    if n == n0 - 9:
                        take_aux((s["kv_v"], T + 1))
                        pe.wait_ge(s["xt_lo"], T + 1)
                        if t == 0:
                            pe.wait_ge(job_done, job_end[3 * layer + 1])
                        for bt in range(B):
                            for kc in range(KC):
                                last = three(aux[:, bt * 2 * DH:(bt + 1) * 2 * DH],
                                             xt[:, T % 2, 0, bt, kc, :], xt[:, T % 2, 1, bt, kc, :],
                                             wkv[layer][:, 0, kc, :], wkv[layer][:, 1, kc, :],
                                             kc == 0, kc == KC - 1)
                        last.then_inc(s["kv"], 1)
                    if n == n0 - 5:
                        take_aux((s["k_lo"], T + 1))
                        if layer == 0:
                            pe.wait_ge(s["k_dup"], T + 1)
                        for bt in range(B):
                            last = te.transpose(aux[:, bt * P:(bt + 1) * P], k_d[:, bt, :], ident[:, :])
                        last.then_inc(s["kt"], 1)
                if k == 0 and 0 <= m + 1 < NU:
                    u = m + 1
                    take_aux((s["q_lo"], u + 1))
                    if u >= U0:
                        pe.wait_ge(s["q_na"], u - U0 + 1)
                    for h in range(HU):
                        last = te.transpose(aux[0:DH, h * P:(h + 1) * P], q_n[:, h * DH:(h + 1) * DH], ident[:, :])
                    last.then_inc(s["q_t"], 1)
                if k == 1 and 0 <= m + 1 < NU:
                    u = m + 1
                    layer = u // U0
                    take_aux((s["null"], u + 1))
                    pe.wait_ge(s["q_dup"], u + 1)
                    if u == 0:
                        pe.wait_ge(setup["big"], 1)
                    for h in range(HU):
                        cols = slice(h * P, (h + 1) * P)
                        te.matmul(aux[:, h:h + 1], q_a[:, u % 2, cols], kn_a[:, layer:layer + 1], start=True, stop=False)
                        last = te.matmul(aux[:, h:h + 1], q_b[:, u % 2, cols], kn_b[:, layer:layer + 1],
                                         start=False, stop=True)
                    last.then_inc(s["q_null"], 1)
                if k == 2 and 0 <= m - 1 < NU:
                    u = m - 1
                    layer, hg = u // U0, (u % UNITS) // B
                    take_aux((s["y_acc"], u + 1))
                    if u % U0 == 0:
                        pe.wait_ge(job_done, job_end[3 * layer + 2])
                    for cc in range(UW // P):
                        rows_ = hg * (UW // P) + cc
                        last = three(aux[:, 0:D], ot_hi[:, cc * P:(cc + 1) * P], ot_lo[:, cc * P:(cc + 1) * P],
                                     wo[layer][:, 0, rows_, :], wo[layer][:, 1, rows_, :],
                                     cc == 0, cc == UW // P - 1)
                    last.then_inc(s["y"], 1)
                if 0 <= n < N:
                    for gi in plan.of(n):
                        _, j0, nb = plan.groups[gi]
                        pe.wait_ge(s["probs"], n + 1)
                        if gi >= 2:
                            pe.wait_ge(s["p_lo"], gi - 1)
                        for jj in range(nb):
                            j = j0 + jj
                            last = te.transpose(tp[gi % 2][:, jj * P:(jj + 1) * P],
                                                probs[:, n % 2, j * P:(j + 1) * P], ident[:, :])
                        last.then_inc(s["pt"], 1)
                        if gi >= 1:
                            pv(gi - 1)
                elif n == N:
                    pv(len(plan.groups) - 1)
                if k == 1 and 0 <= m - 1 < NU:
                    u = m - 1
                    take_aux((s["ot_lo"], u + 1))
                    pe.wait_ge(s["o_n"], u + 1)
                    o_f = o_n[:, :, :].rearrange("p h d -> p (h d)")
                    for cc in range(UW // P):
                        last = te.transpose(aux[:, cc * P:(cc + 1) * P], o_f[:, cc * P:(cc + 1) * P], ident[:, :])
                    last.then_inc(s["ot"], 1)
                if k == 2 and 0 <= m + 2 < NU:
                    u = m + 2
                    layer = u // U0
                    T, hg, bt = u // UNITS, (u % UNITS) // B, u % B
                    take_aux((s["q_nd"], u + 1) if u < U0 else (s["q_na"], u - U0 + 1))
                    if hg == 0:
                        pe.wait_ge(s["xt_lo"], T + 1)
                        if T % TILES == 0:
                            pe.wait_ge(job_done, job_end[3 * layer])
                    for kc in range(KC):
                        cols = slice(hg * UW, (hg + 1) * UW)
                        last = three(aux[:, 0:UW], xt[:, T % 2, 0, bt, kc, :], xt[:, T % 2, 1, bt, kc, :],
                                     wq[layer][:, 0, kc, cols], wq[layer][:, 1, kc, cols],
                                     kc == 0, kc == KC - 1)
                    last.then_inc(s["q_proj"], 1)

            def x_t(cn):
                ch = cn % CHUNKS
                for kc, bank in enumerate((op, aux)):
                    if cn == 0:
                        for sem_, value in free:
                            pe.wait_ge(sem_, value)
                        pe.wait_ge(s["x_new"], STEPS * B)
                    else:
                        pe.wait_ge(f["xt_lo"], KC * (cn - 1) + kc + 1)
                        if kc == 1:
                            pe.wait_ge(f["shifted"], cn)
                    if cn >= CHUNKS:
                        pe.wait_ge(f["y"], CHUNK * EB * (cn - CHUNKS + 1))
                    for i_ in range(CHUNK):
                        last = te.transpose(bank[:, i_ * P:(i_ + 1) * P], x[:, ch * CHUNK + i_, kc * P:(kc + 1) * P],
                                            ident[:, :])
                    last.then_inc(f["xt"], 1)

            def logits(cn):
                layer = cn // CHUNKS
                pe.wait_ge(f["xt_lo"], KC * (cn + 1))
                for i_ in range(CHUNK):
                    cols = slice(i_ * P, (i_ + 1) * P)
                    for kc in range(KC):
                        last = three(aux[:, i_ * E:(i_ + 1) * E], mx_hi[:, cn % 2, kc, cols], mx_lo[:, cn % 2, kc, cols],
                                     wt_s[:, layer, 0, kc, :], wt_s[:, layer, 1, kc, :], kc == 0, kc == KC - 1)
                last.then_inc(f["logit"], 1)

            def gate_up(en):
                cn, e = divmod(en, EB)
                layer = cn // CHUNKS
                if en >= 2:
                    pe.wait_ge(f["h"], en - 1)
                if cn % CHUNKS == 0:
                    pe.wait_ge(job_done, job_end[9 + 4 * layer] if e >= E else job_end[7 + 4 * layer])
                for name, at_ in (("gate", 0), ("up", 512)):
                    for kc in range(KC):
                        if e < E:
                            w_hi, w_lo = (moe_view(layer, hl, name, 2048)[:, (e * KC + kc) * M:(e * KC + kc + 1) * M]
                                          for hl in range(2))
                        else:
                            c0 = kc * SM + (e - E) * M
                            w_hi, w_lo = (moe_view(layer, hl, "s" + name, 512)[:, c0:c0 + M] for hl in range(2))
                        last = three(sc[en % 2][:, at_:at_ + 512], w_hi, w_lo,
                                     mx_hi[:, cn % 2, kc, :], mx_lo[:, cn % 2, kc, :], kc == 0, kc == KC - 1)
                last.then_inc(f["gu"], 1)

            def down(en):
                cn, e = divmod(en, EB)
                layer = cn // CHUNKS
                pe.wait_ge(f["h_lo"], en + 1)
                if cn % CHUNKS == 0:
                    pe.wait_ge(job_done, job_end[9 + 4 * layer] if e >= E else job_end[8 + 4 * layer])
                name, c0 = ("down", e * D) if e < E else ("sdown", (e - E) * D)
                size = 2048 if e < E else 512
                w_hi, w_lo = (moe_view(layer, hl, name, size)[:, c0:c0 + D] for hl in range(2))
                for i_ in range(CHUNK):
                    if i_ % 2 == 0 and en >= 1:
                        pe.wait_ge(f["y"], CHUNK * (en - 1) + i_ + 2)
                    cols = slice(i_ * P, (i_ + 1) * P)
                    last = three(tp[i_ // 2][:, (i_ % 2) * D:(i_ % 2 + 1) * D], h_hi[:, en % 2, cols],
                                 h_lo[:, en % 2, cols], w_hi, w_lo, True, True)
                    if i_ % 2 == 1:
                        last.then_inc(f["down"], 1)

            x_t(0)
            logits(0)
            for en in range(2 * CHUNKS * EB + 1):
                cn, e = divmod(en, EB)
                if en < 2 * CHUNKS * EB:
                    gate_up(en)
                if en >= 1:
                    down(en - 1)
                if cn + 1 < 2 * CHUNKS:
                    if e == 4:
                        x_t(cn + 1)
                    if e == 6:
                        logits(cn + 1)


def kernel(**inputs):
    import numpy as np
    import concourse.bacc as bacc
    from concourse.bass_utils import run_bass_kernel_spmd

    nc = bacc.Bacc("TRN2", target_bir_lowering=False, num_devices=1)
    arrays, aps = {}, {}
    for name, value in inputs.items():
        v = np.ascontiguousarray(value)
        if v.dtype == np.bool_:
            v = v.view(np.int32)
        arrays["in_" + name] = v
        aps[name] = nc.dram_tensor("in_" + name, v.shape, mybir.dt.from_np(v.dtype), kind="ExternalInput").ap()
    out = nc.dram_tensor("out", (B, S, D), F32, kind="ExternalOutput").ap()
    model(nc, aps, out)
    return run_bass_kernel_spmd(nc, [arrays], core_ids=[0]).results[0]["out"]
```

```python
import concourse.bass as bass
from concourse import mybir
from contextlib import ExitStack

F32 = mybir.dt.float32
F16 = mybir.dt.float16
I32 = mybir.dt.int32
U8 = mybir.dt.uint8
ALU = mybir.AluOpType
ACT = mybir.ActivationFunctionType
AX = mybir.AxisListType.X

P = 128
B, S, D = 2, 1024, 256
H, DH = 16, 64
INNER = H * DH
TILES = S // P
KC = D // P
HU = 4
HG = H // HU
UNITS = HG * B
STEPS = 2 * TILES
UW = HU * DH
E, M = 8, 128
SM = 256
G = 64
CHUNK = 4
CHUNKS = B * TILES // CHUNK
EB = E + SM // M

WS = 256.0
BIG = 60000.0
NEG = -1.0e30
EPS = 1e-5
TAB = S + P


class Plan:

    def __init__(self):
        self.steps = STEPS * UNITS * HU
        self.groups = []
        self.first_group = []
        for n in range(self.steps):
            self.first_group.append(len(self.groups))
            nk = self.tile(n) + 1
            for j in range(0, nk, 4):
                self.groups.append((n, j, min(4, nk - j)))
        self.first_group.append(len(self.groups))

    def tile(self, n):
        return (n // (UNITS * HU)) % TILES

    def layer(self, n):
        return n // (UNITS * HU * TILES)

    def unit(self, n):
        return n // HU

    def of(self, n):
        return range(self.first_group[n], self.first_group[n + 1])

    def at(self, n):
        return list(self.of(n)) if 0 <= n < self.steps else []

    def groups_done(self, n):
        return self.first_group[n + 1]


def model(nc, a, out):
    plan = Plan()
    N = plan.steps
    ctx = ExitStack()
    with ctx:
        def sb(name, shape, dt=F32):
            return ctx.enter_context(nc.sbuf_tensor(name, shape, dt))

        def pb(name, shape):
            return ctx.enter_context(nc.psum_tensor(name, shape, F32))

        def sem(name):
            return ctx.enter_context(nc.semaphore(name))

        table = nc.dram_tensor("rel_table", (H, P, TAB + P), F32).ap()

        x = sb("x", [P, B * TILES, D])
        bias = sb("bias", [P, 2, HU, S])
        moe_w = sb("moe_w", [P, 7680])
        wq = [sb(f"wq{i}", [P, 2, KC, INNER], F16) for i in range(2)]
        wkv = [sb(f"wkv{i}", [P, 2, KC, 2 * DH], F16) for i in range(2)]
        wo = [sb(f"wo{i}", [P, 2, INNER // P, D], F16) for i in range(2)]
        stage = sb("stage", [P, 2, 2048])
        k_a = [sb(f"k_a{i}", [P, B, S], F16) for i in range(2)]
        k_b = [sb(f"k_b{i}", [P, B, S], F16) for i in range(2)]
        v_s = [sb(f"v_s{i}", [P, B * TILES, 2, DH], F16) for i in range(2)]
        q_a = sb("q_a", [P, 2, HU * P], F16)
        q_b = sb("q_b", [P, 2, HU * P], F16)
        q_n = sb("q_n", [P, 2, UW])
        q_sq = sb("q_sq", [P, UW])
        q_ss = sb("q_ss", [P, HU])
        q_r = sb("q_r", [P, HU])
        xt = sb("xt", [P, 2, 2, B, KC, P], F16)
        xn = sb("xn", [P, B, D])
        st6 = sb("st6", [P, B, 6])
        mv = sb("mv", [P, B, 2])
        rstd = sb("rstd", [P, B])
        k_d = sb("k_d", [P, B, 2 * DH])
        k_sq = sb("k_sq", [P, B, DH])
        k_ss = sb("k_ss", [P, B])
        k_r = sb("k_r", [P, B])
        biased = sb("biased", [P, 2, S])
        probs = sb("probs", [P, 2, S])
        p_hi = sb("p_hi", [P, 4, 4 * P], F16)
        p_lo = sb("p_lo", [P, 4, 4 * P], F16)
        neg_null = sb("neg_null", [P, 2, HU])
        neg_max = sb("neg_max", [P, 2, HU])
        rows = sb("rows", [P, 2, HU])
        d_null = sb("d_null", [P, HU])
        p_null = sb("p_null", [P, HU])
        denom = sb("denom", [P, HU])
        r_den = sb("r_den", [P, HU])
        o_null = sb("o_null", [P, HU, DH])
        o_raw = sb("o_raw", [P, HU, DH])
        o_n = sb("o_n", [P, HU, DH])
        ot_hi = sb("ot_hi", [P, UW], F16)
        ot_lo = sb("ot_lo", [P, UW], F16)
        y_acc = sb("y_acc", [P, B, D])
        y_st = sb("y_st", [P, 6])
        y_mv = sb("y_mv", [P, 2])
        y_rs = sb("y_rs", [P, 1])
        y_n = sb("y_n", [P, D])
        ident = sb("ident", [P, P])
        mhalf = sb("mhalf", [P, 16])
        k_scale = sb("k_scale", [P, DH])
        q_scale = sb("q_scale", [P, DH])
        null_b = [sb(f"null_b{i}", [P, H]) for i in range(2)]
        null_k = sb("null_k", [P, DH])
        null_kd = p_hi[:, 0, :].bitcast(F32).rearrange("p (l n) -> p l n", l=2)
        null_v = sb("null_v", [P, DH])
        null_sq = sb("null_sq", [P, DH])
        null_r = sb("null_r", [P, 1])
        kn_a = sb("kn_a", [P, 2], F16)
        kn_b = sb("kn_b", [P, 2], F16)
        g_in = [sb(f"g_in{i}", [P, KC]) for i in range(2)]
        g_out = [sb(f"g_out{i}", [P, D]) for i in range(2)]
        mask_words = probs[:, 0, :].bitcast(I32).rearrange("p (l n) -> p l n", l=2)
        mask8 = probs[:, 0, :].bitcast(U8).rearrange("p (l n) -> p l n", l=2)
        ones64 = sb("ones64", [G, P])
        w1_sb = bias[:, 1, 0, 0:KC * D].rearrange("p (k n) -> p k n", k=KC)
        w2_sb = bias[:, 1, 1, 0:KC * H].rearrange("p (k n) -> p k n", k=KC)
        b2_sb = sb("b2_sb", [H, 1])
        rel_i = sb("rel_i", [P, TILES], I32)
        rel_f = sb("rel_f", [P, TILES])
        r_st = sb("r_st", [P, TILES, 6])
        r_mv = sb("r_mv", [P, TILES, 2])
        r_rs = sb("r_rs", [P, TILES])
        rh = moe_w[:, 0:2048].rearrange("p (k n) -> p k n", k=TILES)
        re = moe_w[:, 2048:4096].rearrange("p (k n) -> p k n", k=TILES)
        rht = moe_w[:, 4096:6144].rearrange("p (c k n) -> p c k n", c=KC, k=TILES)
        rvec = moe_w[:, 6144:7424].rearrange("p (v n) -> p v n", v=5)
        tab = biased[0:H, :, :].rearrange("p a n -> p (a n)")[:, 0:TAB]
        wt_n = sb("wt_n", [E, 2, D])
        wg_n = sb("wg_n", [E, 2, G])
        cond_n = sb("cond_n", [B, G])
        wt_s = sb("wt_s", [P, 2, 2, KC, E], F16)
        wt_f = sb("wt_f", [P, 2, KC, E])
        wg_t = sb("wg_t", [G, 2, E])
        cond_t = sb("cond_t", [G, B])
        cond_b = p_lo[0:G, 0, :].bitcast(F32).rearrange("p (b n) -> p b n", b=B)
        lg_half = sb("lg_half", [P, 2, B, E])
        place = sb("place", [P, E])
        mx_hi, mx_lo = (t_[:, :, :].rearrange("p a (k n) -> p a k n", k=KC) for t_ in (k_a[0], k_b[0]))
        gl = [sb(f"gl{i}", [P, CHUNK, E]) for i in range(6)]
        gm = [sb(f"gm{i}", [P, CHUNK]) for i in range(6)]
        comb = sb("comb", [P, 2, CHUNK, E])
        g_t = biased[:, 0, 0:512]
        g_l = biased[:, 1, 0:512]
        h_f = probs[:, :, 0:512]
        h_hi = p_hi[:, 0:2, :]
        h_lo = p_lo[:, 0:2, :]
        moe_h = [moe_w[:, :].bitcast(F16),
                 bias[:, :, :, :].rearrange("p a h n -> p (a h n)")[:, 0:7680].bitcast(F16)]

        def moe_view(layer, hl, off, n):
            base = 2 * off_base[off]
            size = off_size[off]
            return moe_h[layer][:, base + hl * size: base + hl * size + n]

        sizes = {"gate": 2048, "up": 2048, "down": 2048, "sgate": 512, "sup": 512, "sdown": 512}
        off_base, off_size, at = {}, {}, 0
        for name, size in sizes.items():
            off_base[name], off_size[name] = at, size
            at += size

        sc = [pb(f"sc{i}", [P, S]) for i in range(2)]
        tp = [pb(f"tp{i}", [P, 512]) for i in range(2)]
        op = pb("op", [P, 512])
        aux = pb("aux", [P, 512])

        def free_banks(n):
            return n < N - 4 and all(plan.tile(max(i, 0)) < TILES // 2 for i in range(n + 1, n + 4))

        def banks(n):
            if free_banks(n):
                return aux, sc[n // 2 % 2][:, 512:1024]
            return aux, aux

        def sems(part, names):
            return {name: sem(part + "_" + name) for name in names.split()}

        setup = sems("setup", """mhalf ident rel kn0 place ones penalty big pad nss nrinv nkd nt nka nkb
                    mt mtd cb lg lgh stats rstd z tanh h pt t mm tab""")
        s = sems("attn", """scores bias biased probs
                    pt p_hi p_lo pv
                    q_proj q_sq q_ss q_r q_nd q_na q_t q_hi q_lo q_dup q_null null
                    x_st x_rs xn xt xt_hi xt_lo kv kv_act kv_r kv_d kv_v k_dup kt k_hi k_lo
                    d_null p_null denom r_den o_null o_raw o_n ot ot_hi ot_lo y y_acc
                    y_st y_rs y_n x_new""")
        f = sems("moe", """xt xt_hi xt_lo logit shifted exp comb gu tenth leaky h h_hi h_lo down y out""")
        job_done = sem("job_done")
        dve_chain = sem("dve_chain")
        pool_chain = sem("pool_chain")
        table_in = [sem(f"table_in{i}") for i in range(HG)]
        s_bias = [sem(f"bias_in{i}") for i in range(2)]
        s_stage = [sem(f"stage_in{i}") for i in range(2)]
        s_in = {name: sem("in_" + name) for name in ("x", "rel", "w1", "w2", "head", "mask", "moe")}

        def bcast(ap, n):
            return bass.AP(ap.tensor, ap.offset, [[0, P], [1, n]])

        def flat(t):
            names_ = {3: "p a b -> p (a b)", 4: "p a b c -> p (a b c)"}
            return t.rearrange(names_[len(t.shape)]) if len(t.shape) > 2 else t

        jobs = []
        for i, pre in ((0, "L0_cond_"), (1, "L1_cond_")):
            w_o = a[pre + ("Wout" if i == 0 else "Wo")]
            jobs.append(([(a[pre + "Wq"].rearrange("(k p) n -> p k n", p=P), 0, (KC, INNER))],
                         [(flat(wq[i][:, 0]), flat(wq[i][:, 1]), 0, 2048)], i, INNER))
            jobs.append(([(a[pre + "Wkv"].rearrange("(k p) n -> p k n", p=P), 0, (KC, 2 * DH))],
                         [(flat(wkv[i][:, 0]), flat(wkv[i][:, 1]), 0, 256)], i, 2 * DH))
            jobs.append(([(w_o.rearrange("(c p) n -> p c n", p=P), 0, (INNER // P, D))],
                         [(flat(wo[i][:, 0]), flat(wo[i][:, 1]), 0, 2048)], None, 0))
        for i, pre in ((0, "L2_cond_"), (1, "L3_cond_")):
            def ends(name):
                return moe_view(i, 0, name, sizes[name]), moe_view(i, 1, name, sizes[name])
            jobs.append(([(a[pre + "w_gate"].rearrange("e (k p) m -> p (e k) m", p=P), 0, (E * KC, M))],
                         [(*ends("gate"), 0, 2048)], None, 0))
            jobs.append(([(a[pre + "w_up"].rearrange("e (k p) m -> p (e k) m", p=P), 0, (E * KC, M))],
                         [(*ends("up"), 0, 2048)], None, 0))
            jobs.append(([(a[pre + "w_down"].rearrange("e m n -> m e n"), 0, (E, D))],
                         [(*ends("down"), 0, 2048)], None, 0))
            jobs.append(([(a[pre + "sw_gate"].rearrange("(k p) m -> p k m", p=P), 0, (KC, SM)),
                          (a[pre + "sw_up"].rearrange("(k p) m -> p k m", p=P), 512, (KC, SM)),
                          (a[pre + "sw_down"].rearrange("(k p) m -> p k m", p=P), 1024, (SM // P, D))],
                         [(*ends("sgate"), 0, 512), (*ends("sup"), 512, 512),
                          (*ends("sdown"), 1024, 512)], None, 0))
        PIECE = 256
        pieces = []
        job_end = []
        for jn, (_, ends_, gain, per) in enumerate(jobs):
            for hi, lo, at, size in ends_:
                step = min(PIECE, per) if gain is not None else PIECE
                for c in range(0, size, step):
                    w = min(step, size - c)
                    pieces.append((jn, hi[:, c:c + w], lo[:, c:c + w], at + c, w, gain,
                                   (at + c) // per if gain is not None else 0))
            job_end.append(len(pieces))
        stage_value = []
        so_far = [0, 0]
        for jn, (loads, *_rest) in enumerate(jobs):
            so_far[jn % 2] += 16 * len(loads)
            stage_value.append(so_far[jn % 2])

        def kv_acts(T):
            return 5 * min(T + 1, TILES) + 3 * max(0, T + 1 - TILES)

        def load_at(jn):
            return 4 * (jn - 3) + 1

        def load_job(eng, jn):
            if jn >= 2:
                eng.wait_ge(job_done, job_end[jn - 2])
            for src, at_, (c, n_) in jobs[jn][0]:
                eng.dma_start(stage[:, jn % 2, at_:at_ + c * n_].rearrange("p (c n) -> p c n", c=c),
                              src).then_inc(s_stage[jn % 2], 16)

        def load_bias(eng, g):
            step, hg = g // HG, g % HG
            layer, t = step // TILES, step % TILES
            w = P * (t + 1)
            if g >= 2:
                eng.wait_ge(s["biased"], UNITS // HG * HU * (g - 1))
            if layer == 0:
                if step == 0:
                    eng.wait_ge(table_in[hg], 16)
                src = table[hg * HU:(hg + 1) * HU, :, (TILES - 1 - t) * P + P - 1:TILES * P + P - 1]\
                    .rearrange("h p j -> p h j")
            else:
                src = a["fside_16xSxS_0"][hg * HU:(hg + 1) * HU, t * P:(t + 1) * P, 0:w]\
                    .rearrange("h p j -> p h j")
            eng.dma_start(bias[:, g % 2, :, 0:w], src).then_inc(s_bias[g % 2], 16)

        HEAD_LOADS = 13
        NU = N // HU
        U0 = NU // 2
        STEP_N = UNITS * HU
        FIRST, LAST = -20, N + 8

        block = ctx.enter_context(nc.Block())

        @block.sync
        def _(sp):
            load_job(sp, 0)
            load_job(sp, 1)
            sp.dma_start(w1_sb[:, :, :], a["L0_cond_w1"].rearrange("(k p) n -> p k n", p=P)).then_inc(s_in["w1"], 16)
            sp.dma_start(w2_sb[:, :, :], a["L0_cond_w2"].rearrange("(k p) n -> p k n", p=P)).then_inc(s_in["w2"], 16)
            sp.dma_start(b2_sb[:, :], a["L0_cond_b2"].rearrange("(h a) -> h a", a=1)).then_inc(s_in["w2"], 16)
            load_job(sp, 2)
            sp.wait_ge(setup["tab"], 2)
            sp.wait_ge(setup["pad"], 1)
            for hg in range(HG):
                dst = bass.AP(table.tensor, hg * HU * P * (TAB + P), [[P * (TAB + P), HU], [TAB + P + 1, P], [1, TAB]])
                sp.dma_start(dst, tab[hg * HU:(hg + 1) * HU, :].unsqueeze(1).to_broadcast([HU, P, TAB]))\
                    .then_inc(table_in[hg], 16)
            n_jobs = 3
            for g in range(STEPS * HG):
                load_bias(sp, g)
                if n_jobs < 10 and g == load_at(n_jobs):
                    load_job(sp, n_jobs)
                    n_jobs += 1
            for jn in range(n_jobs, len(jobs)):
                load_job(sp, jn)
            for ch in range(CHUNKS):
                sp.wait_ge(f["y"], CHUNK * EB * (CHUNKS + ch + 1))
                bt, t0 = divmod(ch * CHUNK, TILES)
                sp.dma_start(out[bt, t0 * P:(t0 + CHUNK) * P, :].rearrange("(t p) n -> p t n", p=P),
                             x[:, ch * CHUNK:(ch + 1) * CHUNK, :]).then_inc(f["out"], 16)
            sp.wait_ge(f["out"], 16 * CHUNKS)

        @block.gpsimd
        def _(pool):
            gp = nc.gpsimd
            chain = [0]

            def link(ins):
                chain[0] += 1
                ins.then_inc(pool_chain, 1)
                pool.wait_ge(pool_chain, chain[0])

            gp.memset(mhalf[:, :], -0.5).then_inc(setup["mhalf"], 1)
            link(gp.memset(ident[:, :], 0.0))
            gp.affine_select(out=ident[:, :], in_=ident[:, :], compare_op=ALU.not_equal, fill=1.0, base=0,
                             pattern=[[-1, P]], channel_multiplier=1).then_inc(setup["ident"], 1)
            link(gp.iota(rel_i[:, :], [[-P, TILES]], base=S - 1, channel_multiplier=-1))
            gp.tensor_copy(rel_f[:, :], rel_i[:, :]).then_inc(setup["rel"], 1)
            gp.memset(tab[:, S:TAB], NEG).then_inc(setup["pad"], 1)
            gp.memset(kn_b[:, :], 0.0).then_inc(setup["kn0"], 1)
            gp.memset(ones64[:, :], 1.0).then_inc(setup["ones"], 1)
            for e in range(E):
                gp.memset(place[:, e:e + 1], float(E - e)).then_inc(setup["place"], 1)
            pool.wait_ge(setup["place"], E)
            gp.memset(q_b[DH:P, :, :], BIG).then_inc(setup["big"], 1)
            pool.wait_ge(s_in["mask"], 2 * 16)
            for i in range(2):
                gp.tensor_scalar(k_b[i][DH:P, :, :].rearrange("p b n -> p (b n)"), mask8[DH:P, i, :],
                                 -1.0, BIG, ALU.add, ALU.mult).then_inc(setup["penalty"], 1)
            pool.wait_ge(setup["big"], 1)
            pool.wait_ge(setup["penalty"], 2)

            def piece(n):
                jn, hi, lo, at_, w, gain, gc = pieces[n]
                pool.wait_ge(s_stage[jn % 2], stage_value[jn])
                src = stage[:, jn % 2, at_:at_ + w]
                if gain is None:
                    link(gp.tensor_scalar(src, src, WS, 1.0, ALU.mult, ALU.mult))
                else:
                    link(gp.tensor_scalar(src, src, g_in[gain][:, gc:gc + 1], WS, ALU.mult, ALU.mult))
                link(gp.tensor_copy(hi, src))
                gp.tensor_tensor(lo, src, hi, ALU.subtract).then_inc(job_done, 1)

            split = [0]

            def split_to(n):
                while split[0] < n:
                    piece(split[0])
                    split[0] += 1

            def rel_rstd(r):
                pool.wait_ge(setup["stats"], r + 1)
                link(gp.tensor_scalar(r_rs[:, :], r_mv[:, :, 1], EPS, 0.0, ALU.add, ALU.add))
                gp.tensor_tensor(r_rs[:, :], r_rs[:, :], mhalf[:, 0:TILES], ALU.pow).then_inc(setup["rstd"], 1)

            pool.wait_ge(s_in["head"], 16 * HEAD_LOADS)
            pool.wait_ge(setup["nss"], 1)
            link(gp.tensor_tensor(null_r[:, :], null_r[:, :], mhalf[:, 0:1], ALU.pow))
            gp.tensor_scalar(null_r[:, :], null_r[:, :], 1e12, 1.0, ALU.min, ALU.mult).then_inc(setup["nrinv"], 1)
            rel_rstd(0)
            split_to(job_end[1])
            rel_rstd(1)
            split_to(job_end[2])
            for n in range(FIRST, LAST):
                m, k = divmod(n, HU)
                if k == 1 and 1 <= m <= NU:
                    u = m - 1
                    pool.wait_ge(s["o_raw"], u + 1)
                    pool.wait_ge(s["r_den"], u + 1)
                    if u >= 1:
                        pool.wait_ge(s["ot"], u)
                    gp.tensor_tensor(o_n[:, :, :], o_raw[:, :, :],
                                     r_den[:, :].unsqueeze(2).to_broadcast([P, HU, DH]), ALU.mult)\
                        .then_inc(s["o_n"], 1)
                if k == 1 and 0 <= m + 3 < U0:
                    u = m + 3
                    pool.wait_ge(s["q_ss"], u + 1)
                    if u >= 1:
                        pool.wait_ge(s["q_nd"], u)
                    link(gp.tensor_tensor(q_r[:, :], q_ss[:, :], mhalf[:, 0:HU], ALU.pow))
                    gp.tensor_scalar(q_r[:, :], q_r[:, :], 1e12 / WS, 1.0, ALU.min, ALU.mult).then_inc(s["q_r"], 1)
                g, at_g = divmod(n + 8, 2 * HU)
                if at_g == 0 and TILES * HG <= g < STEPS * HG:
                    t = (g // HG) % TILES
                    pool.wait_ge(s_bias[g % 2], 16 * (g // 2 + 1))
                    blk = bias[:, g % 2, :, t * P:(t + 1) * P]
                    gp.affine_select(out=blk, in_=blk, compare_op=ALU.is_ge, fill=NEG, base=0,
                                     pattern=[[0, HU], [-1, P]], channel_multiplier=1).then_inc(s["bias"], 1)
                if k == 3 and 0 <= m < NU:
                    u = m
                    pool.wait_ge(s["probs"], HU * (u + 1))
                    gp.tensor_tensor(d_null[:, :], neg_max[:, u % 2, :], neg_null[:, u % 2, :], ALU.subtract)\
                        .then_inc(s["d_null"], 1)
                if k == 0 and 1 <= m <= NU:
                    u = m - 1
                    pool.wait_ge(s["p_null"], u + 1)
                    if u >= 1:
                        pool.wait_ge(s["r_den"], u)
                    gp.tensor_tensor(denom[:, :], rows[:, u % 2, :], p_null[:, :], ALU.add).then_inc(s["denom"], 1)
                    if u >= 1:
                        pool.wait_ge(s["o_raw"], u)
                    gp.tensor_tensor(o_null[:, :, :], null_v[:, :].unsqueeze(1).to_broadcast([P, HU, DH]),
                                     p_null[:, :].unsqueeze(2).to_broadcast([P, HU, DH]), ALU.mult)\
                        .then_inc(s["o_null"], 1)
                for T in range(STEPS):
                    n0 = T * STEP_N
                    if n == n0 - 18:
                        pool.wait_ge(s["x_st"], T + 1)
                        link(gp.tensor_scalar(rstd[:, :], mv[:, :, 1], EPS, 0.0, ALU.add, ALU.add))
                        gp.tensor_tensor(rstd[:, :], rstd[:, :], mhalf[:, 0:B], ALU.pow).then_inc(s["x_rs"], 1)
                    if n == n0 - 12 and T < TILES:
                        pool.wait_ge(s["kv_act"], kv_acts(T))
                        link(gp.tensor_tensor(k_r[:, :], k_ss[:, :], mhalf[:, 0:B], ALU.pow))
                        gp.tensor_scalar(k_r[:, :], k_r[:, :], 1e12 / WS, 1.0, ALU.min, ALU.mult)\
                            .then_inc(s["kv_r"], 1)
                    if n == n0 - 10 and T < TILES:
                        pool.wait_ge(s["kv_d"], T + 1)
                        gp.tensor_copy(k_d[:, :, DH:2 * DH], k_d[:, :, 0:DH]).then_inc(s["k_dup"], 1)
                for p_ in range(STEPS * B):
                    T, bt = divmod(p_, B)
                    mu = T * UNITS + (HG - 1) * B + bt
                    if n == HU * (mu + 2):
                        pool.wait_ge(s["y_st"], p_ + 1)
                        link(gp.tensor_scalar(y_rs[:, :], y_mv[:, 1:2], EPS, 0.0, ALU.add, ALU.add))
                        gp.tensor_tensor(y_rs[:, :], y_rs[:, :], mhalf[:, 0:1], ALU.pow).then_inc(s["y_rs"], 1)
                    if n == HU * (mu + 2) + 2:
                        pool.wait_ge(s["y_n"], p_ + 1)
                        link(gp.tensor_tensor(y_n[:, :], y_n[:, :], g_out[T // TILES][:, :], ALU.mult))
                        x_t = x[:, bt * TILES + T % TILES, :]
                        gp.tensor_tensor(x_t, x_t, y_n[:, :], ALU.add).then_inc(s["x_new"], 1)
                if k == 2 and split[0] < job_end[9] and n >= 2 * HU * load_at(pieces[split[0]][0]):
                    split_to(split[0] + 1)
            split_to(job_end[9])
            pool.wait_ge(s["biased"], N)
            for en in range(2 * CHUNKS * EB):
                if split[0] < len(pieces):
                    split_to(split[0] + 1)
                pool.wait_ge(f["h_hi"], en + 1)
                gp.tensor_tensor(h_lo[:, en % 2, :], h_f[:, en % 2, :], h_hi[:, en % 2, :], ALU.subtract)\
                    .then_inc(f["h_lo"], 1)

        @block.scalar
        def _(act):
            ac = nc.scalar
            for i, v in enumerate(("w0", "b0", "g0", "b1", "g1")):
                act.dma_start(rvec[:, i, :], bcast(a["L0_cond_" + v], D)).then_inc(s_in["rel"], 16)
            act.dma_start(k_scale[:, :], bcast(a["L0_cond_k_scale"], DH)).then_inc(s_in["head"], 16)
            act.dma_start(q_scale[:, :], bcast(a["L0_cond_q_scale"], DH)).then_inc(s_in["head"], 16)
            for i, pre in ((0, "L0_cond_"), (1, "L1_cond_")):
                act.dma_start(g_in[i][:, :], a[pre + ("g_norm" if i == 0 else "g_in")].rearrange("(k p) -> p k", p=P),
                              allow_slow_non_contiguous=True).then_inc(s_in["head"], 16)
                act.dma_start(g_out[i][:, :], bcast(a[pre + "g_out"], D)).then_inc(s_in["head"], 16)
                act.dma_start(null_b[i][:, :], bcast(a[pre + "null_attn_bias"], H)).then_inc(s_in["head"], 16)
            act.dma_start(null_k[:, :], bcast(a["cond_64"][0, :], DH)).then_inc(s_in["head"], 16)
            act.dma_start(null_v[:, :], bcast(a["cond_64"][1, :], DH)).then_inc(s_in["head"], 16)
            act.dma_start(cond_n[:, :], a["cond_64"]).then_inc(s_in["head"], 16)
            for i, pre in ((0, "L2_cond_"), (1, "L3_cond_")):
                act.dma_start(wt_n[:, i, :], a[pre + "wt"]).then_inc(s_in["head"], 16)
                act.dma_start(wg_n[:, i, :], a[pre + "wg"]).then_inc(s_in["moe"], 16)
            for i, v in enumerate(("mask_BxS_bf1", "mask_BxS_bk0")):
                mk = a[v]
                act.dma_start(mask_words[DH:P, i, :], bass.AP(mk.tensor, mk.offset, [[0, DH], [1, B * S // 4]]))\
                    .then_inc(s_in["mask"], 16)
            act.dma_start(x[:, :, :], a["x"].rearrange("b (t p) n -> p (b t) n", p=P)).then_inc(s_in["x"], 16)

            act.wait_ge(setup["nt"], 1)
            ac.activation(kn_a[:, :], aux[:, 0:2 * P].rearrange("p (l n) -> p l n", l=2)[:, :, 0], ACT.Copy)\
                .then_inc(setup["nka"], 1)
            for r in range(2):
                act.wait_ge(setup["z"], r + 1)
                ac.activation(re, rh, ACT.Tanh, scale=0.5).then_inc(setup["tanh"], 1)
                for kc in range(KC):
                    act.wait_ge(setup["pt"], KC * r + kc + 1)
                    ac.activation(rht[:, kc, :, :].rearrange("p k n -> p (k n)"), sc[kc][:, :], ACT.Copy)\
                        .then_inc(setup["t"], 1)

            for n in range(FIRST, LAST):
                m, k = divmod(n, HU)
                first, second = banks(n)
                i = n + 1
                if 0 <= i < N:
                    w = P * (plan.tile(i) + 1)
                    u = plan.unit(i)
                    act.wait_ge(s["biased"], i + 1)
                    if i >= 2:
                        act.wait_ge(s["pt"], plan.groups_done(i - 2))
                    if i % HU == 0 and u >= 2:
                        act.wait_ge(s["denom"], u - 1)
                    ac.activation(probs[:, i % 2, 0:w], biased[:, i % 2, 0:w], ACT.Exp,
                                  bias=neg_max[:, u % 2, i % HU:i % HU + 1], scale=-1.0,
                                  accum_out=rows[:, u % 2, i % HU:i % HU + 1]).then_inc(s["probs"], 1)
                if k == 3 and 0 <= m + 2 < NU:
                    u = m + 2
                    act.wait_ge(s["q_t"], u + 1)
                    if u >= 2:
                        act.wait_ge(s["scores"], HU * (u - 1))
                    ac.activation(q_b[0:DH, u % 2, :], first[0:DH, :], ACT.Copy).then_inc(s["q_hi"], 1)
                    act.wait_ge(s["q_hi"], u + 1)
                    ac.activation(q_a[0:DH, u % 2, :], q_b[0:DH, u % 2, :], ACT.Copy).then_inc(s["q_dup"], 1)
                if k == 0 and 1 <= m <= NU:
                    u = m - 1
                    act.wait_ge(s["d_null"], u + 1)
                    if u >= 1:
                        act.wait_ge(s["o_null"], u)
                    ac.activation(p_null[:, :], d_null[:, :], ACT.Exp).then_inc(s["p_null"], 1)
                if k == 1 and 0 <= m + 3 < NU:
                    u = m + 3
                    act.wait_ge(s["q_proj"], u + 1)
                    if u < U0:
                        if u >= 1:
                            act.wait_ge(s["q_ss"], u)
                        ac.activation(q_sq[:, :], first[:, 0:UW], ACT.Square).then_inc(s["q_sq"], 1)
                    ac.activation(q_n[:, u % 2, :], first[:, 0:UW], ACT.Copy, scale=1.0 if u < U0 else DH ** -0.5 / WS)\
                        .then_inc(s["q_na"], 1)

                def small():
                    for T in range(STEPS):
                        n0 = T * STEP_N
                        layer, t = divmod(T, TILES)
                        if n == n0 - 16:
                            act.wait_ge(s["xt"], T + 1)
                            if T >= 2:
                                act.wait_ge(s["q_proj"], UNITS * (T - 1))
                            ac.activation(xt[:, T % 2, 0, :, :, :].rearrange("p b c n -> p (b c n)"), second[:, :], ACT.Copy)\
                                .then_inc(s["xt_hi"], 1)
                        if n == n0 - 12:
                            act.wait_ge(s["kv"], T + 1)
                            if T >= 1:
                                act.wait_ge(s["kt"], T)
                            kv_ps = second[:, 0:B * 2 * DH].rearrange("p (b n) -> p b n", b=B)
                            if layer == 0:
                                for bt in range(B):
                                    ac.activation(k_sq[:, bt, :], kv_ps[:, bt, 0:DH], ACT.Square,
                                                  accum_out=k_ss[:, bt:bt + 1]).then_inc(s["kv_act"], 1)
                                    ac.activation(k_d[:, bt, 0:DH], kv_ps[:, bt, 0:DH], ACT.Copy).then_inc(s["kv_act"], 1)
                            else:
                                for i_ in range(2):
                                    ac.activation(k_d[:, :, i_ * DH:(i_ + 1) * DH], kv_ps[:, :, 0:DH], ACT.Copy,
                                                  scale=1.0 / WS).then_inc(s["kv_act"], 1)
                            ac.activation(v_s[layer][:, t::TILES, 0, :], kv_ps[:, :, DH:2 * DH], ACT.Copy, scale=1.0 / WS)\
                                .then_inc(s["kv_act"], 1)
                        if n == n0 - 8:
                            act.wait_ge(s["kt"], T + 1)
                            ac.activation(k_a[layer][:, :, t * P:(t + 1) * P],
                                          second[:, 0:B * P].rearrange("p (b n) -> p b n", b=B), ACT.Copy)\
                                .then_inc(s["k_hi"], 1)
                    if k == 2 and 0 <= m - 1 < NU:
                        u = m - 1
                        act.wait_ge(s["ot"], u + 1)
                        ac.activation(ot_hi[:, :], second[:, 0:UW], ACT.Copy).then_inc(s["ot_hi"], 1)

                now = plan.at(n)
                for j in range(max(1, len(now))):
                    if j < len(now):
                        gi = now[j]
                        nb = plan.groups[gi][2]
                        act.wait_ge(s["pt"], gi + 1)
                        if gi >= 4:
                            act.wait_ge(s["pv"], gi - 3)
                        ac.activation(p_hi[:, gi % 4, 0:nb * P], tp[gi % 2][:, 0:nb * P], ACT.Copy)\
                            .then_inc(s["p_hi"], 1)
                    if j == 0:
                        small()

            def x_hi(cn):
                for kc, bank in enumerate((op, aux)):
                    act.wait_ge(f["xt"], KC * cn + kc + 1)
                    if cn >= 2 and kc == 0:
                        act.wait_ge(f["gu"], EB * (cn - 1))
                    ac.activation(mx_hi[:, cn % 2, kc, :], bank[:, :], ACT.Copy).then_inc(f["xt_hi"], 1)

            def gate_exp(cn):
                act.wait_ge(f["shifted"], cn + 1)
                ac.activation(gl[1][:, :, :], gl[0][:, :, :], ACT.Exp).then_inc(f["exp"], 1)

            x_hi(0)
            gate_exp(0)
            for en in range(2 * CHUNKS * EB):
                cn, e = divmod(en, EB)
                act.wait_ge(f["gu"], en + 1)
                if en >= 1:
                    act.wait_ge(f["leaky"], en)
                ac.activation(g_t, sc[en % 2][:, 0:512], ACT.Copy, scale=0.01 / WS).then_inc(f["tenth"], 1)
                act.wait_ge(f["h"], en + 1)
                if en >= 2:
                    act.wait_ge(f["down"], 2 * (en - 1))
                ac.activation(h_hi[:, en % 2, :], h_f[:, en % 2, :], ACT.Copy).then_inc(f["h_hi"], 1)
                if cn + 1 < 2 * CHUNKS and e == 4:
                    x_hi(cn + 1)
                if cn + 1 < 2 * CHUNKS and e == 6:
                    gate_exp(cn + 1)

        @block.vector
        def _(dve):
            ve = nc.vector
            chain = [0]

            def link(ins):
                chain[0] += 1
                ins.then_inc(dve_chain, 1)
                dve.wait_ge(dve_chain, chain[0])

            dve.wait_ge(s_in["head"], 16 * HEAD_LOADS)
            ve.tensor_tensor_reduce(out=null_sq[:, :], in0=null_k[:, :], in1=null_k[:, :], scale=1.0, scalar=0.0,
                                    op0=ALU.mult, op1=ALU.add, accum_out=null_r[:, :]).then_inc(setup["nss"], 1)
            link(ve.scalar_tensor_tensor(k_scale[:, :], k_scale[:, :], 8.0, q_scale[:, :], ALU.mult, ALU.mult))
            dve.wait_ge(setup["nrinv"], 1)
            for i in range(2):
                half = slice(i * DH, (i + 1) * DH)
                ve.scalar_tensor_tensor(null_kd[:, 0, half], null_k[:, :], null_r[:, 0:1], k_scale[:, :],
                                        ALU.mult, ALU.mult)
                last = ve.tensor_copy(null_kd[:, 1, half], null_k[:, :])
            last.then_inc(setup["nkd"], 1)
            dve.wait_ge(setup["nka"], 1)
            dve.wait_ge(setup["kn0"], 1)
            ve.tensor_tensor(kn_b[0:DH, :], aux[0:DH, 0:2 * P].rearrange("p (l n) -> p l n", l=2)[:, :, 0],
                             kn_a[0:DH, :], ALU.subtract).then_inc(setup["nkb"], 1)
            dve.wait_ge(setup["mt"], 1)
            link(ve.tensor_scalar(wt_f[:, :, :, :].rearrange("p l k e -> p (l k e)"), op[:, 0:32], WS, None, ALU.mult))
            for l in range(2):
                link(ve.tensor_copy(wt_s[:, l, 0, :, :], wt_f[:, l, :, :]))
                ve.tensor_tensor(wt_s[:, l, 1, :, :], wt_f[:, l, :, :], wt_s[:, l, 0, :, :], ALU.subtract)
            ve.tensor_copy(wg_t[:, :, :].rearrange("p l e -> p (l e)"), op[0:G, 32:48])
            link(ve.tensor_copy(cond_t[:, :], op[0:G, 48:50]))
            dve.wait_ge(setup["ones"], 1)
            for b in range(B):
                last = ve.tensor_scalar(cond_b[:, b, :], ones64[:, :], cond_t[:, b:b + 1], None, ALU.mult)
            last.then_inc(setup["cb"], 1)
            dve.wait_ge(setup["lg"], 1)
            ve.tensor_scalar(lg_half[:, :, :, :].rearrange("p l b e -> p (l b e)"), op[:, 64:96], 0.5, None, ALU.mult)\
                .then_inc(setup["lgh"], 1)

            dve.wait_ge(s_in["rel"], 5 * 16)
            dve.wait_ge(setup["rel"], 1)
            for k in range(TILES):
                last = ve.scalar_tensor_tensor(rh[:, k, :], rvec[:, 0, :], rel_f[:, k:k + 1], rvec[:, 1, :],
                                               ALU.mult, ALU.add)
            link(last)
            for r in range(2):
                if r == 1:
                    dve.wait_ge(setup["mm"], 1)
                    for i in range(2):
                        last = ve.scalar_tensor_tensor(rh[:, 4 * i:4 * i + 4, :],
                                                       sc[i][:, :].rearrange("p (k n) -> p k n", k=4), 0.5,
                                                       rvec[:, 3, :].unsqueeze(1).to_broadcast([P, 4, D]),
                                                       ALU.mult, ALU.add)
                    link(last)
                for k in range(TILES):
                    last = ve.bn_stats(r_st[:, k, :], rh[:, k, :])
                link(last)
                for k in range(TILES):
                    last = ve.bn_aggr(r_mv[:, k, :], r_st[:, k, :])
                last.then_inc(setup["stats"], 1)
                dve.wait_ge(setup["rstd"], r + 1)
                for k in range(TILES):
                    last = ve.tensor_scalar(rh[:, k, :], rh[:, k, :], r_mv[:, k, 0:1], r_rs[:, k:k + 1],
                                            ALU.subtract, ALU.mult)
                link(last)
                ve.tensor_tensor(rh, rh, rvec[:, 2 + 2 * r, :].unsqueeze(1).to_broadcast([P, TILES, D]), ALU.mult)\
                    .then_inc(setup["z"], 1)
                dve.wait_ge(setup["tanh"], r + 1)
                ve.scalar_tensor_tensor(rh, re, 1.0, rh, ALU.add, ALU.mult).then_inc(setup["h"], 1)
            for i in range(2):
                dve.wait_ge(setup["mm"], 2 + i)
                ve.tensor_scalar(tab[:, i * 512:(i + 1) * 512], tp[i][0:H, :], 0.5, b2_sb[:, 0:1], ALU.mult, ALU.add)\
                    .then_inc(setup["tab"], 1)

            dve.wait_ge(s_in["x"], 16)
            for n in range(FIRST, LAST):
                m, k = divmod(n, HU)
                first, second = banks(n)
                if k == 1 and 1 <= m <= NU:
                    u = m - 1
                    dve.wait_ge(s["o_null"], u + 1)
                    dve.wait_ge(s["pv"], plan.groups_done(n - 2))
                    ve.tensor_tensor(o_raw[:, :, :], op[:, 0:UW].rearrange("p (h d) -> p h d", h=HU),
                                     o_null[:, :, :], ALU.add).then_inc(s["o_raw"], 1)
                    dve.wait_ge(s["denom"], u + 1)
                    ve.reciprocal(r_den[:, :], denom[:, :]).then_inc(s["r_den"], 1)
                i = n + 2
                if 0 <= i < N:
                    w = P * (plan.tile(i) + 1)
                    u = plan.unit(i)
                    g = i // (2 * HU)
                    dve.wait_ge(s["scores"], i + 1)
                    if i >= 2:
                        dve.wait_ge(s["probs"], i - 1)
                    if i % HU == 0:
                        dve.wait_ge(s["null"], u + 1)
                        if u >= 2:
                            dve.wait_ge(s["d_null"], u - 1)
                    if g < TILES * HG:
                        dve.wait_ge(s_bias[g % 2], 16 * (g // 2 + 1))
                    else:
                        dve.wait_ge(s["bias"], g - TILES * HG + 1)
                    ve.tensor_tensor_reduce(out=biased[:, i % 2, 0:w], in0=sc[i % 2][:, 0:w],
                                            in1=bias[:, g % 2, i % HU, 0:w], scale=-1.0,
                                            scalar=neg_null[:, u % 2, i % HU:i % HU + 1],
                                            op0=ALU.add, op1=ALU.min,
                                            accum_out=neg_max[:, u % 2, i % HU:i % HU + 1]).then_inc(s["biased"], 1)
                for T in range(STEPS):
                    n0 = T * STEP_N
                    layer, t = divmod(T, TILES)
                    tiles = [bt * TILES + t for bt in range(B)]
                    if n == n0 - 18:
                        if layer == 1:
                            dve.wait_ge(s["x_new"], B * (T - TILES + 1))
                        for bt in range(B):
                            last = ve.bn_stats(st6[:, bt, :], x[:, tiles[bt], :])
                        link(last)
                        for bt in range(B):
                            last = ve.bn_aggr(mv[:, bt, :], st6[:, bt, :])
                        last.then_inc(s["x_st"], 1)
                    if n == n0 - 17:
                        dve.wait_ge(s["x_rs"], T + 1)
                        for bt in range(B):
                            last = ve.tensor_scalar(xn[:, bt, :], x[:, tiles[bt], :], mv[:, bt, 0:1],
                                                    rstd[:, bt:bt + 1], ALU.subtract, ALU.mult)
                        last.then_inc(s["xn"], 1)
                if k == 3 and 0 <= m + 2 < NU:
                    u = m + 2
                    dve.wait_ge(s["q_hi"], u + 1)
                    ve.tensor_tensor(q_a[DH:P, u % 2, :], first[0:DH, :], q_b[0:DH, u % 2, :], ALU.subtract)\
                        .then_inc(s["q_lo"], 1)
                if k == 0 and 0 <= m + 1 < NU:
                    u = m + 1
                    hg = (u % UNITS) // B
                    dve.wait_ge(s["q_null"], u + 1)
                    if u >= 2:
                        dve.wait_ge(s["d_null"], u - 1)
                    ve.scalar_tensor_tensor(neg_null[:, u % 2, :], first[:, 0:HU], -1.0,
                                            null_b[u // U0][:, hg * HU:(hg + 1) * HU], ALU.mult, ALU.subtract)\
                        .then_inc(s["null"], 1)

                def small():
                    for T in range(STEPS):
                        n0 = T * STEP_N
                        layer, t = divmod(T, TILES)
                        if n == n0 - 16:
                            dve.wait_ge(s["xt_hi"], T + 1)
                            ve.tensor_tensor(xt[:, T % 2, 1, :, :, :].rearrange("p b c n -> p (b c n)"), second[:, :],
                                             xt[:, T % 2, 0, :, :, :].rearrange("p b c n -> p (b c n)"), ALU.subtract)\
                                .then_inc(s["xt_lo"], 1)
                        if n == n0 - 12:
                            dve.wait_ge(s["kv_act"], kv_acts(T))
                            kv_ps = second[:, 0:B * 2 * DH].rearrange("p (b n) -> p b n", b=B)
                            ve.scalar_tensor_tensor(v_s[layer][:, t::TILES, 1, :], kv_ps[:, :, DH:2 * DH], 1.0 / WS,
                                                    v_s[layer][:, t::TILES, 0, :], ALU.mult, ALU.subtract)\
                                .then_inc(s["kv_v"], 1)
                        if n == n0 - 8:
                            dve.wait_ge(s["k_hi"], T + 1)
                            cols = slice(t * P, (t + 1) * P)
                            ve.tensor_tensor(k_b[layer][0:DH, :, cols],
                                             second[0:DH, 0:B * P].rearrange("p (b n) -> p b n", b=B),
                                             k_a[layer][0:DH, :, cols], ALU.subtract).then_inc(s["k_lo"], 1)
                    if k == 2 and 0 <= m - 1 < NU:
                        u = m - 1
                        dve.wait_ge(s["ot_hi"], u + 1)
                        ve.tensor_tensor(ot_lo[:, :], second[:, 0:UW], ot_hi[:, :], ALU.subtract).then_inc(s["ot_lo"], 1)
                    if k == 3 and 0 <= m - 1 < NU:
                        u = m - 1
                        bt = u % B
                        dve.wait_ge(s["y"], u + 1)
                        if (u % UNITS) // B == 0:
                            T = u // UNITS
                            if T >= 1:
                                dve.wait_ge(s["y_n"], B * (T - 1) + bt + 1)
                            ve.tensor_scalar(y_acc[:, bt, :], second[:, 0:D], 1.0 / WS, None, ALU.mult)\
                                .then_inc(s["y_acc"], 1)
                        else:
                            dve.wait_ge(s["y_acc"], u - 1)
                            ve.scalar_tensor_tensor(y_acc[:, bt, :], second[:, 0:D], 1.0 / WS, y_acc[:, bt, :],
                                                    ALU.mult, ALU.add).then_inc(s["y_acc"], 1)

                now = plan.at(n)
                for j in range(max(1, len(now))):
                    if j < len(now):
                        gi = now[j]
                        nb = plan.groups[gi][2]
                        dve.wait_ge(s["p_hi"], gi + 1)
                        ve.tensor_tensor(p_lo[:, gi % 4, 0:nb * P], tp[gi % 2][:, 0:nb * P],
                                         p_hi[:, gi % 4, 0:nb * P], ALU.subtract).then_inc(s["p_lo"], 1)
                    if j == 0:
                        small()
                if k == 1 and 0 <= m + 3 < U0:
                    u = m + 3
                    dve.wait_ge(s["q_sq"], u + 1)
                    ve.reduce_sum(q_ss[:, :], q_sq[:, :].rearrange("p (h d) -> p h d", h=HU), AX)\
                        .then_inc(s["q_ss"], 1)
                if k == 3 and 0 <= m + 3 < U0:
                    u = m + 3
                    dve.wait_ge(s["q_r"], u + 1)
                    dve.wait_ge(s["q_na"], u + 1)
                    q_h = q_n[:, u % 2, :].rearrange("p (h d) -> p h d", h=HU)
                    ve.tensor_tensor(q_h, q_h, q_r[:, :].unsqueeze(2).to_broadcast([P, HU, DH]), ALU.mult)\
                        .then_inc(s["q_nd"], 1)
                for T in range(TILES):
                    if n == T * STEP_N - 11:
                        dve.wait_ge(s["kv_r"], T + 1)
                        for bt in range(B):
                            last = ve.scalar_tensor_tensor(k_d[:, bt, 0:DH], k_d[:, bt, 0:DH],
                                                           k_r[:, bt:bt + 1], k_scale[:, :], ALU.mult, ALU.mult)
                        last.then_inc(s["kv_d"], 1)
                for p_ in range(STEPS * B):
                    T, bt = divmod(p_, B)
                    mu = T * UNITS + (HG - 1) * B + bt
                    if n == HU * (mu + 2):
                        dve.wait_ge(s["y_acc"], mu + 1)
                        link(ve.bn_stats(y_st[:, :], y_acc[:, bt, :]))
                        ve.bn_aggr(y_mv[:, :], y_st[:, :]).then_inc(s["y_st"], 1)
                    if n == HU * (mu + 2) + 1:
                        dve.wait_ge(s["y_rs"], p_ + 1)
                        ve.tensor_scalar(y_n[:, :], y_acc[:, bt, :], y_mv[:, 0:1], y_rs[:, 0:1],
                                         ALU.subtract, ALU.mult).then_inc(s["y_n"], 1)

            def x_lo(cn):
                for kc, bank in enumerate((op, aux)):
                    dve.wait_ge(f["xt_hi"], KC * cn + kc + 1)
                    ve.tensor_tensor(mx_lo[:, cn % 2, kc, :], bank[:, :], mx_hi[:, cn % 2, kc, :], ALU.subtract)\
                        .then_inc(f["xt_lo"], 1)

            def over_e(t_):
                return t_[:, :].unsqueeze(2).to_broadcast([P, CHUNK, E])

            def gate_shift(cn):
                layer, ch = divmod(cn, CHUNKS)
                bt = ch * CHUNK // TILES
                dve.wait_ge(f["logit"], cn + 1)
                link(ve.scalar_tensor_tensor(gl[2][:, :, :], aux[:, 0:CHUNK * E].rearrange("p (t e) -> p t e", t=CHUNK),
                                             0.5 / WS, lg_half[:, layer, bt, :].unsqueeze(1).to_broadcast([P, CHUNK, E]),
                                             ALU.mult, ALU.add))
                link(ve.reduce_max(gm[0][:, :], gl[2][:, :, :], AX))
                ve.tensor_tensor(gl[0][:, :, :], gl[2][:, :, :], over_e(gm[0]), ALU.subtract).then_inc(f["shifted"], 1)

            def gate_pick(cn):
                dve.wait_ge(f["exp"], cn + 1)
                sc_ = gl[2]
                link(ve.reduce_sum(gm[0][:, :], gl[1][:, :, :], AX))
                link(ve.reciprocal(gm[1][:, :], gm[0][:, :]))
                link(ve.tensor_tensor(sc_[:, :, :], gl[1][:, :, :], over_e(gm[1]), ALU.mult))
                left = sc_
                order = place[:, :].unsqueeze(1).to_broadcast([P, CHUNK, E])
                for r in range(2):
                    link(ve.reduce_max(gm[2 + r][:, :], left[:, :, :], AX))
                    link(ve.tensor_tensor(gl[3][:, :, :], left[:, :, :], over_e(gm[2 + r]), ALU.is_equal))
                    link(ve.tensor_tensor(gl[3][:, :, :], gl[3][:, :, :], order, ALU.mult))
                    link(ve.reduce_max(gm[4][:, :], gl[3][:, :, :], AX))
                    link(ve.tensor_tensor(gl[3][:, :, :], gl[3][:, :, :], over_e(gm[4]), ALU.is_equal))
                    link(ve.scalar_tensor_tensor(gl[4 + r][:, :, :], gl[3][:, :, :], -4.0, left[:, :, :],
                                                 ALU.mult, ALU.add))
                    left = gl[4 + r]
                link(ve.scalar_tensor_tensor(gm[4][:, :], gm[2][:, :], 1e-20, gm[3][:, :], ALU.add, ALU.add))
                link(ve.reciprocal(gm[5][:, :], gm[4][:, :]))
                link(ve.tensor_scalar(gl[3][:, :, :], left[:, :, :], 0.0, 1.0 / WS, ALU.is_lt, ALU.mult))
                link(ve.tensor_tensor(gl[3][:, :, :], gl[3][:, :, :], sc_[:, :, :], ALU.mult))
                ve.tensor_tensor(comb[:, cn % 2, :, :], gl[3][:, :, :], over_e(gm[5]), ALU.mult).then_inc(f["comb"], 1)

            def y_evict(en):
                cn, e = divmod(en, EB)
                ch = cn % CHUNKS
                for i in range(CHUNK):
                    if i % 2 == 0:
                        dve.wait_ge(f["down"], 2 * en + i // 2 + 1)
                    if e == 0 and i == 0:
                        dve.wait_ge(f["comb"], cn + 1)
                    if e > 0:
                        dve.wait_ge(f["y"], CHUNK * (en - 1) + i + 1)
                    x_t = x[:, ch * CHUNK + i, :]
                    weight = comb[:, cn % 2, i, e:e + 1] if e < E else 1.0 / WS
                    ve.scalar_tensor_tensor(x_t, tp[i // 2][:, (i % 2) * D:(i % 2 + 1) * D], weight, x_t,
                                            ALU.mult, ALU.add).then_inc(f["y"], 1)

            dve.wait_ge(setup["place"], E)
            x_lo(0)
            gate_shift(0)
            gate_pick(0)
            for en in range(2 * CHUNKS * EB + 1):
                cn, e = divmod(en, EB)
                if en < 2 * CHUNKS * EB:
                    dve.wait_ge(f["tenth"], en + 1)
                    ve.scalar_tensor_tensor(g_l, sc[en % 2][:, 0:512], 1.0 / WS, g_t, ALU.mult, ALU.max)\
                        .then_inc(f["leaky"], 1)
                    dve.wait_ge(f["leaky"], en + 1)
                    if en >= 2:
                        dve.wait_ge(f["h_lo"], en - 1)
                    ve.scalar_tensor_tensor(h_f[:, en % 2, :], sc[en % 2][:, 512:1024], 1.0 / WS, g_l,
                                            ALU.mult, ALU.mult).then_inc(f["h"], 1)
                if en >= 1:
                    y_evict(en - 1)
                if cn + 1 < 2 * CHUNKS:
                    if e == 4:
                        x_lo(cn + 1)
                    if e == 6:
                        gate_shift(cn + 1)
                    if e == 7:
                        gate_pick(cn + 1)

        @block.tensor
        def _(pe):
            te = nc.tensor

            def three(out_, l_hi, l_lo, r_hi, r_lo, first, last):
                te.matmul(out_, l_hi, r_hi, start=first, stop=False)
                te.matmul(out_, l_hi, r_lo, start=False, stop=False)
                return te.matmul(out_, l_lo, r_hi, start=False, stop=last)

            pe.wait_ge(setup["ident"], 1)
            pe.wait_ge(setup["nkd"], 1)
            for i in range(2):
                last = te.transpose(aux[:, i * P:(i + 1) * P], null_kd[:, i, :], ident[:, :])
            last.then_inc(setup["nt"], 1)
            pe.wait_ge(s_in["head"], 16 * HEAD_LOADS)
            pe.wait_ge(s_in["moe"], 2 * 16)
            for l in range(2):
                for kc in range(KC):
                    at_ = (l * KC + kc) * E
                    te.transpose(op[:, at_:at_ + E], wt_n[:, l, kc * P:(kc + 1) * P], ident[0:E, 0:E])
                te.transpose(op[0:G, 32 + l * E:32 + (l + 1) * E], wg_n[:, l, :], ident[0:E, 0:E])
            te.transpose(op[0:G, 48:50], cond_n[:, :], ident[0:B, 0:B]).then_inc(setup["mt"], 1)
            pe.wait_ge(setup["cb"], 1)
            for l in range(2):
                for b in range(B):
                    at_ = 64 + (l * B + b) * E
                    last = te.matmul(op[:, at_:at_ + E], cond_b[:, b, :], wg_t[:, l, :], start=True, stop=True)
            last.then_inc(setup["lg"], 1)
            for r in range(2):
                pe.wait_ge(setup["h"], r + 1)
                for kc in range(KC):
                    for k in range(TILES):
                        last = te.transpose(sc[kc][:, k * P:(k + 1) * P], rh[:, k, kc * P:(kc + 1) * P], ident[:, :])
                    last.then_inc(setup["pt"], 1)
                pe.wait_ge(setup["t"], KC * (r + 1))
                if r == 0:
                    pe.wait_ge(s_in["w1"], 16)
                    for k in range(TILES):
                        for kc in range(KC):
                            last = te.matmul(sc[k // 4][:, (k % 4) * D:(k % 4 + 1) * D], rht[:, kc, k, :],
                                             w1_sb[:, kc, :], start=(kc == 0), stop=(kc == KC - 1))
                    last.then_inc(setup["mm"], 1)
                else:
                    pe.wait_ge(s_in["w2"], 2 * 16)
                    for i in range(2):
                        for kc in range(KC):
                            last = te.matmul(tp[i][0:H, :], w2_sb[:, kc, :],
                                             rht[:, kc, 4 * i:4 * i + 4, :].rearrange("p k n -> p (k n)"),
                                             start=(kc == 0), stop=(kc == KC - 1))
                        last.then_inc(setup["mm"], 1)

            free = {0: [], 1: [], 2: [(setup["nkb"], 1)]}

            def release(b_):
                for sem_, value in free[b_]:
                    pe.wait_ge(sem_, value)

            def take(second_, *after):
                b_ = slot_n // 2 % 2 if second_ and free_banks(slot_n) else 2
                release(b_)
                free[b_] = after

            def pv(gi):
                n, j0, nb = plan.groups[gi]
                layer, h = plan.layer(n), n % HU
                bt = plan.unit(n) % B
                nk = plan.tile(n) + 1
                u = plan.unit(n)
                if gi == plan.first_group[n] and h == 0 and u >= 1:
                    pe.wait_ge(s["o_raw"], u)
                if gi == plan.first_group[n] and plan.unit(n) % UNITS == 0 and h == 0:
                    pe.wait_ge(s["kv_v"], plan.unit(n) // UNITS + 1)
                pe.wait_ge(s["p_lo"], gi + 1)
                o_h = op[:, h * DH:(h + 1) * DH]
                for jj in range(nb):
                    j = j0 + jj
                    v_hi = v_s[layer][:, bt * TILES + j, 0, :]
                    v_lo = v_s[layer][:, bt * TILES + j, 1, :]
                    cols = slice(jj * P, (jj + 1) * P)
                    last = three(o_h, p_hi[:, gi % 4, cols], p_lo[:, gi % 4, cols], v_hi, v_lo,
                                 j == 0, j == nk - 1)
                last.then_inc(s["pv"], 1)

            for n in range(FIRST, LAST):
                m, k = divmod(n, HU)
                slot_n = n
                first, second = banks(n)
                i = n + 3
                if 0 <= i < N:
                    layer, t, u = plan.layer(i), plan.tile(i), plan.unit(i)
                    bt, h = u % B, i % HU
                    if i == 0:
                        pe.wait_ge(setup["penalty"], 2)
                        pe.wait_ge(setup["mm"], 3)
                    if h == 0:
                        pe.wait_ge(s["q_dup"], u + 1)
                        pe.wait_ge(s["q_lo"], u + 1)
                        if u % UNITS == 0:
                            pe.wait_ge(s["k_lo"], u // UNITS + 1)
                    if i >= 2:
                        pe.wait_ge(s["biased"], i - 1)
                    cols = slice(h * P, (h + 1) * P)
                    w = P * (t + 1)
                    if w > 512:
                        release(i % 2)
                        free[i % 2] = ()
                    for c0 in range(0, w, 512):
                        cw = min(512, w - c0)
                        o_ = sc[i % 2][:, c0:c0 + cw]
                        te.matmul(o_, q_a[:, u % 2, cols], k_a[layer][:, bt, c0:c0 + cw], start=True, stop=False)
                        last = te.matmul(o_, q_b[:, u % 2, cols], k_b[layer][:, bt, c0:c0 + cw],
                                         start=False, stop=True)
                    last.then_inc(s["scores"], 1)
                if k == 3 and 0 <= m + 2 < NU:
                    u = m + 2
                    take(False, (s["q_lo"], u + 1))
                    pe.wait_ge(s["q_na"], u + 1)
                    if u < U0:
                        pe.wait_ge(s["q_nd"], u + 1)
                    for h in range(HU):
                        last = te.transpose(first[0:DH, h * P:(h + 1) * P], q_n[:, u % 2, h * DH:(h + 1) * DH], ident[:, :])
                    last.then_inc(s["q_t"], 1)
                if k == 0 and 0 <= m + 1 < NU:
                    u = m + 1
                    layer = u // U0
                    take(False, (s["null"], u + 1))
                    pe.wait_ge(s["q_dup"], u + 1)
                    if u == 0:
                        pe.wait_ge(setup["big"], 1)
                    for h in range(HU):
                        cols = slice(h * P, (h + 1) * P)
                        te.matmul(first[:, h:h + 1], q_a[:, u % 2, cols], kn_a[:, layer:layer + 1], start=True, stop=False)
                        last = te.matmul(first[:, h:h + 1], q_b[:, u % 2, cols], kn_b[:, layer:layer + 1],
                                         start=False, stop=True)
                    last.then_inc(s["q_null"], 1)
                if k == 1 and 0 <= m + 3 < NU:
                    u = m + 3
                    layer = u // U0
                    T, hg, bt = u // UNITS, (u % UNITS) // B, u % B
                    take(False, (s["q_na"], u + 1), (s["q_sq"], min(u + 1, U0)))
                    if hg == 0:
                        pe.wait_ge(s["xt_lo"], T + 1)
                        if T % TILES == 0:
                            pe.wait_ge(job_done, job_end[3 * layer])
                    for kc in range(KC):
                        cols = slice(hg * UW, (hg + 1) * UW)
                        last = three(first[:, 0:UW], xt[:, T % 2, 0, bt, kc, :], xt[:, T % 2, 1, bt, kc, :],
                                     wq[layer][:, 0, kc, cols], wq[layer][:, 1, kc, cols],
                                     kc == 0, kc == KC - 1)
                    last.then_inc(s["q_proj"], 1)

                def small():
                    for T in range(STEPS):
                        n0 = T * STEP_N
                        layer, t = divmod(T, TILES)
                        if n == n0 - 16:
                            take(True, (s["xt_lo"], T + 1))
                            pe.wait_ge(s["xn"], T + 1)
                            for bt in range(B):
                                for kc in range(KC):
                                    at_ = (bt * KC + kc) * P
                                    last = te.transpose(second[:, at_:at_ + P], xn[:, bt, kc * P:(kc + 1) * P], ident[:, :])
                            last.then_inc(s["xt"], 1)
                        if n == n0 - 12:
                            take(True, (s["kv_v"], T + 1))
                            pe.wait_ge(s["xt_lo"], T + 1)
                            if t == 0:
                                pe.wait_ge(job_done, job_end[3 * layer + 1])
                            for bt in range(B):
                                for kc in range(KC):
                                    last = three(second[:, bt * 2 * DH:(bt + 1) * 2 * DH],
                                                 xt[:, T % 2, 0, bt, kc, :], xt[:, T % 2, 1, bt, kc, :],
                                                 wkv[layer][:, 0, kc, :], wkv[layer][:, 1, kc, :],
                                                 kc == 0, kc == KC - 1)
                            last.then_inc(s["kv"], 1)
                        if n == n0 - 8:
                            take(True, (s["k_lo"], T + 1))
                            if layer == 0:
                                pe.wait_ge(s["k_dup"], T + 1)
                            for bt in range(B):
                                last = te.transpose(second[:, bt * P:(bt + 1) * P], k_d[:, bt, :], ident[:, :])
                            last.then_inc(s["kt"], 1)
                    if k == 2 and 0 <= m - 1 < NU:
                        u = m - 1
                        take(True, (s["ot_lo"], u + 1))
                        pe.wait_ge(s["o_n"], u + 1)
                        o_f = o_n[:, :, :].rearrange("p h d -> p (h d)")
                        for cc in range(UW // P):
                            last = te.transpose(second[:, cc * P:(cc + 1) * P], o_f[:, cc * P:(cc + 1) * P], ident[:, :])
                        last.then_inc(s["ot"], 1)
                    if k == 3 and 0 <= m - 1 < NU:
                        u = m - 1
                        layer, hg = u // U0, (u % UNITS) // B
                        take(True, (s["y_acc"], u + 1))
                        if u % U0 == 0:
                            pe.wait_ge(job_done, job_end[3 * layer + 2])
                        for cc in range(UW // P):
                            rows_ = hg * (UW // P) + cc
                            last = three(second[:, 0:D], ot_hi[:, cc * P:(cc + 1) * P], ot_lo[:, cc * P:(cc + 1) * P],
                                         wo[layer][:, 0, rows_, :], wo[layer][:, 1, rows_, :],
                                         cc == 0, cc == UW // P - 1)
                        last.then_inc(s["y"], 1)

                now, before = plan.at(n), plan.at(n - 1)
                for j in range(max(1, len(now), len(before))):
                    if j < len(now):
                        gi = now[j]
                        _, j0, nb = plan.groups[gi]
                        pe.wait_ge(s["probs"], n + 1)
                        if gi >= 2:
                            pe.wait_ge(s["p_lo"], gi - 1)
                        for jj in range(nb):
                            last = te.transpose(tp[gi % 2][:, jj * P:(jj + 1) * P],
                                                probs[:, n % 2, (j0 + jj) * P:(j0 + jj + 1) * P], ident[:, :])
                        last.then_inc(s["pt"], 1)
                    if j < len(before):
                        pv(before[j])
                    if j == 0:
                        small()

            def x_t(cn):
                ch = cn % CHUNKS
                for kc, bank in enumerate((op, aux)):
                    if cn == 0:
                        release(2)
                        pe.wait_ge(s["x_new"], STEPS * B)
                    else:
                        pe.wait_ge(f["xt_lo"], KC * (cn - 1) + kc + 1)
                        if kc == 1:
                            pe.wait_ge(f["shifted"], cn)
                    if cn >= CHUNKS:
                        pe.wait_ge(f["y"], CHUNK * EB * (cn - CHUNKS + 1))
                    for i_ in range(CHUNK):
                        last = te.transpose(bank[:, i_ * P:(i_ + 1) * P], x[:, ch * CHUNK + i_, kc * P:(kc + 1) * P],
                                            ident[:, :])
                    last.then_inc(f["xt"], 1)

            def logits(cn):
                layer = cn // CHUNKS
                pe.wait_ge(f["xt_lo"], KC * (cn + 1))
                for i_ in range(CHUNK):
                    cols = slice(i_ * P, (i_ + 1) * P)
                    for kc in range(KC):
                        last = three(aux[:, i_ * E:(i_ + 1) * E], mx_hi[:, cn % 2, kc, cols], mx_lo[:, cn % 2, kc, cols],
                                     wt_s[:, layer, 0, kc, :], wt_s[:, layer, 1, kc, :], kc == 0, kc == KC - 1)
                last.then_inc(f["logit"], 1)

            def gate_up(en):
                cn, e = divmod(en, EB)
                layer = cn // CHUNKS
                if en >= 2:
                    pe.wait_ge(f["h"], en - 1)
                if cn % CHUNKS == 0:
                    pe.wait_ge(job_done, job_end[9 + 4 * layer] if e >= E else job_end[7 + 4 * layer])
                for name, at_ in (("gate", 0), ("up", 512)):
                    for kc in range(KC):
                        if e < E:
                            w_hi, w_lo = (moe_view(layer, hl, name, 2048)[:, (e * KC + kc) * M:(e * KC + kc + 1) * M]
                                          for hl in range(2))
                        else:
                            c0 = kc * SM + (e - E) * M
                            w_hi, w_lo = (moe_view(layer, hl, "s" + name, 512)[:, c0:c0 + M] for hl in range(2))
                        last = three(sc[en % 2][:, at_:at_ + 512], w_hi, w_lo,
                                     mx_hi[:, cn % 2, kc, :], mx_lo[:, cn % 2, kc, :], kc == 0, kc == KC - 1)
                last.then_inc(f["gu"], 1)

            def down(en):
                cn, e = divmod(en, EB)
                layer = cn // CHUNKS
                pe.wait_ge(f["h_lo"], en + 1)
                if cn % CHUNKS == 0:
                    pe.wait_ge(job_done, job_end[9 + 4 * layer] if e >= E else job_end[8 + 4 * layer])
                name, c0 = ("down", e * D) if e < E else ("sdown", (e - E) * D)
                size = 2048 if e < E else 512
                w_hi, w_lo = (moe_view(layer, hl, name, size)[:, c0:c0 + D] for hl in range(2))
                for i_ in range(CHUNK):
                    if i_ % 2 == 0 and en >= 1:
                        pe.wait_ge(f["y"], CHUNK * (en - 1) + i_ + 2)
                    cols = slice(i_ * P, (i_ + 1) * P)
                    last = three(tp[i_ // 2][:, (i_ % 2) * D:(i_ % 2 + 1) * D], h_hi[:, en % 2, cols],
                                 h_lo[:, en % 2, cols], w_hi, w_lo, True, True)
                    if i_ % 2 == 1:
                        last.then_inc(f["down"], 1)

            x_t(0)
            logits(0)
            for en in range(2 * CHUNKS * EB + 1):
                cn, e = divmod(en, EB)
                if en < 2 * CHUNKS * EB:
                    gate_up(en)
                if en >= 1:
                    down(en - 1)
                if cn + 1 < 2 * CHUNKS:
                    if e == 4:
                        x_t(cn + 1)
                    if e == 6:
                        logits(cn + 1)


def kernel(**inputs):
    import numpy as np
    import concourse.bacc as bacc
    from concourse.bass_utils import run_bass_kernel_spmd

    nc = bacc.Bacc("TRN2", target_bir_lowering=False, num_devices=1)
    arrays, aps = {}, {}
    for name, value in inputs.items():
        v = np.ascontiguousarray(value)
        if v.dtype == np.bool_:
            v = v.view(np.int32)
        arrays["in_" + name] = v
        aps[name] = nc.dram_tensor("in_" + name, v.shape, mybir.dt.from_np(v.dtype), kind="ExternalInput").ap()
    out = nc.dram_tensor("out", (B, S, D), F32, kind="ExternalOutput").ap()
    model(nc, aps, out)
    return run_bass_kernel_spmd(nc, [arrays], core_ids=[0]).results[0]["out"]
```

```python
import concourse.bass as bass
from concourse import mybir
from contextlib import ExitStack

F32 = mybir.dt.float32
F16 = mybir.dt.float16
I32 = mybir.dt.int32
U8 = mybir.dt.uint8
ALU = mybir.AluOpType
ACT = mybir.ActivationFunctionType
AX = mybir.AxisListType.X

P = 128
B, S, D = 2, 1024, 256
H, DH = 16, 64
INNER = H * DH
TILES = S // P
KC = D // P
HU = 4
HG = H // HU
UNITS = HG * B
STEPS = 2 * TILES
UW = HU * DH
E, M = 8, 128
SM = 256
G = 64
CHUNK = 4
CHUNKS = B * TILES // CHUNK
EB = E + SM // M

WS = 256.0
BIG = 60000.0
NEG = -1.0e30
EPS = 1e-5
TAB = S + P


class Plan:

    def __init__(self):
        self.steps = STEPS * UNITS * HU
        self.groups = []
        self.first_group = []
        for n in range(self.steps):
            self.first_group.append(len(self.groups))
            nk = self.tile(n) + 1
            for j in range(0, nk, 4):
                self.groups.append((n, j, min(4, nk - j)))
        self.first_group.append(len(self.groups))

    def tile(self, n):
        return (n // (UNITS * HU)) % TILES

    def layer(self, n):
        return n // (UNITS * HU * TILES)

    def unit(self, n):
        return n // HU

    def of(self, n):
        return range(self.first_group[n], self.first_group[n + 1])

    def at(self, n):
        return list(self.of(n)) if 0 <= n < self.steps else []

    def groups_done(self, n):
        return self.first_group[n + 1]


def model(nc, a, out):
    plan = Plan()
    N = plan.steps
    ctx = ExitStack()
    with ctx:
        def sb(name, shape, dt=F32):
            return ctx.enter_context(nc.sbuf_tensor(name, shape, dt))

        def pb(name, shape):
            return ctx.enter_context(nc.psum_tensor(name, shape, F32))

        def sem(name):
            return ctx.enter_context(nc.semaphore(name))

        table = nc.dram_tensor("rel_table", (H, P, TAB + P), F32).ap()

        x = sb("x", [P, B * TILES, D])
        bias = sb("bias", [P, 2, HU, S])
        moe_w = sb("moe_w", [P, 7680])
        wq = [sb(f"wq{i}", [P, 2, KC, INNER], F16) for i in range(2)]
        wkv = [sb(f"wkv{i}", [P, 2, KC, 2 * DH], F16) for i in range(2)]
        wo = [sb(f"wo{i}", [P, 2, INNER // P, D], F16) for i in range(2)]
        stage = sb("stage", [P, 2, 2048])
        k_a = [sb(f"k_a{i}", [P, B, S], F16) for i in range(2)]
        k_b = [sb(f"k_b{i}", [P, B, S], F16) for i in range(2)]
        v_s = [sb(f"v_s{i}", [P, B * TILES, 2, DH], F16) for i in range(2)]
        q_a = sb("q_a", [P, 2, HU * P], F16)
        q_b = sb("q_b", [P, 2, HU * P], F16)
        q_n = sb("q_n", [P, 2, UW])
        q_sq = sb("q_sq", [P, HU, DH])
        q_ss = sb("q_ss", [P, HU])
        q_r = sb("q_r", [P, HU])
        xt = sb("xt", [P, 2, 2, B, KC, P], F16)
        xn = sb("xn", [P, B, D])
        st6 = sb("st6", [P, B, 6])
        mv = sb("mv", [P, B, 2])
        rstd = sb("rstd", [P, B])
        k_d = sb("k_d", [P, B, 2 * DH])
        k_sq = sb("k_sq", [P, B, DH])
        k_ss = sb("k_ss", [P, B])
        k_r = sb("k_r", [P, B])
        biased = sb("biased", [P, 2, S])
        probs = sb("probs", [P, 2, S])
        p_hi = sb("p_hi", [P, 4, 4 * P], F16)
        p_lo = sb("p_lo", [P, 4, 4 * P], F16)
        neg_null = sb("neg_null", [P, 2, HU])
        neg_max = sb("neg_max", [P, 2, HU])
        rows = sb("rows", [P, 2, HU])
        d_null = sb("d_null", [P, HU])
        p_null = sb("p_null", [P, HU])
        denom = sb("denom", [P, HU])
        r_den = sb("r_den", [P, HU])
        o_null = sb("o_null", [P, HU, DH])
        o_raw = sb("o_raw", [P, HU, DH])
        o_n = sb("o_n", [P, HU, DH])
        ot_hi = sb("ot_hi", [P, UW], F16)
        ot_lo = sb("ot_lo", [P, UW], F16)
        y_acc = sb("y_acc", [P, B, D])
        y_st = sb("y_st", [P, 6])
        y_mv = sb("y_mv", [P, 2])
        y_rs = sb("y_rs", [P, 1])
        y_s = sb("y_s", [P, D])
        ident = sb("ident", [P, P])
        mhalf = sb("mhalf", [P, 16])
        k_scale = sb("k_scale", [P, DH])
        q_scale = sb("q_scale", [P, DH])
        null_b = [sb(f"null_b{i}", [P, H]) for i in range(2)]
        null_k = sb("null_k", [P, DH])
        null_kd = p_hi[:, 0, :].bitcast(F32).rearrange("p (l n) -> p l n", l=2)
        null_v = sb("null_v", [P, DH])
        null_sq = sb("null_sq", [P, DH])
        null_r = sb("null_r", [P, 1])
        kn_a = sb("kn_a", [P, 2], F16)
        kn_b = sb("kn_b", [P, 2], F16)
        g_in = [sb(f"g_in{i}", [P, KC]) for i in range(2)]
        g_out = [sb(f"g_out{i}", [P, D]) for i in range(2)]
        mask_words = probs[:, 0, :].bitcast(I32).rearrange("p (l n) -> p l n", l=2)
        mask8 = probs[:, 0, :].bitcast(U8).rearrange("p (l n) -> p l n", l=2)
        ones64 = sb("ones64", [G, P])
        w1_sb = bias[:, 1, 0, 0:KC * D].rearrange("p (k n) -> p k n", k=KC)
        w2_sb = bias[:, 1, 1, 0:KC * H].rearrange("p (k n) -> p k n", k=KC)
        b2_sb = sb("b2_sb", [H, 1])
        rel_i = sb("rel_i", [P, TILES], I32)
        rel_f = sb("rel_f", [P, TILES])
        r_st = sb("r_st", [P, TILES, 6])
        r_mv = sb("r_mv", [P, TILES, 2])
        r_rs = sb("r_rs", [P, TILES])
        rh = moe_w[:, 0:2048].rearrange("p (k n) -> p k n", k=TILES)
        re = moe_w[:, 2048:4096].rearrange("p (k n) -> p k n", k=TILES)
        rht = moe_w[:, 4096:6144].rearrange("p (c k n) -> p c k n", c=KC, k=TILES)
        rvec = moe_w[:, 6144:7424].rearrange("p (v n) -> p v n", v=5)
        tab = moe_w[0:H, 0:TAB]
        wt_n = sb("wt_n", [E, 2, D])
        wg_n = sb("wg_n", [E, 2, G])
        cond_n = sb("cond_n", [B, G])
        wt_s = sb("wt_s", [P, 2, 2, KC, E], F16)
        wt_f = sb("wt_f", [P, 2, KC, E])
        wg_t = sb("wg_t", [G, 2, E])
        cond_t = sb("cond_t", [G, B])
        cond_b = p_lo[0:G, 0, :].bitcast(F32).rearrange("p (b n) -> p b n", b=B)
        lg_half = sb("lg_half", [P, 2, B, E])
        place = sb("place", [P, E])
        mx_hi, mx_lo = (t_[:, :, :].rearrange("p a (k n) -> p a k n", k=KC) for t_ in (k_a[0], k_b[0]))
        gl = [sb(f"gl{i}", [P, CHUNK, E]) for i in range(6)]
        gm = [sb(f"gm{i}", [P, CHUNK]) for i in range(6)]
        comb = sb("comb", [P, 2, CHUNK, E])
        g_t = biased[:, 0, 0:512]
        g_l = biased[:, 1, 0:512]
        h_f = probs[:, :, 0:512]
        h_hi, h_lo = p_hi, p_lo
        moe_h = [moe_w[:, :].bitcast(F16),
                 bias[:, :, :, :].rearrange("p a h n -> p (a h n)")[:, 0:7680].bitcast(F16)]

        def moe_view(layer, hl, off, n):
            base = 2 * off_base[off]
            size = off_size[off]
            return moe_h[layer][:, base + hl * size: base + hl * size + n]

        sizes = {"gate": 2048, "up": 2048, "down": 2048, "sgate": 512, "sup": 512, "sdown": 512}
        off_base, off_size, at = {}, {}, 0
        for name, size in sizes.items():
            off_base[name], off_size[name] = at, size
            at += size

        sc = [pb(f"sc{i}", [P, S]) for i in range(2)]
        tp = [pb(f"tp{i}", [P, 512]) for i in range(2)]
        op = pb("op", [P, 512])
        aux = pb("aux", [P, 512])

        def heads(t, e):
            return t.rearrange("p (c e q) -> p e c q", e=2, q=P)[:, e]

        def free_banks(n):
            return 0 <= n < N - 4 and all(plan.tile(i) < TILES // 2 for i in range(n + 1, n + 4))

        def banks(n):
            if free_banks(n):
                return sc[1][:, 512:1024] if n % HU == 0 else aux, sc[n % 2][:, 512:1024]
            return aux, aux

        def sems(part, names):
            return {name: sem(part + "_" + name) for name in names.split()}

        setup = sems("setup", """mhalf ident rel kn0 place ones penalty big nss nrinv nkd nt nka nkb
                    mt cb lg lgh stats rstd z tanh h pt t mm tab""")
        s = sems("attn", """scores bias biased probs
                    pt p_hi p_lo pv
                    q_proj q_ss q_nd q_na q_t q_hi q_lo q_dup q_null null
                    x_st x_rs xn xt xt_hi xt_lo kv kv_act kv_r kv_d kv_v k_dup kt k_hi k_lo
                    d_null p_null denom r_den o_null o_raw o_n ot ot_hi ot_lo y y_s y_acc
                    y_st y_rs y_n x_new""")
        f = sems("moe", """xt xt_hi xt_lo logit shifted exp comb gu tenth leaky h h_hi h_lo down y out""")
        job_done = sem("job_done")
        dve_chain = sem("dve_chain")
        pool_chain = sem("pool_chain")
        table_in = [sem(f"table_in{i}") for i in range(HG)]
        table_rest = [sem(f"table_rest{i}") for i in range(HG)]
        s_bias = [sem(f"bias_in{i}") for i in range(2)]
        s_stage = [sem(f"stage_in{i}") for i in range(2)]
        s_in = {name: sem("in_" + name) for name in ("x", "rel", "w1", "w2", "head", "mask", "moe")}

        def bcast(ap, n):
            return bass.AP(ap.tensor, ap.offset, [[0, P], [1, n]])

        def flat(t):
            names_ = {3: "p a b -> p (a b)", 4: "p a b c -> p (a b c)"}
            return t.rearrange(names_[len(t.shape)]) if len(t.shape) > 2 else t

        jobs = []
        for i, pre in ((0, "L0_cond_"), (1, "L1_cond_")):
            w_o = a[pre + ("Wout" if i == 0 else "Wo")]
            jobs.append(([(a[pre + "Wkv"].rearrange("(k p) n -> p k n", p=P), 0, (KC, 2 * DH))],
                         [(flat(wkv[i][:, 0]), flat(wkv[i][:, 1]), 0, 256)], i, 2 * DH))
            jobs.append(([(a[pre + "Wq"].rearrange("(k p) n -> p k n", p=P), 0, (KC, INNER))],
                         [(flat(wq[i][:, 0]), flat(wq[i][:, 1]), 0, 2048)], i, INNER))
            jobs.append(([(w_o.rearrange("(c p) n -> p c n", p=P), 0, (INNER // P, D))],
                         [(flat(wo[i][:, 0]), flat(wo[i][:, 1]), 0, 2048)], None, 0))
        for i, pre in ((0, "L2_cond_"), (1, "L3_cond_")):
            def ends(name):
                return moe_view(i, 0, name, sizes[name]), moe_view(i, 1, name, sizes[name])
            jobs.append(([(a[pre + "w_gate"].rearrange("e (k p) m -> p (e k) m", p=P), 0, (E * KC, M))],
                         [(*ends("gate"), 0, 2048)], None, 0))
            jobs.append(([(a[pre + "w_up"].rearrange("e (k p) m -> p (e k) m", p=P), 0, (E * KC, M))],
                         [(*ends("up"), 0, 2048)], None, 0))
            jobs.append(([(a[pre + "w_down"].rearrange("e m n -> m e n"), 0, (E, D))],
                         [(*ends("down"), 0, 2048)], None, 0))
            jobs.append(([(a[pre + "sw_gate"].rearrange("(k p) m -> p k m", p=P), 0, (KC, SM)),
                          (a[pre + "sw_up"].rearrange("(k p) m -> p k m", p=P), 512, (KC, SM)),
                          (a[pre + "sw_down"].rearrange("(k p) m -> p k m", p=P), 1024, (SM // P, D))],
                         [(*ends("sgate"), 0, 512), (*ends("sup"), 512, 512),
                          (*ends("sdown"), 1024, 512)], None, 0))
        PIECE = 256
        pieces = []
        job_end = []
        for jn, (_, ends_, gain, per) in enumerate(jobs):
            for hi, lo, at, size in ends_:
                step = min(PIECE, per) if gain is not None else PIECE
                for c in range(0, size, step):
                    w = min(step, size - c)
                    pieces.append((jn, hi[:, c:c + w], lo[:, c:c + w], at + c, w, gain,
                                   (at + c) // per if gain is not None else 0))
            job_end.append(len(pieces))
        stage_value = []
        so_far = [0, 0]
        for jn, (loads, *_rest) in enumerate(jobs):
            so_far[jn % 2] += 16 * len(loads)
            stage_value.append(so_far[jn % 2])

        def kv_acts(T):
            return 5 * min(T + 1, TILES) + 3 * max(0, T + 1 - TILES)

        def load_at(jn):
            return 4 * (jn - 3) + 1 + (TILES * HG // 2 if jn >= 6 else 0)

        def y_adds(u):
            T, at_ = divmod(u, UNITS)
            return T * (UNITS - B) + max(0, at_ - B + 1)

        def load_job(eng, jn):
            if jn >= 2:
                eng.wait_ge(job_done, job_end[jn - 2])
            for src, at_, (c, n_) in jobs[jn][0]:
                eng.dma_start(stage[:, jn % 2, at_:at_ + c * n_].rearrange("p (c n) -> p c n", c=c),
                              src).then_inc(s_stage[jn % 2], 16)

        def write_table(eng, hg, last):
            j0, j1 = (S - P, TAB) if last else (0, S - P)
            dst = bass.AP(table.tensor, hg * HU * P * (TAB + P) + j0,
                          [[P * (TAB + P), HU], [TAB + P + 1, P], [1, j1 - j0]])
            eng.dma_start(dst, tab[hg * HU:(hg + 1) * HU, j0:j1].unsqueeze(1).to_broadcast([HU, P, j1 - j0]))\
                .then_inc((table_in if last else table_rest)[hg], 16)

        def load_bias(eng, g):
            step, hg = g // HG, g % HG
            layer, t = step // TILES, step % TILES
            w = P * (t + 1)
            if g >= 2:
                eng.wait_ge(s["biased"], UNITS // HG * HU * (g - 1))
            if layer == 0:
                if step == 0:
                    eng.wait_ge(table_in[hg], 16)
                if step == 1:
                    eng.wait_ge(table_rest[hg], 16)
                src = table[hg * HU:(hg + 1) * HU, :, (TILES - 1 - t) * P + P - 1:TILES * P + P - 1]\
                    .rearrange("h p j -> p h j")
            else:
                src = a["fside_16xSxS_0"][hg * HU:(hg + 1) * HU, t * P:(t + 1) * P, 0:w]\
                    .rearrange("h p j -> p h j")
            eng.dma_start(bias[:, g % 2, :, 0:w], src).then_inc(s_bias[g % 2], 16)

        HEAD_LOADS = 13
        NU = N // HU
        U0 = NU // 2
        STEP_N = UNITS * HU
        FIRST, LAST = -20, N + 8

        TABLE_AT = {-17: 4, -15: 5, -14: 6, -10: 7, -8: 8}

        block = ctx.enter_context(nc.Block())

        @block.sync
        def _(sp):
            load_job(sp, 0)
            load_job(sp, 1)
            sp.dma_start(w1_sb[:, :, :], a["L0_cond_w1"].rearrange("(k p) n -> p k n", p=P)).then_inc(s_in["w1"], 16)
            sp.dma_start(w2_sb[:, :, :], a["L0_cond_w2"].rearrange("(k p) n -> p k n", p=P)).then_inc(s_in["w2"], 16)
            sp.dma_start(b2_sb[:, :], a["L0_cond_b2"].rearrange("(h a) -> h a", a=1)).then_inc(s_in["w2"], 16)
            load_job(sp, 2)
            sp.wait_ge(setup["tab"], 3)
            write_table(sp, 0, True)
            load_bias(sp, 0)
            for hg in range(1, HG):
                write_table(sp, hg, True)
            load_bias(sp, 1)
            write_table(sp, 0, False)
            n_jobs = 3
            for g in range(2, STEPS * HG):
                load_bias(sp, g)
                if g - 1 < HG:
                    write_table(sp, g - 1, False)
                if n_jobs < 10 and g == load_at(n_jobs) + 1:
                    load_job(sp, n_jobs)
                    n_jobs += 1
            for jn in range(n_jobs, len(jobs)):
                load_job(sp, jn)
            for ch in range(CHUNKS):
                sp.wait_ge(f["y"], CHUNK * EB * (CHUNKS + ch + 1))
                bt, t0 = divmod(ch * CHUNK, TILES)
                sp.dma_start(out[bt, t0 * P:(t0 + CHUNK) * P, :].rearrange("(t p) n -> p t n", p=P),
                             x[:, ch * CHUNK:(ch + 1) * CHUNK, :]).then_inc(f["out"], 16)
            sp.wait_ge(f["out"], 16 * CHUNKS)

        @block.gpsimd
        def _(pool):
            gp = nc.gpsimd
            chain = [0]

            def link(ins):
                chain[0] += 1
                ins.then_inc(pool_chain, 1)
                pool.wait_ge(pool_chain, chain[0])

            gp.memset(mhalf[:, :], -0.5).then_inc(setup["mhalf"], 1)
            link(gp.memset(ident[:, :], 0.0))
            gp.affine_select(out=ident[:, :], in_=ident[:, :], compare_op=ALU.not_equal, fill=1.0, base=0,
                             pattern=[[-1, P]], channel_multiplier=1).then_inc(setup["ident"], 1)
            link(gp.iota(rel_i[:, :], [[-P, TILES]], base=S - 1, channel_multiplier=-1))
            gp.tensor_copy(rel_f[:, :], rel_i[:, :]).then_inc(setup["rel"], 1)
            gp.memset(kn_b[:, :], 0.0).then_inc(setup["kn0"], 1)
            gp.memset(ones64[:, :], 1.0).then_inc(setup["ones"], 1)
            for e in range(E):
                gp.memset(place[:, e:e + 1], float(E - e)).then_inc(setup["place"], 1)
            def rel_rstd(r):
                pool.wait_ge(setup["stats"], r + 1)
                link(gp.tensor_scalar(r_rs[:, :], r_mv[:, :, 1], EPS, 0.0, ALU.add, ALU.add))
                gp.tensor_tensor(r_rs[:, :], r_rs[:, :], mhalf[:, 0:TILES], ALU.pow).then_inc(setup["rstd"], 1)

            rel_rstd(0)
            pool.wait_ge(setup["rstd"], 1)
            pool.wait_ge(setup["place"], E)
            gp.memset(q_b[DH:P, :, :], BIG).then_inc(setup["big"], 1)
            pool.wait_ge(s_in["mask"], 2 * 16)
            for i in range(2):
                gp.tensor_scalar(k_b[i][DH:P, :, :].rearrange("p b n -> p (b n)"), mask8[DH:P, i, :],
                                 -1.0, BIG, ALU.add, ALU.mult).then_inc(setup["penalty"], 1)
            pool.wait_ge(setup["big"], 1)
            pool.wait_ge(setup["penalty"], 2)

            def piece(n):
                jn, hi, lo, at_, w, gain, gc = pieces[n]
                pool.wait_ge(s_stage[jn % 2], stage_value[jn])
                src = stage[:, jn % 2, at_:at_ + w]
                if gain is None:
                    link(gp.tensor_scalar(src, src, WS, 1.0, ALU.mult, ALU.mult))
                else:
                    link(gp.tensor_scalar(src, src, g_in[gain][:, gc:gc + 1], WS, ALU.mult, ALU.mult))
                link(gp.tensor_copy(hi, src))
                gp.tensor_tensor(lo, src, hi, ALU.subtract).then_inc(job_done, 1)

            split = [0]

            def split_to(n):
                while split[0] < n:
                    piece(split[0])
                    split[0] += 1

            pool.wait_ge(s_in["head"], 16 * HEAD_LOADS)
            split_to(job_end[0] + 5)
            pool.wait_ge(setup["nss"], 1)
            link(gp.tensor_tensor(null_r[:, :], null_r[:, :], mhalf[:, 0:1], ALU.pow))
            gp.tensor_scalar(null_r[:, :], null_r[:, :], 1e12, 1.0, ALU.min, ALU.mult).then_inc(setup["nrinv"], 1)
            for n in range(FIRST, LAST):
                m, k = divmod(n, HU)
                if TABLE_AT.get(n) == 4:
                    rel_rstd(1)
                if k == 1 and 1 <= m <= NU:
                    u = m - 1
                    pool.wait_ge(s["o_raw"], u + 1)
                    pool.wait_ge(s["r_den"], u + 1)
                    if u >= 1:
                        pool.wait_ge(s["ot"], u)
                    gp.tensor_tensor(o_n[:, :, :], o_raw[:, :, :],
                                     r_den[:, :].unsqueeze(2).to_broadcast([P, HU, DH]), ALU.mult)\
                        .then_inc(s["o_n"], 1)
                if k == 2 and 0 <= m + 3 < U0:
                    u = m + 3
                    pool.wait_ge(s["q_ss"], HU * (u + 1))
                    if u >= 1:
                        pool.wait_ge(s["q_nd"], u)
                    link(gp.tensor_tensor(q_r[:, :], q_ss[:, :], mhalf[:, 0:HU], ALU.pow))
                    link(gp.tensor_scalar(q_r[:, :], q_r[:, :], 1e12 / WS, 1.0, ALU.min, ALU.mult))
                    pool.wait_ge(s["q_na"], u + 1)
                    q_h = q_n[:, u % 2, :].rearrange("p (h d) -> p h d", h=HU)
                    gp.tensor_tensor(q_h, q_h, q_r[:, :].unsqueeze(2).to_broadcast([P, HU, DH]), ALU.mult)\
                        .then_inc(s["q_nd"], 1)
                g, at_g = divmod(n + 4, 2 * HU)
                if at_g == 0 and TILES * HG <= g < STEPS * HG:
                    t = (g // HG) % TILES
                    pool.wait_ge(s_bias[g % 2], 16 * (g // 2 + 1))
                    blk = bias[:, g % 2, :, t * P:(t + 1) * P]
                    gp.affine_select(out=blk, in_=blk, compare_op=ALU.is_ge, fill=NEG, base=0,
                                     pattern=[[0, HU], [-1, P]], channel_multiplier=1).then_inc(s["bias"], 1)
                if k == 3 and 0 <= m < NU:
                    u = m
                    pool.wait_ge(s["probs"], HU * (u + 1))
                    gp.tensor_tensor(d_null[:, :], neg_max[:, u % 2, :], neg_null[:, u % 2, :], ALU.subtract)\
                        .then_inc(s["d_null"], 1)
                    pool.wait_ge(s["p_null"], u + 1)
                    if u >= 1:
                        pool.wait_ge(s["r_den"], u)
                    gp.tensor_tensor(denom[:, :], rows[:, u % 2, :], p_null[:, :], ALU.add).then_inc(s["denom"], 1)
                    if u >= 1:
                        pool.wait_ge(s["o_raw"], u)
                    gp.tensor_tensor(o_null[:, :, :], null_v[:, :].unsqueeze(1).to_broadcast([P, HU, DH]),
                                     p_null[:, :].unsqueeze(2).to_broadcast([P, HU, DH]), ALU.mult)\
                        .then_inc(s["o_null"], 1)
                for T in range(STEPS):
                    n0 = T * STEP_N
                    if n == n0 - 17:
                        pool.wait_ge(s["x_st"], T + 1)
                        link(gp.tensor_scalar(rstd[:, :], mv[:, :, 1], EPS, 0.0, ALU.add, ALU.add))
                        gp.tensor_tensor(rstd[:, :], rstd[:, :], mhalf[:, 0:B], ALU.pow).then_inc(s["x_rs"], 1)
                    if n == n0 - 11 and T < TILES:
                        pool.wait_ge(s["kv_act"], kv_acts(T))
                        link(gp.tensor_tensor(k_r[:, :], k_ss[:, :], mhalf[:, 0:B], ALU.pow))
                        gp.tensor_scalar(k_r[:, :], k_r[:, :], 1e12 / WS, 1.0, ALU.min, ALU.mult)\
                            .then_inc(s["kv_r"], 1)
                    if n == n0 - 9 and T < TILES:
                        pool.wait_ge(s["kv_d"], T + 1)
                        gp.tensor_copy(k_d[:, :, DH:2 * DH], k_d[:, :, 0:DH]).then_inc(s["k_dup"], 1)
                if k == 0 and 2 <= m <= NU + 1 and (m - 2) % UNITS >= B:
                    u = m - 2
                    pool.wait_ge(s["y_s"], u + 1)
                    if y_adds(u) >= 2:
                        pool.wait_ge(s["y_acc"], y_adds(u) - 1)
                    y_t = y_acc[:, u % B, :]
                    gp.tensor_tensor(y_t, y_t, y_s[:, :], ALU.add).then_inc(s["y_acc"], 1)
                for p_ in range(STEPS * B):
                    T, bt = divmod(p_, B)
                    mu = T * UNITS + (HG - 1) * B + bt
                    if n == HU * (mu + 2) + 1:
                        pool.wait_ge(s["y_st"], p_ + 1)
                        link(gp.tensor_scalar(y_rs[:, :], y_mv[:, 1:2], EPS, 0.0, ALU.add, ALU.add))
                        gp.tensor_tensor(y_rs[:, :], y_rs[:, :], mhalf[:, 0:1], ALU.pow).then_inc(s["y_rs"], 1)
                    if n == HU * (mu + 2) + 3:
                        pool.wait_ge(s["y_n"], p_ + 1)
                        y_t = y_acc[:, bt, :]
                        link(gp.tensor_tensor(y_t, y_t, g_out[T // TILES][:, :], ALU.mult))
                        x_t = x[:, bt * TILES + T % TILES, :]
                        gp.tensor_tensor(x_t, x_t, y_t, ALU.add).then_inc(s["x_new"], 1)
                if n < 0 and split[0] < job_end[2]:
                    split_to(split[0] + 1)
                if k == 1 and job_end[2] <= split[0] < job_end[9] and n >= 2 * HU * load_at(pieces[split[0]][0]):
                    if split[0] == job_end[5]:
                        for hg in range(HG):
                            pool.wait_ge(table_rest[hg], 16)
                    split_to(split[0] + 1)
            split_to(job_end[9])
            pool.wait_ge(s["biased"], N)
            for en in range(2 * CHUNKS * EB):
                if split[0] < len(pieces):
                    split_to(split[0] + 1)
                pool.wait_ge(f["h_hi"], en + 1)
                gp.tensor_tensor(h_lo[:, en % 4, :], h_f[:, en % 2, :], h_hi[:, en % 4, :], ALU.subtract)\
                    .then_inc(f["h_lo"], 1)

        @block.scalar
        def _(act):
            ac = nc.scalar
            for i, v in enumerate(("w0", "b0", "g0", "b1", "g1")):
                act.dma_start(rvec[:, i, :], bcast(a["L0_cond_" + v], D)).then_inc(s_in["rel"], 16)
            act.dma_start(k_scale[:, :], bcast(a["L0_cond_k_scale"], DH)).then_inc(s_in["head"], 16)
            act.dma_start(q_scale[:, :], bcast(a["L0_cond_q_scale"], DH)).then_inc(s_in["head"], 16)
            for i, pre in ((0, "L0_cond_"), (1, "L1_cond_")):
                act.dma_start(g_in[i][:, :], a[pre + ("g_norm" if i == 0 else "g_in")].rearrange("(k p) -> p k", p=P),
                              allow_slow_non_contiguous=True).then_inc(s_in["head"], 16)
                act.dma_start(g_out[i][:, :], bcast(a[pre + "g_out"], D)).then_inc(s_in["head"], 16)
                act.dma_start(null_b[i][:, :], bcast(a[pre + "null_attn_bias"], H)).then_inc(s_in["head"], 16)
            act.dma_start(null_k[:, :], bcast(a["cond_64"][0, :], DH)).then_inc(s_in["head"], 16)
            act.dma_start(null_v[:, :], bcast(a["cond_64"][1, :], DH)).then_inc(s_in["head"], 16)
            act.dma_start(cond_n[:, :], a["cond_64"]).then_inc(s_in["head"], 16)
            for i, pre in ((0, "L2_cond_"), (1, "L3_cond_")):
                act.dma_start(wt_n[:, i, :], a[pre + "wt"]).then_inc(s_in["head"], 16)
                act.dma_start(wg_n[:, i, :], a[pre + "wg"]).then_inc(s_in["moe"], 16)
            for i, v in enumerate(("mask_BxS_bf1", "mask_BxS_bk0")):
                mk = a[v]
                act.dma_start(mask_words[DH:P, i, :], bass.AP(mk.tensor, mk.offset, [[0, DH], [1, B * S // 4]]))\
                    .then_inc(s_in["mask"], 16)
            act.dma_start(x[:, :, :], a["x"].rearrange("b (t p) n -> p (b t) n", p=P)).then_inc(s_in["x"], 16)

            def table_stage(p_):
                r, part = divmod(p_, 4)
                if part == 2:
                    act.wait_ge(setup["z"], r + 1)
                    ac.activation(re, rh, ACT.Tanh, scale=0.5).then_inc(setup["tanh"], 1)
                elif part == 3:
                    for kc in range(KC):
                        act.wait_ge(setup["pt"], KC * r + kc + 1)
                        ac.activation(rht[:, kc, :, :].rearrange("p k n -> p (k n)"), sc[kc][:, :], ACT.Copy)\
                            .then_inc(setup["t"], 1)

            table_stage(2)
            table_stage(3)
            act.wait_ge(setup["nt"], 1)
            ac.activation(kn_a[:, :], aux[:, 0:2 * P].rearrange("p (l n) -> p l n", l=2)[:, :, 0], ACT.Copy)\
                .then_inc(setup["nka"], 1)
            for n in range(FIRST, LAST):
                m, k = divmod(n, HU)
                if n in TABLE_AT:
                    table_stage(TABLE_AT[n])
                first, second = banks(n)
                i = n + 1
                if 0 <= i < N:
                    w = P * (plan.tile(i) + 1)
                    u = plan.unit(i)
                    act.wait_ge(s["biased"], i + 1)
                    if i >= 2:
                        act.wait_ge(s["pt"], plan.groups_done(i - 2))
                    if i % HU == 0 and u >= 2:
                        act.wait_ge(s["denom"], u - 1)
                    ac.activation(probs[:, i % 2, 0:w], biased[:, i % 2, 0:w], ACT.Exp,
                                  bias=neg_max[:, u % 2, i % HU:i % HU + 1], scale=-1.0,
                                  accum_out=rows[:, u % 2, i % HU:i % HU + 1]).then_inc(s["probs"], 1)
                if k == 0 and 0 <= m - 2 < NU:
                    u = m - 2
                    act.wait_ge(s["y"], u + 1)
                    if u % UNITS < B:
                        if u >= UNITS:
                            act.wait_ge(s["x_new"], (u // UNITS - 1) * B + u % B + 1)
                        dst = y_acc[:, u % B, :]
                    else:
                        if y_adds(u) >= 2:
                            act.wait_ge(s["y_acc"], y_adds(u) - 1)
                        dst = y_s[:, :]
                    ac.activation(dst, first[:, 0:D], ACT.Copy, scale=1.0 / WS).then_inc(s["y_s"], 1)
                if k == 3 and 0 <= m + 2 < NU:
                    u = m + 2
                    act.wait_ge(s["q_t"], u + 1)
                    if u >= 2:
                        act.wait_ge(s["scores"], HU * (u - 1))
                    for e in range(2):
                        ac.activation(heads(q_b[0:DH, u % 2, :], e),
                                      first[e * DH:(e + 1) * DH, 0:UW].rearrange("p (c q) -> p c q", q=P), ACT.Copy)\
                            .then_inc(s["q_hi"], 1)
                    act.wait_ge(s["q_hi"], 2 * (u + 1))
                    ac.activation(q_a[0:DH, u % 2, :], q_b[0:DH, u % 2, :], ACT.Copy).then_inc(s["q_dup"], 1)
                if k == 1 and 0 <= m + 3 < NU:
                    u = m + 3
                    act.wait_ge(s["q_proj"], u + 1)
                    if u < U0:
                        if u >= 1:
                            act.wait_ge(s["q_nd"], u)
                        for h in range(HU):
                            ac.activation(q_sq[:, h, :], first[:, h * DH:(h + 1) * DH], ACT.Square,
                                          accum_out=q_ss[:, h:h + 1]).then_inc(s["q_ss"], 1)
                    ac.activation(q_n[:, u % 2, :], first[:, 0:UW], ACT.Copy, scale=1.0 if u < U0 else DH ** -0.5 / WS)\
                        .then_inc(s["q_na"], 1)

                def small():
                    for T in range(STEPS):
                        n0 = T * STEP_N
                        layer, t = divmod(T, TILES)
                        if n == n0 - 15:
                            act.wait_ge(s["xt"], T + 1)
                            if T >= 2:
                                act.wait_ge(s["q_proj"], UNITS * (T - 1))
                            ac.activation(xt[:, T % 2, 0, :, :, :].rearrange("p b c n -> p (b c n)"), second[:, :], ACT.Copy)\
                                .then_inc(s["xt_hi"], 1)
                        if n == n0 - 11:
                            act.wait_ge(s["kv"], T + 1)
                            if T >= 1:
                                act.wait_ge(s["kt"], T)
                            kv_ps = second[:, 0:B * 2 * DH].rearrange("p (b n) -> p b n", b=B)
                            if layer == 0:
                                for bt in range(B):
                                    ac.activation(k_sq[:, bt, :], kv_ps[:, bt, 0:DH], ACT.Square,
                                                  accum_out=k_ss[:, bt:bt + 1]).then_inc(s["kv_act"], 1)
                                    ac.activation(k_d[:, bt, 0:DH], kv_ps[:, bt, 0:DH], ACT.Copy).then_inc(s["kv_act"], 1)
                            else:
                                for i_ in range(2):
                                    ac.activation(k_d[:, :, i_ * DH:(i_ + 1) * DH], kv_ps[:, :, 0:DH], ACT.Copy,
                                                  scale=1.0 / WS).then_inc(s["kv_act"], 1)
                            ac.activation(v_s[layer][:, t::TILES, 0, :], kv_ps[:, :, DH:2 * DH], ACT.Copy, scale=1.0 / WS)\
                                .then_inc(s["kv_act"], 1)
                        if n == n0 - 7:
                            act.wait_ge(s["kt"], T + 1)
                            ac.activation(k_a[layer][:, :, t * P:(t + 1) * P],
                                          second[:, 0:B * P].rearrange("p (b n) -> p b n", b=B), ACT.Copy)\
                                .then_inc(s["k_hi"], 1)
                    if k == 2 and 0 <= m - 1 < NU:
                        u = m - 1
                        act.wait_ge(s["ot"], u + 1)
                        ac.activation(ot_hi[:, :], second[:, 0:UW], ACT.Copy).then_inc(s["ot_hi"], 1)

                now = plan.at(n)
                for j in range(max(1, len(now))):
                    if j < len(now):
                        gi = now[j]
                        nb = plan.groups[gi][2]
                        act.wait_ge(s["pt"], gi + 1)
                        if gi >= 4:
                            act.wait_ge(s["pv"], gi - 3)
                        ac.activation(p_hi[:, gi % 4, 0:nb * P], tp[gi % 2][:, 0:nb * P], ACT.Copy)\
                            .then_inc(s["p_hi"], 1)
                    if j == 0:
                        small()
                if k == 3 and 0 <= m < NU:
                    u = m
                    act.wait_ge(s["d_null"], u + 1)
                    if u >= 1:
                        act.wait_ge(s["o_null"], u)
                    ac.activation(p_null[:, :], d_null[:, :], ACT.Exp).then_inc(s["p_null"], 1)

            def x_hi(cn):
                for kc, bank in enumerate((op, aux)):
                    act.wait_ge(f["xt"], KC * cn + kc + 1)
                    if cn >= 2 and kc == 0:
                        act.wait_ge(f["gu"], EB * (cn - 1))
                    ac.activation(mx_hi[:, cn % 2, kc, :], bank[:, :], ACT.Copy).then_inc(f["xt_hi"], 1)

            def gate_exp(cn):
                act.wait_ge(f["shifted"], cn + 1)
                ac.activation(gl[1][:, :, :], gl[0][:, :, :], ACT.Exp).then_inc(f["exp"], 1)

            x_hi(0)
            gate_exp(0)
            for en in range(2 * CHUNKS * EB):
                cn, e = divmod(en, EB)
                act.wait_ge(f["gu"], en + 1)
                if en >= 1:
                    act.wait_ge(f["leaky"], en)
                ac.activation(g_t, sc[en % 2][:, 0:512], ACT.Copy, scale=0.01 / WS).then_inc(f["tenth"], 1)
                act.wait_ge(f["h"], en + 1)
                if en >= 4:
                    act.wait_ge(f["down"], 2 * (en - 3))
                ac.activation(h_hi[:, en % 4, :], h_f[:, en % 2, :], ACT.Copy).then_inc(f["h_hi"], 1)
                if cn + 1 < 2 * CHUNKS and e == 4:
                    x_hi(cn + 1)
                if cn + 1 < 2 * CHUNKS and e == 6:
                    gate_exp(cn + 1)

        @block.vector
        def _(dve):
            ve = nc.vector
            chain = [0]

            def link(ins):
                chain[0] += 1
                ins.then_inc(dve_chain, 1)
                dve.wait_ge(dve_chain, chain[0])

            def table_stage(p_):
                r, part = divmod(p_, 4)
                if r == 2:
                    for i in range(2):
                        dve.wait_ge(setup["mm"], 2 + i)
                        ve.tensor_scalar(tab[:, i * 512:(i + 1) * 512], tp[i][0:H, :], 0.5, b2_sb[:, 0:1],
                                         ALU.mult, ALU.add).then_inc(setup["tab"], 1)
                    ve.memset(tab[:, S:TAB], NEG).then_inc(setup["tab"], 1)
                elif part == 0:
                    if r == 0:
                        dve.wait_ge(s_in["rel"], 5 * 16)
                        dve.wait_ge(setup["rel"], 1)
                        for k in range(TILES):
                            last = ve.scalar_tensor_tensor(rh[:, k, :], rvec[:, 0, :], rel_f[:, k:k + 1],
                                                           rvec[:, 1, :], ALU.mult, ALU.add)
                    else:
                        dve.wait_ge(setup["mm"], 1)
                        for i in range(2):
                            last = ve.scalar_tensor_tensor(rh[:, 4 * i:4 * i + 4, :],
                                                           sc[i][:, :].rearrange("p (k n) -> p k n", k=4), 0.5,
                                                           rvec[:, 3, :].unsqueeze(1).to_broadcast([P, 4, D]),
                                                           ALU.mult, ALU.add)
                    link(last)
                    for k in range(TILES):
                        last = ve.bn_stats(r_st[:, k, :], rh[:, k, :])
                    link(last)
                    for k in range(TILES):
                        last = ve.bn_aggr(r_mv[:, k, :], r_st[:, k, :])
                    last.then_inc(setup["stats"], 1)
                elif part == 1:
                    dve.wait_ge(setup["rstd"], r + 1)
                    for k in range(TILES):
                        last = ve.tensor_scalar(rh[:, k, :], rh[:, k, :], r_mv[:, k, 0:1], r_rs[:, k:k + 1],
                                                ALU.subtract, ALU.mult)
                    link(last)
                    ve.tensor_tensor(rh, rh, rvec[:, 2 + 2 * r, :].unsqueeze(1).to_broadcast([P, TILES, D]), ALU.mult)\
                        .then_inc(setup["z"], 1)
                elif part == 2:
                    dve.wait_ge(setup["tanh"], r + 1)
                    ve.scalar_tensor_tensor(rh, re, 1.0, rh, ALU.add, ALU.mult).then_inc(setup["h"], 1)

            for p_ in range(3):
                table_stage(p_)
            dve.wait_ge(s_in["head"], 16 * HEAD_LOADS)
            ve.tensor_tensor_reduce(out=null_sq[:, :], in0=null_k[:, :], in1=null_k[:, :], scale=1.0, scalar=0.0,
                                    op0=ALU.mult, op1=ALU.add, accum_out=null_r[:, :]).then_inc(setup["nss"], 1)
            link(ve.scalar_tensor_tensor(k_scale[:, :], k_scale[:, :], 8.0, q_scale[:, :], ALU.mult, ALU.mult))
            dve.wait_ge(setup["nrinv"], 1)
            for i in range(2):
                half = slice(i * DH, (i + 1) * DH)
                ve.scalar_tensor_tensor(null_kd[:, 0, half], null_k[:, :], null_r[:, 0:1], k_scale[:, :],
                                        ALU.mult, ALU.mult)
                last = ve.tensor_copy(null_kd[:, 1, half], null_k[:, :])
            last.then_inc(setup["nkd"], 1)
            dve.wait_ge(setup["nka"], 1)
            dve.wait_ge(setup["kn0"], 1)
            ve.tensor_tensor(kn_b[0:DH, :], aux[0:DH, 0:2 * P].rearrange("p (l n) -> p l n", l=2)[:, :, 0],
                             kn_a[0:DH, :], ALU.subtract).then_inc(setup["nkb"], 1)
            dve.wait_ge(setup["mt"], 1)
            link(ve.tensor_scalar(wt_f[:, :, :, :].rearrange("p l k e -> p (l k e)"), op[:, 0:32], WS, None, ALU.mult))
            for l in range(2):
                link(ve.tensor_copy(wt_s[:, l, 0, :, :], wt_f[:, l, :, :]))
                ve.tensor_tensor(wt_s[:, l, 1, :, :], wt_f[:, l, :, :], wt_s[:, l, 0, :, :], ALU.subtract)
            ve.tensor_copy(wg_t[:, :, :].rearrange("p l e -> p (l e)"), op[0:G, 32:48])
            link(ve.tensor_copy(cond_t[:, :], op[0:G, 48:50]))
            dve.wait_ge(setup["ones"], 1)
            for b in range(B):
                last = ve.tensor_scalar(cond_b[:, b, :], ones64[:, :], cond_t[:, b:b + 1], None, ALU.mult)
            last.then_inc(setup["cb"], 1)
            dve.wait_ge(setup["lg"], 1)
            ve.tensor_scalar(lg_half[:, :, :, :].rearrange("p l b e -> p (l b e)"), op[:, 64:96], 0.5, None, ALU.mult)\
                .then_inc(setup["lgh"], 1)

            dve.wait_ge(s_in["x"], 16)
            for n in range(FIRST, LAST):
                m, k = divmod(n, HU)
                if n in TABLE_AT:
                    table_stage(TABLE_AT[n])
                first, second = banks(n)
                if k == 1 and 1 <= m <= NU:
                    u = m - 1
                    dve.wait_ge(s["o_null"], u + 1)
                    dve.wait_ge(s["pv"], plan.groups_done(n - 2))
                    ve.tensor_tensor(o_raw[:, :, :], op[:, 0:UW].rearrange("p (h d) -> p h d", h=HU),
                                     o_null[:, :, :], ALU.add).then_inc(s["o_raw"], 1)
                    dve.wait_ge(s["denom"], u + 1)
                    ve.reciprocal(r_den[:, :], denom[:, :]).then_inc(s["r_den"], 1)
                i = n + 2
                if 0 <= i < N:
                    w = P * (plan.tile(i) + 1)
                    u = plan.unit(i)
                    g = i // (2 * HU)
                    dve.wait_ge(s["scores"], i + 1)
                    if i >= 2:
                        dve.wait_ge(s["probs"], i - 1)
                    if i % HU == 0:
                        dve.wait_ge(s["null"], u + 1)
                        if u >= 2:
                            dve.wait_ge(s["d_null"], u - 1)
                    if g < TILES * HG:
                        dve.wait_ge(s_bias[g % 2], 16 * (g // 2 + 1))
                    else:
                        dve.wait_ge(s["bias"], g - TILES * HG + 1)
                    ve.tensor_tensor_reduce(out=biased[:, i % 2, 0:w], in0=sc[i % 2][:, 0:w],
                                            in1=bias[:, g % 2, i % HU, 0:w], scale=-1.0,
                                            scalar=neg_null[:, u % 2, i % HU:i % HU + 1],
                                            op0=ALU.add, op1=ALU.min,
                                            accum_out=neg_max[:, u % 2, i % HU:i % HU + 1]).then_inc(s["biased"], 1)
                for T in range(STEPS):
                    n0 = T * STEP_N
                    layer, t = divmod(T, TILES)
                    tiles = [bt * TILES + t for bt in range(B)]
                    if n == n0 - 17:
                        if layer == 1:
                            dve.wait_ge(s["x_new"], B * (T - TILES + 1))
                        for bt in range(B):
                            last = ve.bn_stats(st6[:, bt, :], x[:, tiles[bt], :])
                        link(last)
                        for bt in range(B):
                            last = ve.bn_aggr(mv[:, bt, :], st6[:, bt, :])
                        last.then_inc(s["x_st"], 1)
                    if n == n0 - 16:
                        dve.wait_ge(s["x_rs"], T + 1)
                        for bt in range(B):
                            last = ve.tensor_scalar(xn[:, bt, :], x[:, tiles[bt], :], mv[:, bt, 0:1],
                                                    rstd[:, bt:bt + 1], ALU.subtract, ALU.mult)
                        last.then_inc(s["xn"], 1)
                if k == 3 and 0 <= m + 2 < NU:
                    u = m + 2
                    dve.wait_ge(s["q_hi"], 2 * (u + 1))
                    for e in range(2):
                        ve.tensor_tensor(heads(q_a[DH:P, u % 2, :], e),
                                         first[e * DH:(e + 1) * DH, 0:UW].rearrange("p (c q) -> p c q", q=P),
                                         heads(q_b[0:DH, u % 2, :], e), ALU.subtract).then_inc(s["q_lo"], 1)
                def small():
                    for T in range(STEPS):
                        n0 = T * STEP_N
                        layer, t = divmod(T, TILES)
                        if n == n0 - 15:
                            dve.wait_ge(s["xt_hi"], T + 1)
                            ve.tensor_tensor(xt[:, T % 2, 1, :, :, :].rearrange("p b c n -> p (b c n)"), second[:, :],
                                             xt[:, T % 2, 0, :, :, :].rearrange("p b c n -> p (b c n)"), ALU.subtract)\
                                .then_inc(s["xt_lo"], 1)
                        if n == n0 - 11:
                            dve.wait_ge(s["kv_act"], kv_acts(T))
                            kv_ps = second[:, 0:B * 2 * DH].rearrange("p (b n) -> p b n", b=B)
                            ve.scalar_tensor_tensor(v_s[layer][:, t::TILES, 1, :], kv_ps[:, :, DH:2 * DH], 1.0 / WS,
                                                    v_s[layer][:, t::TILES, 0, :], ALU.mult, ALU.subtract)\
                                .then_inc(s["kv_v"], 1)
                        if n == n0 - 7:
                            dve.wait_ge(s["k_hi"], T + 1)
                            cols = slice(t * P, (t + 1) * P)
                            ve.tensor_tensor(k_b[layer][0:DH, :, cols],
                                             second[0:DH, 0:B * P].rearrange("p (b n) -> p b n", b=B),
                                             k_a[layer][0:DH, :, cols], ALU.subtract).then_inc(s["k_lo"], 1)
                    if k == 0 and 0 <= m + 1 < NU:
                        u = m + 1
                        hg = (u % UNITS) // B
                        dve.wait_ge(s["q_null"], u + 1)
                        if u >= 2:
                            dve.wait_ge(s["d_null"], u - 1)
                        ve.scalar_tensor_tensor(neg_null[:, u % 2, :], second[:, 0:HU], -1.0,
                                                null_b[u // U0][:, hg * HU:(hg + 1) * HU], ALU.mult, ALU.subtract)\
                            .then_inc(s["null"], 1)
                    if k == 2 and 0 <= m - 1 < NU:
                        u = m - 1
                        dve.wait_ge(s["ot_hi"], u + 1)
                        ve.tensor_tensor(ot_lo[:, :], second[:, 0:UW], ot_hi[:, :], ALU.subtract).then_inc(s["ot_lo"], 1)

                now = plan.at(n)
                for j in range(max(1, len(now))):
                    if j < len(now):
                        gi = now[j]
                        nb = plan.groups[gi][2]
                        dve.wait_ge(s["p_hi"], gi + 1)
                        ve.tensor_tensor(p_lo[:, gi % 4, 0:nb * P], tp[gi % 2][:, 0:nb * P],
                                         p_hi[:, gi % 4, 0:nb * P], ALU.subtract).then_inc(s["p_lo"], 1)
                    if j == 0:
                        small()
                for T in range(TILES):
                    if n == T * STEP_N - 10:
                        dve.wait_ge(s["kv_r"], T + 1)
                        for bt in range(B):
                            last = ve.scalar_tensor_tensor(k_d[:, bt, 0:DH], k_d[:, bt, 0:DH],
                                                           k_r[:, bt:bt + 1], k_scale[:, :], ALU.mult, ALU.mult)
                        last.then_inc(s["kv_d"], 1)
                for p_ in range(STEPS * B):
                    T, bt = divmod(p_, B)
                    mu = T * UNITS + (HG - 1) * B + bt
                    if n == HU * (mu + 2) + 1:
                        dve.wait_ge(s["y_acc"], y_adds(mu))
                        link(ve.bn_stats(y_st[:, :], y_acc[:, bt, :]))
                        ve.bn_aggr(y_mv[:, :], y_st[:, :]).then_inc(s["y_st"], 1)
                    if n == HU * (mu + 2) + 2:
                        dve.wait_ge(s["y_rs"], p_ + 1)
                        ve.tensor_scalar(y_acc[:, bt, :], y_acc[:, bt, :], y_mv[:, 0:1], y_rs[:, 0:1],
                                         ALU.subtract, ALU.mult).then_inc(s["y_n"], 1)

            def x_lo(cn):
                for kc, bank in enumerate((op, aux)):
                    dve.wait_ge(f["xt_hi"], KC * cn + kc + 1)
                    ve.tensor_tensor(mx_lo[:, cn % 2, kc, :], bank[:, :], mx_hi[:, cn % 2, kc, :], ALU.subtract)\
                        .then_inc(f["xt_lo"], 1)

            def over_e(t_):
                return t_[:, :].unsqueeze(2).to_broadcast([P, CHUNK, E])

            def gate_shift(cn):
                layer, ch = divmod(cn, CHUNKS)
                bt = ch * CHUNK // TILES
                dve.wait_ge(f["logit"], cn + 1)
                link(ve.scalar_tensor_tensor(gl[2][:, :, :], aux[:, 0:CHUNK * E].rearrange("p (t e) -> p t e", t=CHUNK),
                                             0.5 / WS, lg_half[:, layer, bt, :].unsqueeze(1).to_broadcast([P, CHUNK, E]),
                                             ALU.mult, ALU.add))
                link(ve.reduce_max(gm[0][:, :], gl[2][:, :, :], AX))
                ve.tensor_tensor(gl[0][:, :, :], gl[2][:, :, :], over_e(gm[0]), ALU.subtract).then_inc(f["shifted"], 1)

            def gate_pick(cn):
                dve.wait_ge(f["exp"], cn + 1)
                sc_ = gl[2]
                link(ve.reduce_sum(gm[0][:, :], gl[1][:, :, :], AX))
                link(ve.reciprocal(gm[1][:, :], gm[0][:, :]))
                link(ve.tensor_tensor(sc_[:, :, :], gl[1][:, :, :], over_e(gm[1]), ALU.mult))
                left = sc_
                order = place[:, :].unsqueeze(1).to_broadcast([P, CHUNK, E])
                for r in range(2):
                    link(ve.reduce_max(gm[2 + r][:, :], left[:, :, :], AX))
                    link(ve.tensor_tensor(gl[3][:, :, :], left[:, :, :], over_e(gm[2 + r]), ALU.is_equal))
                    link(ve.tensor_tensor(gl[3][:, :, :], gl[3][:, :, :], order, ALU.mult))
                    link(ve.reduce_max(gm[4][:, :], gl[3][:, :, :], AX))
                    link(ve.tensor_tensor(gl[3][:, :, :], gl[3][:, :, :], over_e(gm[4]), ALU.is_equal))
                    link(ve.scalar_tensor_tensor(gl[4 + r][:, :, :], gl[3][:, :, :], -4.0, left[:, :, :],
                                                 ALU.mult, ALU.add))
                    left = gl[4 + r]
                link(ve.scalar_tensor_tensor(gm[4][:, :], gm[2][:, :], 1e-20, gm[3][:, :], ALU.add, ALU.add))
                link(ve.reciprocal(gm[5][:, :], gm[4][:, :]))
                link(ve.tensor_scalar(gl[3][:, :, :], left[:, :, :], 0.0, 1.0 / WS, ALU.is_lt, ALU.mult))
                link(ve.tensor_tensor(gl[3][:, :, :], gl[3][:, :, :], sc_[:, :, :], ALU.mult))
                ve.tensor_tensor(comb[:, cn % 2, :, :], gl[3][:, :, :], over_e(gm[5]), ALU.mult).then_inc(f["comb"], 1)

            def y_evict(en):
                cn, e = divmod(en, EB)
                ch = cn % CHUNKS
                for i in range(CHUNK):
                    if i % 2 == 0:
                        dve.wait_ge(f["down"], 2 * en + i // 2 + 1)
                    if e == 0 and i == 0:
                        dve.wait_ge(f["comb"], cn + 1)
                    if e > 0:
                        dve.wait_ge(f["y"], CHUNK * (en - 1) + i + 1)
                    x_t = x[:, ch * CHUNK + i, :]
                    weight = comb[:, cn % 2, i, e:e + 1] if e < E else 1.0 / WS
                    ve.scalar_tensor_tensor(x_t, tp[i // 2][:, (i % 2) * D:(i % 2 + 1) * D], weight, x_t,
                                            ALU.mult, ALU.add).then_inc(f["y"], 1)

            dve.wait_ge(setup["place"], E)
            x_lo(0)
            gate_shift(0)
            gate_pick(0)
            for en in range(2 * CHUNKS * EB + 2):
                cn, e = divmod(en, EB)
                if en < 2 * CHUNKS * EB:
                    dve.wait_ge(f["tenth"], en + 1)
                    ve.scalar_tensor_tensor(g_l, sc[en % 2][:, 0:512], 1.0 / WS, g_t, ALU.mult, ALU.max)\
                        .then_inc(f["leaky"], 1)
                    dve.wait_ge(f["leaky"], en + 1)
                    if en >= 2:
                        dve.wait_ge(f["h_lo"], en - 1)
                    ve.scalar_tensor_tensor(h_f[:, en % 2, :], sc[en % 2][:, 512:1024], 1.0 / WS, g_l,
                                            ALU.mult, ALU.mult).then_inc(f["h"], 1)
                if en >= 2:
                    y_evict(en - 2)
                if cn + 1 < 2 * CHUNKS:
                    if e == 4:
                        x_lo(cn + 1)
                    if e == 6:
                        gate_shift(cn + 1)
                    if e == 7:
                        gate_pick(cn + 1)

        @block.tensor
        def _(pe):
            te = nc.tensor

            def three(out_, l_hi, l_lo, r_hi, r_lo, first, last):
                te.matmul(out_, l_hi, r_hi, start=first, stop=False)
                te.matmul(out_, l_hi, r_lo, start=False, stop=False)
                return te.matmul(out_, l_lo, r_hi, start=False, stop=last)

            def table_stage(p_):
                r, part = divmod(p_, 4)
                if part != 3:
                    return
                pe.wait_ge(setup["h"], r + 1)
                for kc in range(KC):
                    for k in range(TILES):
                        last = te.transpose(sc[kc][:, k * P:(k + 1) * P], rh[:, k, kc * P:(kc + 1) * P], ident[:, :])
                    last.then_inc(setup["pt"], 1)
                pe.wait_ge(setup["t"], KC * (r + 1))
                if r == 0:
                    pe.wait_ge(s_in["w1"], 16)
                    for k in range(TILES):
                        for kc in range(KC):
                            last = te.matmul(sc[k // 4][:, (k % 4) * D:(k % 4 + 1) * D], rht[:, kc, k, :],
                                             w1_sb[:, kc, :], start=(kc == 0), stop=(kc == KC - 1))
                    last.then_inc(setup["mm"], 1)
                else:
                    pe.wait_ge(s_in["w2"], 2 * 16)
                    for i in range(2):
                        for kc in range(KC):
                            last = te.matmul(tp[i][0:H, :], w2_sb[:, kc, :],
                                             rht[:, kc, 4 * i:4 * i + 4, :].rearrange("p k n -> p (k n)"),
                                             start=(kc == 0), stop=(kc == KC - 1))
                        last.then_inc(setup["mm"], 1)

            pe.wait_ge(setup["ident"], 1)
            table_stage(3)
            pe.wait_ge(setup["nkd"], 1)
            for i in range(2):
                last = te.transpose(aux[:, i * P:(i + 1) * P], null_kd[:, i, :], ident[:, :])
            last.then_inc(setup["nt"], 1)
            pe.wait_ge(s_in["head"], 16 * HEAD_LOADS)
            pe.wait_ge(s_in["moe"], 2 * 16)
            for l in range(2):
                for kc in range(KC):
                    at_ = (l * KC + kc) * E
                    te.transpose(op[:, at_:at_ + E], wt_n[:, l, kc * P:(kc + 1) * P], ident[0:E, 0:E])
                te.transpose(op[0:G, 32 + l * E:32 + (l + 1) * E], wg_n[:, l, :], ident[0:E, 0:E])
            te.transpose(op[0:G, 48:50], cond_n[:, :], ident[0:B, 0:B]).then_inc(setup["mt"], 1)
            pe.wait_ge(setup["cb"], 1)
            for l in range(2):
                for b in range(B):
                    at_ = 64 + (l * B + b) * E
                    last = te.matmul(op[:, at_:at_ + E], cond_b[:, b, :], wg_t[:, l, :], start=True, stop=True)
            last.then_inc(setup["lg"], 1)
            free = {0: [], 1: [], 2: [(setup["nkb"], 1)]}

            def release(b_):
                for sem_, value in free[b_]:
                    pe.wait_ge(sem_, value)

            def take(second_, *after):
                b_ = 2
                if free_banks(slot_n) and (second_ or slot_n % HU == 0):
                    b_ = slot_n % 2 if second_ else 1
                release(b_)
                free[b_] = after

            def pv(gi):
                n, j0, nb = plan.groups[gi]
                layer, h = plan.layer(n), n % HU
                bt = plan.unit(n) % B
                nk = plan.tile(n) + 1
                u = plan.unit(n)
                if gi == plan.first_group[n] and h == 0 and u >= 1:
                    pe.wait_ge(s["o_raw"], u)
                if gi == plan.first_group[n] and plan.unit(n) % UNITS == 0 and h == 0:
                    pe.wait_ge(s["kv_v"], plan.unit(n) // UNITS + 1)
                pe.wait_ge(s["p_lo"], gi + 1)
                o_h = op[:, h * DH:(h + 1) * DH]
                for jj in range(nb):
                    j = j0 + jj
                    v_hi = v_s[layer][:, bt * TILES + j, 0, :]
                    v_lo = v_s[layer][:, bt * TILES + j, 1, :]
                    cols = slice(jj * P, (jj + 1) * P)
                    last = three(o_h, p_hi[:, gi % 4, cols], p_lo[:, gi % 4, cols], v_hi, v_lo,
                                 j == 0, j == nk - 1)
                last.then_inc(s["pv"], 1)

            for n in range(FIRST, LAST):
                m, k = divmod(n, HU)
                if n in TABLE_AT:
                    table_stage(TABLE_AT[n])
                slot_n = n
                first, second = banks(n)
                i = n + 3
                if 0 <= i < N:
                    layer, t, u = plan.layer(i), plan.tile(i), plan.unit(i)
                    bt, h = u % B, i % HU
                    if i == 0:
                        pe.wait_ge(setup["penalty"], 2)
                        pe.wait_ge(setup["mm"], 3)
                    if h == 0:
                        pe.wait_ge(s["q_dup"], u + 1)
                        pe.wait_ge(s["q_lo"], 2 * (u + 1))
                        if u % UNITS == 0:
                            pe.wait_ge(s["k_lo"], u // UNITS + 1)
                    if i >= 2:
                        pe.wait_ge(s["biased"], i - 1)
                    cols = slice(h * P, (h + 1) * P)
                    w = P * (t + 1)
                    if w > 512:
                        release(i % 2)
                        free[i % 2] = ()
                    for c0 in range(0, w, 512):
                        cw = min(512, w - c0)
                        o_ = sc[i % 2][:, c0:c0 + cw]
                        te.matmul(o_, q_a[:, u % 2, cols], k_a[layer][:, bt, c0:c0 + cw], start=True, stop=False)
                        last = te.matmul(o_, q_b[:, u % 2, cols], k_b[layer][:, bt, c0:c0 + cw],
                                         start=False, stop=True)
                    last.then_inc(s["scores"], 1)
                if k == 0 and 0 <= m - 2 < NU:
                    u = m - 2
                    layer, hg = u // U0, (u % UNITS) // B
                    take(False, (s["y_s"], u + 1))
                    pe.wait_ge(s["ot_lo"], u + 1)
                    if u % U0 == 0:
                        pe.wait_ge(job_done, job_end[3 * layer + 2])
                    for cc in range(UW // P):
                        rows_ = hg * (UW // P) + cc
                        last = three(first[:, 0:D], ot_hi[:, cc * P:(cc + 1) * P], ot_lo[:, cc * P:(cc + 1) * P],
                                     wo[layer][:, 0, rows_, :], wo[layer][:, 1, rows_, :],
                                     cc == 0, cc == UW // P - 1)
                    last.then_inc(s["y"], 1)
                if k == 3 and 0 <= m + 2 < NU:
                    u = m + 2
                    take(False, (s["q_lo"], 2 * (u + 1)))
                    pe.wait_ge(s["q_na"], u + 1)
                    if u < U0:
                        pe.wait_ge(s["q_nd"], u + 1)
                    for c in range(UW // P):
                        last = te.transpose(first[:, c * P:(c + 1) * P], q_n[:, u % 2, c * P:(c + 1) * P], ident[:, :])
                    last.then_inc(s["q_t"], 1)
                if k == 1 and 0 <= m + 3 < NU:
                    u = m + 3
                    layer = u // U0
                    T, hg, bt = u // UNITS, (u % UNITS) // B, u % B
                    take(False, (s["q_na"], u + 1), (s["q_ss"], HU * min(u + 1, U0)))
                    if hg == 0:
                        pe.wait_ge(s["xt_lo"], T + 1)
                        if T % TILES == 0:
                            pe.wait_ge(job_done, job_end[3 * layer + 1])
                    for kc in range(KC):
                        cols = slice(hg * UW, (hg + 1) * UW)
                        last = three(first[:, 0:UW], xt[:, T % 2, 0, bt, kc, :], xt[:, T % 2, 1, bt, kc, :],
                                     wq[layer][:, 0, kc, cols], wq[layer][:, 1, kc, cols],
                                     kc == 0, kc == KC - 1)
                    last.then_inc(s["q_proj"], 1)

                def small():
                    for T in range(STEPS):
                        n0 = T * STEP_N
                        layer, t = divmod(T, TILES)
                        if n == n0 - 15:
                            take(True, (s["xt_lo"], T + 1))
                            pe.wait_ge(s["xn"], T + 1)
                            for bt in range(B):
                                for kc in range(KC):
                                    at_ = (bt * KC + kc) * P
                                    last = te.transpose(second[:, at_:at_ + P], xn[:, bt, kc * P:(kc + 1) * P], ident[:, :])
                            last.then_inc(s["xt"], 1)
                        if n == n0 - 11:
                            take(True, (s["kv_v"], T + 1))
                            pe.wait_ge(s["xt_lo"], T + 1)
                            if t == 0:
                                pe.wait_ge(job_done, job_end[3 * layer])
                            for bt in range(B):
                                for kc in range(KC):
                                    last = three(second[:, bt * 2 * DH:(bt + 1) * 2 * DH],
                                                 xt[:, T % 2, 0, bt, kc, :], xt[:, T % 2, 1, bt, kc, :],
                                                 wkv[layer][:, 0, kc, :], wkv[layer][:, 1, kc, :],
                                                 kc == 0, kc == KC - 1)
                            last.then_inc(s["kv"], 1)
                        if n == n0 - 7:
                            take(True, (s["k_lo"], T + 1))
                            if layer == 0:
                                pe.wait_ge(s["k_dup"], T + 1)
                            for bt in range(B):
                                last = te.transpose(second[:, bt * P:(bt + 1) * P], k_d[:, bt, :], ident[:, :])
                            last.then_inc(s["kt"], 1)
                    if k == 0 and 0 <= m + 1 < NU:
                        u = m + 1
                        layer = u // U0
                        take(True, (s["null"], u + 1))
                        pe.wait_ge(s["q_dup"], u + 1)
                        pe.wait_ge(s["q_lo"], 2 * (u + 1))
                        if u == 0:
                            pe.wait_ge(setup["big"], 1)
                        for h in range(HU):
                            cols = slice(h * P, (h + 1) * P)
                            te.matmul(second[:, h:h + 1], q_a[:, u % 2, cols], kn_a[:, layer:layer + 1], start=True, stop=False)
                            last = te.matmul(second[:, h:h + 1], q_b[:, u % 2, cols], kn_b[:, layer:layer + 1],
                                             start=False, stop=True)
                        last.then_inc(s["q_null"], 1)
                    if k == 2 and 0 <= m - 1 < NU:
                        u = m - 1
                        take(True, (s["ot_lo"], u + 1))
                        pe.wait_ge(s["o_n"], u + 1)
                        o_f = o_n[:, :, :].rearrange("p h d -> p (h d)")
                        for cc in range(UW // P):
                            last = te.transpose(second[:, cc * P:(cc + 1) * P], o_f[:, cc * P:(cc + 1) * P], ident[:, :])
                        last.then_inc(s["ot"], 1)

                now, before = plan.at(n), plan.at(n - 1)
                for j in range(max(1, len(now), len(before))):
                    if j < len(now):
                        gi = now[j]
                        _, j0, nb = plan.groups[gi]
                        pe.wait_ge(s["probs"], n + 1)
                        if gi >= 2:
                            pe.wait_ge(s["p_lo"], gi - 1)
                        for jj in range(nb):
                            last = te.transpose(tp[gi % 2][:, jj * P:(jj + 1) * P],
                                                probs[:, n % 2, (j0 + jj) * P:(j0 + jj + 1) * P], ident[:, :])
                        last.then_inc(s["pt"], 1)
                    if j < len(before):
                        pv(before[j])
                    if j == 0:
                        small()

            def x_t(cn):
                ch = cn % CHUNKS
                for kc, bank in enumerate((op, aux)):
                    if cn == 0:
                        release(2)
                        pe.wait_ge(s["x_new"], STEPS * B)
                    else:
                        pe.wait_ge(f["xt_lo"], KC * (cn - 1) + kc + 1)
                        if kc == 1:
                            pe.wait_ge(f["shifted"], cn)
                    if cn >= CHUNKS:
                        pe.wait_ge(f["y"], CHUNK * EB * (cn - CHUNKS + 1))
                    for i_ in range(CHUNK):
                        last = te.transpose(bank[:, i_ * P:(i_ + 1) * P], x[:, ch * CHUNK + i_, kc * P:(kc + 1) * P],
                                            ident[:, :])
                    last.then_inc(f["xt"], 1)

            def logits(cn):
                layer = cn // CHUNKS
                pe.wait_ge(f["xt_lo"], KC * (cn + 1))
                for i_ in range(CHUNK):
                    cols = slice(i_ * P, (i_ + 1) * P)
                    for kc in range(KC):
                        last = three(aux[:, i_ * E:(i_ + 1) * E], mx_hi[:, cn % 2, kc, cols], mx_lo[:, cn % 2, kc, cols],
                                     wt_s[:, layer, 0, kc, :], wt_s[:, layer, 1, kc, :], kc == 0, kc == KC - 1)
                last.then_inc(f["logit"], 1)

            def gate_up(en):
                cn, e = divmod(en, EB)
                layer = cn // CHUNKS
                if en >= 2:
                    pe.wait_ge(f["h"], en - 1)
                if cn % CHUNKS == 0:
                    pe.wait_ge(job_done, job_end[9 + 4 * layer] if e >= E else job_end[7 + 4 * layer])
                for name, at_ in (("gate", 0), ("up", 512)):
                    for kc in range(KC):
                        if e < E:
                            w_hi, w_lo = (moe_view(layer, hl, name, 2048)[:, (e * KC + kc) * M:(e * KC + kc + 1) * M]
                                          for hl in range(2))
                        else:
                            c0 = kc * SM + (e - E) * M
                            w_hi, w_lo = (moe_view(layer, hl, "s" + name, 512)[:, c0:c0 + M] for hl in range(2))
                        last = three(sc[en % 2][:, at_:at_ + 512], w_hi, w_lo,
                                     mx_hi[:, cn % 2, kc, :], mx_lo[:, cn % 2, kc, :], kc == 0, kc == KC - 1)
                last.then_inc(f["gu"], 1)

            def down(en):
                cn, e = divmod(en, EB)
                layer = cn // CHUNKS
                pe.wait_ge(f["h_lo"], en + 1)
                if cn % CHUNKS == 0:
                    pe.wait_ge(job_done, job_end[9 + 4 * layer] if e >= E else job_end[8 + 4 * layer])
                name, c0 = ("down", e * D) if e < E else ("sdown", (e - E) * D)
                size = 2048 if e < E else 512
                w_hi, w_lo = (moe_view(layer, hl, name, size)[:, c0:c0 + D] for hl in range(2))
                for i_ in range(CHUNK):
                    if i_ % 2 == 0 and en >= 1:
                        pe.wait_ge(f["y"], CHUNK * (en - 1) + i_ + 2)
                    cols = slice(i_ * P, (i_ + 1) * P)
                    last = three(tp[i_ // 2][:, (i_ % 2) * D:(i_ % 2 + 1) * D], h_hi[:, en % 4, cols],
                                 h_lo[:, en % 4, cols], w_hi, w_lo, True, True)
                    if i_ % 2 == 1:
                        last.then_inc(f["down"], 1)

            x_t(0)
            logits(0)
            for en in range(2 * CHUNKS * EB + 2):
                cn, e = divmod(en, EB)
                if en < 2 * CHUNKS * EB:
                    gate_up(en)
                if en >= 2:
                    down(en - 2)
                if cn + 1 < 2 * CHUNKS:
                    if e == 4:
                        x_t(cn + 1)
                    if e == 6:
                        logits(cn + 1)


def kernel(**inputs):
    import numpy as np
    import concourse.bacc as bacc
    from concourse.bass_utils import run_bass_kernel_spmd

    nc = bacc.Bacc("TRN2", target_bir_lowering=False, num_devices=1)
    arrays, aps = {}, {}
    for name, value in inputs.items():
        v = np.ascontiguousarray(value)
        if v.dtype == np.bool_:
            v = v.view(np.int32)
        arrays["in_" + name] = v
        aps[name] = nc.dram_tensor("in_" + name, v.shape, mybir.dt.from_np(v.dtype), kind="ExternalInput").ap()
    out = nc.dram_tensor("out", (B, S, D), F32, kind="ExternalOutput").ap()
    model(nc, aps, out)
    return run_bass_kernel_spmd(nc, [arrays], core_ids=[0]).results[0]["out"]
```
